# Optimizing a Trainium2 kernel written in Bass

```python
import numpy as np
import jax
import jax.numpy as jnp

def _softmax(x, axis=-1):
    return jax.nn.softmax(x, axis=axis)

def _gelu(x):
    return jax.nn.gelu(x, approximate=True)

def _silu(x):
    return jax.nn.silu(x)

def _sigmoid(x):
    return jax.nn.sigmoid(x)

def _layernorm(x, axis=-1, eps=1e-05):
    m = jnp.mean(x, axis=axis, keepdims=True)
    v = jnp.var(x, axis=axis, keepdims=True)
    return (x - m) / jnp.sqrt(v + eps)

def _scatter_add(tgt, idx, src, axis=0):
    return tgt.at[idx].add(src)

def _segment_sum(src, seg, n):
    return jax.ops.segment_sum(src, seg, n)
kernel_name = 'mk_gnn_ffn_d1_gnn_r16_8f972c'

def setup_inputs(seed: int=0):
    np.random.seed(seed)
    _w = jnp.asarray

    def _rec_inputs():
        import jax
        import jax.numpy as jnp
        _gk = jax.random.key(seed)
        x = -8.776e-05 + 1 * jax.random.normal(jax.random.fold_in(_gk, 1), (1250, 256), jnp.float32)
        src = jax.random.randint(jax.random.fold_in(_gk, 2), (40000,), 0, 1250, jnp.int32)
        dst = jnp.minimum((1250 * jax.random.uniform(jax.random.fold_in(_gk, 3), (40000,)) ** 2.0).astype(jnp.int32), 19999)
        _o = jnp.argsort(dst, stable=True)
        src = src[_o]
        dst = dst[_o]
        return (x, src, dst)
    x, src, dst = _rec_inputs()

    def _L0_gnn_setup():
        import jax, jax.numpy as jnp
        import numpy as np
        N, E, IN_DIM, HEADS, HEAD_DIM = (1250, 20000, 256, 4, 64)
        OUT_DIM = HEADS * HEAD_DIM
        NEG_SLOPE = 0.2
        LN_EPS = 1e-05
        SM_EPS = 1e-16

        def _gatv2_block(x, edge_index, W_l, W_r, att, bias, gamma, beta):
            src, dst = (edge_index[0], edge_index[1])
            xl = (x @ W_l).reshape(N, HEADS, HEAD_DIM)
            xr = (x @ W_r).reshape(N, HEADS, HEAD_DIM)
            e = xl[src] + xr[dst]
            e = jnp.where(e >= 0, e, NEG_SLOPE * e)
            score = jnp.einsum('ehd,hd->eh', e, att)
            m = jax.ops.segment_max(score, dst, num_segments=N)
            m = jnp.where(jnp.isfinite(m), m, 0.0)
            ex = jnp.exp(score - m[dst])
            denom = jax.ops.segment_sum(ex, dst, num_segments=N)
            alpha = ex / (denom[dst] + SM_EPS)
            agg = jax.ops.segment_sum(alpha[:, :, None] * xl[src], dst, num_segments=N)
            out = agg.reshape(N, OUT_DIM) + bias
            h = jax.nn.elu(out) + x
            mu = jnp.mean(h, axis=-1, keepdims=True)
            var = jnp.mean(jnp.square(h - mu), axis=-1, keepdims=True)
            return (h - mu) * jax.lax.rsqrt(var + LN_EPS) * gamma + beta
        key = jax.random.key(seed)
        ks = jax.random.split(key, 9)
        s = 1.0 / np.sqrt(IN_DIM)
        return {'x': jax.random.normal(ks[0], (N, IN_DIM), jnp.float32), 'edge_index': jax.random.randint(ks[1], (2, E), 0, N, jnp.int32), 'W_l': jax.random.normal(ks[2], (IN_DIM, OUT_DIM), jnp.float32) * s, 'W_r': jax.random.normal(ks[3], (IN_DIM, OUT_DIM), jnp.float32) * s, 'att': jax.random.normal(ks[4], (HEADS, HEAD_DIM), jnp.float32) * s, 'bias': jnp.zeros((OUT_DIM,), jnp.float32), 'gamma': jnp.ones((OUT_DIM,), jnp.float32), 'beta': jnp.zeros((OUT_DIM,), jnp.float32)}
    _L0_gnn_all = _L0_gnn_setup()
    _L0_gnn_in = {k: v for k, v in _L0_gnn_all.items() if k in ('W_l', 'W_r', 'att', 'bias', 'gamma', 'beta')}
    del _L0_gnn_all

    def _L0_ffn_setup():
        import jax, jax.numpy as jnp
        import numpy as np
        D_IN, D_HID, D_OUT = (256, 512, 256)
        N_EXPERTS, TOP_K = (64, 2)
        B, S = (8, 256)
        key = jax.random.key(seed)
        ks = jax.random.split(key, 8)
        scale_in = 1.0 / np.sqrt(D_IN)
        scale_hid = 1.0 / np.sqrt(D_HID)
        return {'x': jax.random.normal(ks[0], (B, S, D_IN), dtype=jnp.float32), 'Wr': jax.random.uniform(ks[1], (D_IN, N_EXPERTS), jnp.float32, -scale_in, scale_in), 'br': jax.random.uniform(ks[2], (N_EXPERTS,), jnp.float32, -scale_in, scale_in), 'W1': jax.random.uniform(ks[3], (N_EXPERTS, D_IN, D_HID), jnp.float32, -scale_in, scale_in), 'b1': jax.random.uniform(ks[4], (N_EXPERTS, D_HID), jnp.float32, -scale_in, scale_in), 'W2': jax.random.uniform(ks[5], (N_EXPERTS, D_HID, D_OUT), jnp.float32, -scale_hid, scale_hid), 'b2': jax.random.uniform(ks[6], (N_EXPERTS, D_OUT), jnp.float32, -scale_hid, scale_hid)}
    _L0_ffn_all = _L0_ffn_setup()
    _L0_ffn_in = {k: v for k, v in _L0_ffn_all.items() if k in ('Wr', 'br', 'W1', 'b1', 'W2', 'b2')}
    del _L0_ffn_all
    return {'x': x, 'src': src, 'dst': dst, 'L0_gnn_W_l': _L0_gnn_in['W_l'], 'L0_gnn_W_r': _L0_gnn_in['W_r'], 'L0_gnn_att': _L0_gnn_in['att'], 'L0_gnn_bias': _L0_gnn_in['bias'], 'L0_gnn_gamma': _L0_gnn_in['gamma'], 'L0_gnn_beta': _L0_gnn_in['beta'], 'L0_ffn_Wr': _L0_ffn_in['Wr'], 'L0_ffn_br': _L0_ffn_in['br'], 'L0_ffn_W1': _L0_ffn_in['W1'], 'L0_ffn_b1': _L0_ffn_in['b1'], 'L0_ffn_W2': _L0_ffn_in['W2'], 'L0_ffn_b2': _L0_ffn_in['b2']}

def reference(x, src, dst, L0_gnn_W_l, L0_gnn_W_r, L0_gnn_att, L0_gnn_bias, L0_gnn_gamma, L0_gnn_beta, L0_ffn_Wr, L0_ffn_br, L0_ffn_W1, L0_ffn_b1, L0_ffn_W2, L0_ffn_b2):
    import jax
    import jax.numpy as jnp

    def _L0_gnn_ref(x, edge_index, W_l, W_r, att, bias, gamma, beta):
        import jax, jax.numpy as jnp
        import numpy as np
        N, E, IN_DIM, HEADS, HEAD_DIM = (1250, 20000, 256, 4, 64)
        OUT_DIM = HEADS * HEAD_DIM
        NEG_SLOPE = 0.2
        LN_EPS = 1e-05
        SM_EPS = 1e-16

        def _gatv2_block(x, edge_index, W_l, W_r, att, bias, gamma, beta):
            src, dst = (edge_index[0], edge_index[1])
            xl = (x @ W_l).reshape(N, HEADS, HEAD_DIM)
            xr = (x @ W_r).reshape(N, HEADS, HEAD_DIM)
            e = xl[src] + xr[dst]
            e = jnp.where(e >= 0, e, NEG_SLOPE * e)
            score = jnp.einsum('ehd,hd->eh', e, att)
            m = jax.ops.segment_max(score, dst, num_segments=N)
            m = jnp.where(jnp.isfinite(m), m, 0.0)
            ex = jnp.exp(score - m[dst])
            denom = jax.ops.segment_sum(ex, dst, num_segments=N)
            alpha = ex / (denom[dst] + SM_EPS)
            agg = jax.ops.segment_sum(alpha[:, :, None] * xl[src], dst, num_segments=N)
            out = agg.reshape(N, OUT_DIM) + bias
            h = jax.nn.elu(out) + x
            mu = jnp.mean(h, axis=-1, keepdims=True)
            var = jnp.mean(jnp.square(h - mu), axis=-1, keepdims=True)
            return (h - mu) * jax.lax.rsqrt(var + LN_EPS) * gamma + beta
        return _gatv2_block(x, edge_index, W_l, W_r, att, bias, gamma, beta)

    def _L0_ffn_ref(x, Wr, br, W1, b1, W2, b2):
        import jax, jax.numpy as jnp
        import numpy as np
        D_IN, D_HID, D_OUT = (256, 512, 256)
        N_EXPERTS, TOP_K = (64, 2)
        B, S = (8, 256)
        Bx, Sx, D = x.shape
        xf = x.reshape(-1, D)
        T = xf.shape[0]
        E = Wr.shape[1]
        logits = xf @ Wr + br
        topk_logits, topk_idx = jax.lax.top_k(logits, TOP_K)
        gates = jax.nn.softmax(topk_logits, axis=1)
        combine = jnp.zeros((T, E), xf.dtype).at[jnp.arange(T)[:, None], topk_idx].add(gates)
        out = jnp.zeros((T, W2.shape[-1]), xf.dtype)
        for e in range(E):
            h = jax.nn.relu(xf @ W1[e] + b1[e])
            y = h @ W2[e] + b2[e]
            out = out + combine[:, e:e + 1] * y
        return out.reshape(Bx, Sx, -1)
    edge_index = jnp.stack([src, dst])
    x = x + _L0_gnn_ref(_layernorm(x, axis=-1), edge_index, L0_gnn_W_l, L0_gnn_W_r, L0_gnn_att, L0_gnn_bias, L0_gnn_gamma, L0_gnn_beta)
    x = x + _L0_ffn_ref(_layernorm(x, axis=-1)[None], L0_ffn_Wr, L0_ffn_br, L0_ffn_W1, L0_ffn_b1, L0_ffn_W2, L0_ffn_b2)[0]
    return x

_drawn_inputs = setup_inputs


def setup_inputs(seed=0):
    import zlib

    import numpy as np

    out = dict(_drawn_inputs(seed))
    spreads = {'L0_gnn_bias': (0.0, 0.1), 'L0_gnn_gamma': (1.0, 0.2), 'L0_gnn_beta': (0.0, 0.1)}
    factors = {'L0_gnn_W_r': 3.145, 'L0_ffn_b1': 8.0, 'L0_ffn_b2': 6.185}
    for name, (base, spread) in spreads.items():
        noise = np.random.default_rng([zlib.crc32(name.encode()), seed]).standard_normal(out[name].shape)
        drawn = base * np.exp(spread * noise) if base else spread * noise
        out[name] = jnp.asarray(drawn.astype(out[name].dtype))
    for name, factor in factors.items():
        out[name] = (out[name] * factor).astype(out[name].dtype)
    return out
```

```python
from contextlib import ExitStack

import numpy as np

import concourse.bass as bass
from concourse import mybir

ALU = mybir.AluOpType
ACT = mybir.ActivationFunctionType
AX_X = mybir.AxisListType.X
F32 = mybir.dt.float32
BF16 = mybir.dt.bfloat16
I32 = mybir.dt.int32

P = 128
N, D = 1250, 256
DX = D + 4
E = 40000
HEADS, HD = 4, 64
NW = -(-N // P)
NREM = N - (NW - 1) * P
NPAD = NW * P
TILES = -(-E // P)
U = 5
CH = 3
NI = -(-(TILES + NW - 1) // (2 * U * CH)) * 2 * U * CH
CI = NI // CH
STEPS = NI // U
ROWS = TILES + 1
EPAD = ROWS * P - E
BIG = 1e30
WPAD = 8
SLOPE = 0.2
LN_EPS = 1e-5
SM_EPS = 1e-16
NE, HID, TOPK = 64, 512, 2
KC, HC = D // P, HID // P
CAP = 96
RING = 8
OVB = (N * TOPK) // CAP
SLOTS = (NE + OVB) * CAP


class Chain:

    def __init__(self, eng, sem):
        self.eng, self.sem, self.n = eng, sem, 0

    def __call__(self, ins):
        ins.then_inc(self.sem, 1)
        self.n += 1
        return self.n

    def then(self, ins):
        self(ins)
        self.eng.wait_ge(self.sem, self.n)


def col(ap, *sizes):
    shape = list(ap.shape)
    for s in sizes:
        ap = ap.unsqueeze(len(shape))
        shape.append(s)
    return ap.broadcast_to(shape)


def load_weights(eng, W1, W2, w1, w2, w_in, q, e):
    eng.dma_start(w1[q][:, :, :], W1[bass.ds(e, 1), :, :].rearrange("e (p c) n -> (e p) c n", c=KC)).then_inc(w_in[q], 16)
    eng.dma_start(w2[q][:, :, :], W2[bass.ds(e, 1), :, :].rearrange("e (p m) n -> (e p) m n", m=HC)).then_inc(w_in[q], 16)


def load_windows(pe, regs, wrow, s):
    pe.load(regs, wrow[0:1, bass.ds(s, 1), 0:U].rearrange("o s u -> o (s u)"))
    return [pe.snap(x, min_val=0, max_val=NW - 1) for x in regs]


def gnn_moe(nc, x, src, dst, Wl, Wr, att, bias, gamma, beta, Rw, Rb, W1, b1, W2, b2, out):
    with ExitStack() as ctx:
        def sb(name, shape, dt=F32):
            return ctx.enter_context(nc.sbuf_tensor(name, shape, dt))

        def dram(name, shape, dt=F32):
            return nc.dram_tensor(name, shape, dt, kind="Internal").ap()

        def sem(name):
            return ctx.enter_context(nc.semaphore(name))

        srcp = dram("srcp", [ROWS, P], I32)
        dstp = dram("dstp", [ROWS, P], I32)
        xl_tab = dram("xl_tab", [NPAD, DX])
        gathered_d = dram("gathered_d", [STEPS, P, U * D])
        rel_d = dram("rel_d", [NI + 2 * U, P], BF16)
        xs_d = dram("xs_d", [SLOTS, D])
        ys_d = dram("ys_d", [SLOTS, D])
        b2_d = dram("b2_d", [NE, 3, D], BF16)

        ident = sb("ident", [P, P])
        prow = sb("prow", [P, 1])
        iota32 = sb("iota32", [P, P])
        iotai = sb("iotai", [P, NI], I32)
        xs = sb("xs", [P, NW, D])
        xn = sb("xn", [P, NW, D])
        xr3 = sb("xr3", [P, NW * 3 * DX], BF16)
        attb = sb("attb", [P, D])
        bg = sb("bg", [P, 3, D])
        S = sb("S", [P, NI + U, HEADS])
        A = sb("A", [P, NI, HEADS])
        REL = sb("REL", [P, NI])
        srcI = sb("srcI", [P, NI + 2 * U], I32)
        wrow = sb("wrow", [1, STEPS, WPAD], I32)
        valid = sb("valid", [CI, CH, P])
        gd = sb("gd", [CI, CH, P])
        h_in = sb("h_in", [P, NW, D])
        gates = sb("gates", [P, NW, TOPK])
        slot = sb("slot", [P, TOPK, NW], I32)
        nov = sb("nov", [1, 1], I32)
        ovx = sb("ovx", [1, OVB], I32)
        b1T = sb("b1T", [P, NE, HC])
        w1 = [sb(f"w1_{q}", [P, KC, HID]) for q in range(RING)]
        w2 = [sb(f"w2_{q}", [P, HC, D]) for q in range(RING)]

        w_in = [sem(f"w_in{q}") for q in range(RING)]
        node_phase(nc, locals())
        score_phase(nc, locals())
        softmax_phase(nc, locals())
        aggregate_phase(nc, locals())
        route_phase(nc, locals())
        expert_phase(nc, locals())
        overflow_phase(nc, locals())
        combine_phase(nc, locals())


def node_phase(nc, v):
    (x, src, dst, Wl, Wr, att, bias, gamma, beta, srcp, dstp, xl_tab, rel_d, ident, prow, iota32, iotai,
     xs, xn, xr3, attb, bg, S, REL, srcI, wrow, valid, gd) = (v[k] for k in (
         "x src dst Wl Wr att bias gamma beta srcp dstp xl_tab rel_d ident prow iota32 iotai "
         "xs xn xr3 attb bg S REL srcI wrow valid gd").split())
    with ExitStack() as ctx:
        def sb(name, shape, dt=F32):
            return ctx.enter_context(nc.sbuf_tensor(name, shape, dt))

        def sem(name):
            return ctx.enter_context(nc.semaphore(name))

        Wlr = sb("Wlr", [P, KC, 2 * D])
        pad = sb("pad", [1, 2, EPAD], I32)
        lastd = sb("lastd", [P, CH], I32)
        lastf = sb("lastf", [P, CH])
        iotak = sb("iotak", [P, NI])
        before = sb("before", [P, CH, NI])
        ones = sb("ones", [P, 1])
        trow = sb("trow", [1, NI])
        wrf = sb("wrf", [1, NI])
        kcol_i = sb("kcol_i", [CI, CH], I32)
        pcol_i = sb("pcol_i", [P, CH], I32)
        kcol = sb("kcol", [CI, CH])
        pcol = sb("pcol", [P, CH])
        tcol = sb("tcol", [CI, CH])
        wcol = sb("wcol", [CI, CH])
        tcol_i = sb("tcol_i", [CI, CH], I32)
        stats = sb("stats", [P, NW, 6])
        mv = sb("mv", [P, NW, 2])
        std = sb("std", [P, NW])
        rstd = sb("rstd", [P, NW])
        xnT = sb("xnT", [P, KC, NPAD])
        xlr = sb("xlr", [P, NW, 2, DX])
        Watt = sb("Watt", [P, KC, 2 * HEADS])
        watp = sb("watp", [P, KC, 2 * D])
        rem = sb("rem", [P, 2, DX])
        srcT = sb("srcT", [CI, CH, P], I32)
        dstT = sb("dstT", [CI, CH, P], I32)
        srcF = sb("srcF", [CI, CH, P])
        dstF = sb("dstF", [CI, CH, P])
        clampd = sb("clampd", [CI, CH, P])
        relm = sb("relm", [CI, CH, P])
        rel16 = sb("rel16", [CI, CH, P], BF16)
        psT = ctx.enter_context(nc.psum_tensor("psT", [P, 2, 512], F32))
        psX = ctx.enter_context(nc.psum_tensor("psX", [P, 2, 512], F32))
        psI = ctx.enter_context(nc.psum_tensor("psI", [P, 512], F32))
        psJ = ctx.enter_context(nc.psum_tensor("psJ", [P, 512], F32))
        psE = ctx.enter_context(nc.psum_tensor("psE", [P, 2, 512], F32))

        x_in, w_in, c_in, pad_set, tables, last_in, items_in, xl_out = map(sem, (
            "x_in", "w_in", "c_in", "pad_set", "tables", "last_in", "items_in", "xl_out"))
        consts, dv, rooted, normed, xT_ps, xT_sb, proj, xl_sb, xr_sb, before_set, t_ps, t_set, rel_set, rel_ps = map(
            sem, ("consts", "dv_node", "rooted", "normed", "xT_ps", "xT_sb", "proj", "xl_sb", "xr_sb",
                  "before_set", "t_ps", "t_set", "rel_set", "rel_ps"))
        iotas, zeroed = sem("iotas"), sem("zeroed")
        rel16_set, rel_out = sem("rel16_set"), sem("rel_out")
        var_set, proj_lin, watt_set = sem("var_set"), sem("proj_lin"), sem("watt_set")
        block = ctx.enter_context(nc.Block())

        @block.sync
        def _(sp):
            sp.wait_ge(zeroed, 1)
            sp.dma_start(xs[:, 0:NW - 1, :], x[0:(NW - 1) * P, :].rearrange("(w p) f -> p w f", p=P)).then_inc(x_in, 16)
            sp.dma_start(xs[0:NREM, NW - 1, :], x[(NW - 1) * P:N, :]).then_inc(x_in, 16)
            sp.dma_start(Wlr[:, :, 0:D], Wl.rearrange("(c p) n -> p c n", p=P)).then_inc(w_in, 16)
            sp.dma_start(Wlr[:, :, D:2 * D], Wr.rearrange("(c p) n -> p c n", p=P)).then_inc(w_in, 16)
            sp.wait_ge(xl_sb, NW)
            sp.dma_start(xl_tab.rearrange("(w p) f -> p w f", p=P), xlr[:, :, 0, :]).then_inc(xl_out, 16)
            sp.wait_ge(xl_out, 16)
            sp.wait_ge(rel16_set, 1)
            sp.dma_start(rel_d[0:NI, :].rearrange("(c k) e -> k c e", c=CH), rel16[:, :, :]).then_inc(rel_out, 16)
            sp.dma_start(rel_d[NI:NI + 2 * U, :], rel16[0:2 * U, 0, :]).then_inc(rel_out, 16)
            sp.wait_ge(rel_out, 32)

        @block.scalar
        def _(act):
            for i, (tab, a) in enumerate(((srcp, src), (dstp, dst))):
                flat = tab.rearrange("t e -> (t e)")
                act.dma_start(flat[0:E].rearrange("(a b) -> a b", a=16), a.rearrange("(a b) -> a b", a=16)).then_inc(tables, 16)
                act.wait_ge(pad_set, 2)
                act.dma_start(flat[E:E + EPAD].rearrange("(a b) -> a b", a=1), pad[0:1, i, :]).then_inc(tables, 16)
            act.wait_ge(tables, 64)
            act.wait_ge(zeroed, 2)
            for c in range(CH):
                n = min(P, TILES - c * P)
                act.dma_start(lastd[0:n, c:c + 1], dstp[c * P:c * P + n, P - 1:P],
                              allow_slow_non_contiguous=True).then_inc(last_in, 16)
            act.dma_start(attb[:, :], att.rearrange("h d -> (h d)").unsqueeze(0).broadcast_to([P, D])).then_inc(c_in, 16)
            for i, a in enumerate((bias, gamma, beta)):
                act.dma_start(bg[:, i, :], a.unsqueeze(0).broadcast_to([P, D])).then_inc(c_in, 16)
            act.wait_ge(var_set, 1)
            nc.scalar.activation(std[:, :], rstd[:, :], ACT.Sqrt).then_inc(rooted, 1)
            for i in range(NW // 2):
                act.wait_ge(xT_ps, i + 1)
                nc.scalar.copy(xnT[:, :, 2 * i * P:(2 * i + 2) * P].rearrange("p c (w q) -> p w c q", q=P),
                               psT[:, i % 2, :].rearrange("p (w c q) -> p w c q", w=2, c=KC)).then_inc(xT_sb, 1)
            for w in range(NW):
                act.wait_ge(proj, w + 1)
                nc.scalar.copy(xlr[:, w, :, 0:D], psX[:, w % 2, :].rearrange("p (j f) -> p j f", j=2))
                act.wait_ge(proj_lin, w + 1)
                nc.scalar.copy(xlr[:, w, :, D:DX], psT[:, w % 2, 0:2 * HEADS].rearrange("p (j h) -> p j h", j=2)).then_inc(xl_sb, 1)
            act.wait_ge(c_in, 64)

        @block.gpsimd
        def _(g):
            nc.gpsimd.memset(ident[:, :], 0.0).then_inc(consts, 1)
            nc.gpsimd.memset(pad[:, 0, :], 0).then_inc(pad_set, 1)
            nc.gpsimd.memset(pad[:, 1, :], NPAD - 1).then_inc(pad_set, 1)
            g.wait_ge(consts, 1)
            nc.gpsimd.affine_select(out=ident[:, :], in_=ident[:, :], compare_op=ALU.not_equal, fill=1.0, base=0,
                                    pattern=[[-1, P]], channel_multiplier=1).then_inc(consts, 1)
            nc.gpsimd.iota(iotai[:, :], pattern=[[1, NI]], base=0, channel_multiplier=0).then_inc(iotas, 1)
            nc.gpsimd.iota(kcol_i[:, :], pattern=[[CI, CH]], base=0, channel_multiplier=1).then_inc(iotas, 1)
            nc.gpsimd.iota(pcol_i[:, :], pattern=[[P, CH]], base=0, channel_multiplier=1).then_inc(iotas, 1)
            g.wait_ge(t_set, 1)
            g.wait_ge(tables, 64)
            for c in range(CH):
                for to, tab in ((srcT, srcp), (dstT, dstp)):
                    nc.gpsimd.indirect_dma_start(out=to[:, c, :], out_offset=None, in_=tab,
                                                 in_offset=bass.IndirectOffsetOnAxis(ap=tcol_i[:, c:c + 1], axis=0)
                                                 ).then_inc(items_in, 16)

        @block.tensor
        def _(pe):
            pe.wait_ge(consts, 2)
            pe.wait_ge(before_set, 1)
            for c in range(CH):
                nc.tensor.matmul(psI[0:1, 0:NI], ones[:, :], before[:, c, :], start=(c == 0), stop=(c == CH - 1))
            for m in range(CH):
                for c in range(CH):
                    last = nc.tensor.matmul(psJ[0:CI, m:m + 1], before[:, c, m * CI:(m + 1) * CI], ones[:, :],
                                            start=(c == 0), stop=(c == CH - 1))
            last.then_inc(t_ps, 1)
            pe.wait_ge(normed, NW)
            for i in range(NW // 2):
                if i >= 2:
                    pe.wait_ge(xT_sb, i - 1)
                for w in range(2):
                    for c in range(KC):
                        q = (w * KC + c) * P
                        last = nc.tensor.transpose(psT[:, i % 2, q:q + P], xn[:, 2 * i + w, c * P:(c + 1) * P], ident[:, :])
                last.then_inc(xT_ps, 1)
            pe.wait_ge(xT_sb, NW // 2)
            pe.wait_ge(w_in, 32)
            pe.wait_ge(watt_set, 1)
            for w in range(NW):
                if w >= 2:
                    pe.wait_ge(xl_sb, w - 1)
                for c in range(KC):
                    last = nc.tensor.matmul(psX[:, w % 2, :], xnT[:, c, w * P:(w + 1) * P], Wlr[:, c, :],
                                            start=(c == 0), stop=(c == KC - 1))
                last.then_inc(proj, 1)
                for c in range(KC):
                    last = nc.tensor.matmul(psT[:, w % 2, 0:2 * HEADS], xnT[:, c, w * P:(w + 1) * P], Watt[:, c, :],
                                            start=(c == 0), stop=(c == KC - 1))
                last.then_inc(proj_lin, 1)
            pe.wait_ge(rel_set, 1)
            for j, a in enumerate((srcF, relm)):
                for c in range(CH):
                    last = nc.tensor.transpose(psE[:, j, c * CI:(c + 1) * CI], a[:, c, :], ident[0:CI, 0:CI])
                last.then_inc(rel_ps, 1)

        @block.vector
        def _(dve):
            c = Chain(dve, dv)
            nc.vector.memset(xs[:, :, :], 0.0).then_inc(zeroed, 1)
            nc.vector.memset(lastd[:, :], 1 << 20).then_inc(zeroed, 1)
            c(nc.vector.memset(ones[:, :], 1.0))
            c(nc.vector.memset(S[:, :, :], 0.0))
            dve.wait_ge(consts, 2)
            dve.wait_ge(iotas, 3)
            c(nc.vector.tensor_copy(prow[:, :], pcol_i[:, 0:1]))
            c(nc.vector.tensor_copy(iota32[:, :], iotai[:, 0:P]))
            c(nc.vector.tensor_copy(iotak[:, :], iotai[:, :]))
            c(nc.vector.tensor_copy(kcol[:, :], kcol_i[:, :]))
            c(nc.vector.tensor_copy(pcol[:, :], pcol_i[:, :]))
            dve.wait_ge(last_in, 48)
            c.then(nc.vector.tensor_scalar(lastd[:, :], lastd[:, :], 7, None, ALU.logical_shift_right))
            c.then(nc.vector.tensor_copy(lastf[:, :], lastd[:, :]))
            c.then(nc.vector.tensor_tensor(lastf[:, :], lastf[:, :], pcol[:, :], ALU.add))
            for j in range(CH):
                c(nc.vector.tensor_scalar(before[:, j, :], iotak[:, :], lastf[:, j:j + 1], None, ALU.is_gt))
            dve.wait_ge(dv, c.n)
            dve.sem_inc(before_set, 1)
            dve.wait_ge(x_in, 32)
            for w in range(NW):
                c(nc.vector.bn_stats(stats[:, w, :], xs[:, w, :]))
            dve.wait_ge(dv, c.n)
            for w in range(NW):
                c(nc.vector.bn_aggr(mv[:, w, :], stats[:, w, :]))
            dve.wait_ge(dv, c.n)
            nc.vector.tensor_scalar(rstd[:, :], mv[:, :, 1], LN_EPS, None, ALU.add).then_inc(var_set, 1)
            dve.wait_ge(rooted, 1)
            c.then(nc.vector.reciprocal(rstd[:, :], std[:, :]))
            for w in range(NW):
                nc.vector.tensor_scalar(xn[:, w, :], xs[:, w, :], mv[:, w, 0:1], rstd[:, w:w + 1],
                                        ALU.subtract, ALU.mult).then_inc(normed, 1)
            dve.wait_ge(t_ps, 1)
            c.then(nc.vector.tensor_tensor(wrf[:, :], iotak[0:1, :], psI[0:1, 0:NI], ALU.subtract))
            c.then(nc.vector.tensor_scalar(wrow[:, :, 0:U], wrf[:, :].rearrange("o (s u) -> o s u", u=U), float(NW - 1), None, ALU.min))
            c.then(nc.vector.tensor_tensor(wcol[:, :], kcol[:, :], psJ[0:CI, 0:CH], ALU.subtract))
            c.then(nc.vector.tensor_scalar(wcol[:, :], wcol[:, :], float(NW - 1), float(P), ALU.min, ALU.mult))
            nc.vector.tensor_scalar(tcol_i[:, :], psJ[0:CI, 0:CH], float(ROWS - 1), None, ALU.min).then_inc(t_set, 1)
            dve.wait_ge(c_in, 64)
            dve.wait_ge(w_in, 32)
            c.then(nc.vector.tensor_tensor(watp[:, :, :].rearrange("p c (j f) -> p (c j) f", j=2),
                                           Wlr[:, :, :].rearrange("p c (j f) -> p (c j) f", j=2),
                                           attb[:, :].unsqueeze(1).broadcast_to([P, 2 * KC, D]), ALU.mult))
            c.then(nc.vector.tensor_reduce(Watt[:, :, :], watp[:, :, :].rearrange("p c (h d) -> p c h d", d=HD), AX_X, ALU.add))
            nc.vector.tensor_scalar(Watt[:, :, :], Watt[:, :, :], SLOPE, None, ALU.mult).then_inc(watt_set, 1)
            c.then(nc.vector.tensor_scalar(attb[:, :], attb[:, :], 1.0 - SLOPE, None, ALU.mult))
            for w in range(NW):
                part = [xr3[:, (3 * w + j) * DX:(3 * w + j + 1) * DX] for j in range(3)]
                dve.wait_ge(xl_sb, w + 1)
                c.then(nc.vector.tensor_copy(part[0], xlr[:, w, 1, :]))
                c.then(nc.vector.tensor_tensor(rem[:, 0, :], xlr[:, w, 1, :], part[0], ALU.subtract))
                c.then(nc.vector.tensor_copy(part[1], rem[:, 0, :]))
                nc.vector.tensor_tensor(part[2], rem[:, 0, :], part[1], ALU.subtract).then_inc(xr_sb, 1)
            dve.wait_ge(items_in, 16 * 2 * CH)
            c(nc.vector.tensor_copy(srcF[:, :, :], srcT[:, :, :]))
            c.then(nc.vector.tensor_copy(dstF[:, :, :], dstT[:, :, :]))
            for j in range(CH):
                c(nc.vector.tensor_scalar(dstF[:, j, :], dstF[:, j, :], wcol[:, j:j + 1], None, ALU.subtract))
            dve.wait_ge(dv, c.n)
            c.then(nc.vector.tensor_scalar(clampd[:, :, :], dstF[:, :, :], 0.0, float(P - 1), ALU.max, ALU.min))
            c.then(nc.vector.tensor_tensor(valid[:, :, :], clampd[:, :, :], dstF[:, :, :], ALU.is_equal))
            c.then(nc.vector.scalar_tensor_tensor(out=relm[:, :, :], in0=dstF[:, :, :], scalar=1.0, in1=valid[:, :, :],
                                                  op0=ALU.add, op1=ALU.mult))
            nc.vector.tensor_scalar(relm[:, :, :], relm[:, :, :], -1.0, None, ALU.add).then_inc(rel_set, 1)
            dve.wait_ge(rel_set, 1)
            nc.vector.tensor_copy(rel16[:, :, :], relm[:, :, :]).then_inc(rel16_set, 1)
            for j in range(CH):
                c(nc.vector.tensor_scalar(gd[:, j, :], clampd[:, j, :], wcol[:, j:j + 1], None, ALU.add))
            dve.wait_ge(rel_ps, 1)
            c(nc.vector.tensor_copy(srcI[:, 0:NI], psE[:, 0, 0:NI]))
            c(nc.vector.memset(srcI[:, NI:NI + 2 * U], 0))
            dve.wait_ge(rel_ps, 2)
            c(nc.vector.tensor_copy(REL[:, 0:NI], psE[:, 1, 0:NI]))
            dve.wait_ge(dv, c.n)


def score_phase(nc, v):
    xl_tab, gathered_d, rel_d, prow, xr3, attb, S, srcI, wrow = (
        v[k] for k in "xl_tab gathered_d rel_d prow xr3 attb S srcI wrow".split())
    with ExitStack() as ctx:
        def sb(name, shape, dt=F32):
            return ctx.enter_context(nc.sbuf_tensor(name, shape, dt))

        def sem(name):
            return ctx.enter_context(nc.semaphore(name))

        idx = sb("idx", [P, 2, U], I32)
        G = [sb(f"G{b}", [P, U, DX]) for b in range(2)]
        lin = sb("lin", [P, 2, U, HEADS])
        esum = sb("esum", [P, 2, U * D])
        leaky = sb("leaky", [P, 2, U * D])
        relb = [sb(f"relb{b}", [P, U * P], BF16) for b in range(2)]
        MT = sb("MT", [P, 2, U * P], BF16)
        psE = [ctx.enter_context(nc.psum_tensor(f"psE{b}", [P, 3 * 512], F32)) for b in range(2)]

        gathered = [sem(f"gathered{b}") for b in range(2)]
        spilled = [sem(f"spilled{b}") for b in range(2)]
        turn = sem("turn")
        idx_set = sem("idx_set")
        rel_in = [sem(f"rel_in{b}") for b in range(2)]
        onehot = sem("onehot")
        expanded = sem("expanded")
        summed = sem("summed")
        leaked = sem("leaked")
        scored = sem("scored")
        mul, reduced, lin_set = sem("mul"), sem("reduced"), sem("lin_set")
        part = sb("part", [P, U, HEADS])
        block = ctx.enter_context(nc.Block())

        @block.gpsimd
        def _(g):
            for b in range(2):
                g.sem_inc(spilled[b], 16)
            with g.Fori(0, STEPS // 2) as i:
                for b in range(2):
                    s = i * 2 + b
                    g.wait_ge(summed, s + 1)
                    g.sem_inc(turn, 1)
                    g.wait_ge(spilled[b], i * 16 + 16)
                    g.sem_inc(turn, 1)
                    g.wait_ge(idx_set, s + 1)
                    g.sem_inc(turn, 1)
                    for u in range(U):
                        nc.gpsimd.indirect_dma_start(
                            out=G[b][:, u, :], out_offset=None, in_=xl_tab,
                            in_offset=bass.IndirectOffsetOnAxis(ap=idx[:, b, u:u + 1], axis=0)).then_inc(gathered[b], 16)

        @block.sync
        def _(sp):
            def load_rel(b, s):
                sp.dma_start(relb[b][:, :], rel_d[bass.ds(s * U, U), :].rearrange("(o u) e -> o (u e)", o=1)
                             .broadcast_to([P, U * P])).then_inc(rel_in[b], 16)

            for b in range(2):
                load_rel(b, b)
            with sp.Fori(0, STEPS // 2) as i:
                for b in range(2):
                    sp.wait_ge(onehot, i * 2 + b + 1)
                    load_rel(b, i * 2 + b + 2)
                    sp.wait_ge(gathered[b], i * (16 * U) + 16 * U)
                    sp.dma_start(gathered_d[bass.ds(i * 2 + b, 1), :, :].rearrange("s p f -> (s p) f"),
                                 G[b][:, :, 0:D]).then_inc(spilled[b], 16)
            for b in range(2):
                sp.wait_ge(spilled[b], 16 * (STEPS // 2 + 1))
                sp.wait_ge(rel_in[b], 16 * (STEPS // 2 + 1))

        @block.tensor
        def _(pe):
            pe.sem_inc(expanded, 2)
            regs = [pe.alloc_register(f"window{u}") for u in range(U)]
            with pe.Fori(0, STEPS // 2) as i:
                for b in range(2):
                    s = i * 2 + b
                    ws = load_windows(pe, regs, wrow, s)
                    pe.wait_ge(onehot, s + 1)
                    pe.wait_ge(summed, s + 1)
                    for u in range(U):
                        w = ws[u]
                        for j in range(3):
                            last = nc.tensor.matmul(psE[b][:, u * D:(u + 1) * D], MT[:, b, u * P:(u + 1) * P],
                                                    xr3[:, bass.ds(w * (3 * DX) + j * DX, D)],
                                                    start=(j == 0), stop=(j == 2))
                        q = U * D + u * HEADS
                        for j in range(3):
                            last = nc.tensor.matmul(psE[b][:, q:q + HEADS], MT[:, b, u * P:(u + 1) * P],
                                                    xr3[:, bass.ds(w * (3 * DX) + j * DX + D, HEADS)],
                                                    start=(j == 0), stop=(j == 2))
                    last.then_inc(expanded, 1)

        @block.scalar
        def _(act):
            act.sem_inc(leaked, 1)

            def copy_idx(b, s):
                nc.scalar.copy(idx[:, b, :], srcI[:, bass.ds(s * U, U)]).then_inc(idx_set, 1)

            copy_idx(0, 0)
            copy_idx(1, 1)
            with act.Fori(0, STEPS // 2) as i:
                for b in range(2):
                    s = i * 2 + b
                    act.wait_ge(summed, s + 3)
                    act.wait_ge(scored, s + 1)
                    nc.scalar.activation(leaky[:, b, :], esum[:, b, :], ACT.Relu).then_inc(leaked, 1)
                    copy_idx(b, s + 2)

        @block.vector
        def _(dve):
            dve.sem_inc(summed, 2)
            nc.vector.memset(lin[:, 1, :, :], 0.0).then_inc(mul, 1)
            dve.wait_ge(mul, 1)
            nc.vector.memset(leaky[:, 1, :], 0.0).then_inc(scored, 1)
            dve.wait_ge(scored, 1)

            def build_onehot(b, n):
                dve.wait_ge(rel_in[b], n)
                nc.vector.tensor_scalar(MT[:, b, :], relb[b][:, :], prow[:, 0:1], None, ALU.is_equal).then_inc(onehot, 1)

            def score(b, s):
                dve.wait_ge(leaked, s + 1)
                nc.vector.tensor_tensor(leaky[:, b, :].rearrange("p (u f) -> p u f", u=U),
                                        leaky[:, b, :].rearrange("p (u f) -> p u f", u=U),
                                        attb[:, :].unsqueeze(1).broadcast_to([P, U, D]), ALU.mult).then_inc(mul, 1)
                dve.wait_ge(mul, s + 2)
                nc.vector.tensor_reduce(part[:, :, :], leaky[:, b, :].rearrange("p (u h d) -> p u h d", u=U, h=HEADS),
                                        AX_X, ALU.add).then_inc(reduced, 1)
                dve.wait_ge(reduced, s + 1)
                nc.vector.tensor_tensor(S[:, bass.ds(s * U, U), :], part[:, :, :], lin[:, b, :, :], ALU.add).then_inc(scored, 1)

            build_onehot(0, 16)
            with dve.Fori(0, STEPS // 2) as i:
                for b in range(2):
                    s = i * 2 + b
                    dve.wait_ge(expanded, s + 2)
                    build_onehot(1 - b, i * 16 + 16 + 16 * b)
                    dve.wait_ge(expanded, s + 3)
                    dve.wait_ge(gathered[b], i * (16 * U) + 16 * U)
                    dve.wait_ge(scored, s + 1)
                    nc.vector.tensor_tensor(lin[:, b, :, :], psE[b][:, U * D:U * DX].rearrange("p (u h) -> p u h", u=U),
                                            G[b][:, :, D:DX], ALU.add).then_inc(lin_set, 1)
                    nc.vector.tensor_tensor(esum[:, b, :].rearrange("p (u f) -> p u f", u=U),
                                            psE[b][:, 0:U * D].rearrange("p (u f) -> p u f", u=U), G[b][:, :, 0:D],
                                            ALU.add).then_inc(summed, 1)
                    score(1 - b, s)
            score(1, STEPS)
            dve.wait_ge(scored, STEPS + 2)


def softmax_phase(nc, v):
    ident, S, A, valid, gd, xs_d, ys_d, W1, W2, w1, w2, w_in = (
        v[k] for k in "ident S A valid gd xs_d ys_d W1 W2 w1 w2 w_in".split())
    with ExitStack() as ctx:
        def sb(name, shape, dt=F32):
            return ctx.enter_context(nc.sbuf_tensor(name, shape, dt))

        def sem(name):
            return ctx.enter_context(nc.semaphore(name))

        full = [CI, CH, HEADS, P]
        T = sb("T", full)
        fpen = sb("fpen", full)
        bpen = sb("bpen", full)
        fwd = sb("fwd", full)
        bwd = sb("bwd", full)
        tot = sb("tot", full)
        cut = sb("cut", [CI, CH, P + 1])
        nvalid = sb("nvalid", [CI, CH, P])
        first = sb("first", [CI, CH, P])
        last_ = sb("last_", [CI, CH, P])
        keep = sb("keep", [CI, 2, CH, P])
        ends = sb("ends", [CI, 4, CH, HEADS])
        row = sb("row", [HEADS, 4, NI])
        link = sb("link", [HEADS, NI + 1])
        solid = sb("solid", [HEADS, NI])
        d0 = sb("d0", [HEADS, 2, NI])
        carry = sb("carry", [HEADS, 2, NI + 1])
        cin = sb("cin", [CI, 2, CH, HEADS])
        pd0 = sb("pd0", [HEADS, 2, NI])
        plink = sb("plink", [HEADS, NI + 1])
        psS = [ctx.enter_context(nc.psum_tensor(f"psS{c}", [P, 512], F32)) for c in range(CH)]
        psR = [ctx.enter_context(nc.psum_tensor(f"psR{j}", [P, 512], F32)) for j in range(4)]
        psC = ctx.enter_context(nc.psum_tensor("psC", [P, 512], F32))
        psA = psR

        dv, pes = sem("dv_soft"), sem("pe_soft")
        ready = sem("ready")
        done = sem("done_pe")
        shifted, expd = sem("shifted"), sem("expd")
        zslot = sb("zslot", [CAP, D])
        zset, zout = sem("zslot_set"), sem("zslot_out")
        block = ctx.enter_context(nc.Block())

        @block.sync
        def _(sp):
            sp.wait_ge(zset, 1)
            sp.dma_start(xs_d.rearrange("(b s) f -> s b f", s=CAP), zslot[:, :].unsqueeze(1).broadcast_to([CAP, NE + OVB, D])
                          ).then_inc(zout, 16)
            sp.dma_start(ys_d[NE * CAP:SLOTS, :].rearrange("(b s) f -> s b f", s=CAP),
                          zslot[:, :].unsqueeze(1).broadcast_to([CAP, OVB, D])).then_inc(zout, 16)
            for q in range(RING):
                load_weights(sp, W1, W2, w1, w2, w_in, q, q)
            sp.wait_ge(zout, 32)

        @block.gpsimd
        def _(g):
            nc.gpsimd.memset(zslot[:, :], 0.0).then_inc(zset, 1)

        @block.tensor
        def _(pe):
            for c in range(CH):
                for h in range(HEADS):
                    last = nc.tensor.transpose(psS[c][0:CI, h * P:(h + 1) * P], S[:, U + c * CI:U + (c + 1) * CI, h], ident[:, :])
            last.then_inc(done, 1)
            for r in range(2):
                pe.wait_ge(ready, 2 * r + 1)
                for j in range(4 if r == 0 else 2):
                    for c in range(CH):
                        last = nc.tensor.transpose(psR[j][0:HEADS, c * CI:(c + 1) * CI], ends[:, j, c, :], ident[0:CI, 0:CI])
                last.then_inc(done, 1)
                pe.wait_ge(ready, 2 * r + 2)
                for j in range(2):
                    for c in range(CH):
                        q = (j * CH + c) * HEADS
                        last = nc.tensor.transpose(psC[0:CI, q:q + HEADS], carry[:, j, c * CI + j:(c + 1) * CI + j],
                                                   ident[0:HEADS, 0:HEADS])
                last.then_inc(done, 1)
            pe.wait_ge(ready, 5)
            for h in range(HEADS):
                for c in range(CH):
                    last = nc.tensor.transpose(psA[h][:, c * CI:(c + 1) * CI], T[:, c, h, :], ident[0:CI, 0:CI])
            last.then_inc(done, 1)

        @block.scalar
        def _(act):
            act.wait_ge(shifted, 1)
            nc.scalar.activation(T[:, :, :, :], T[:, :, :, :], ACT.Exp).then_inc(expd, 1)

        @block.vector
        def _(dve):
            c = Chain(dve, dv)
            V = nc.vector

            def flat(a):
                return a[:, :, :, :].rearrange("p c h e -> p (c h e)")

            def scans(data, op, dead):
                c(V.tensor_tensor_scan(flat(fwd), flat(fpen), flat(data), dead, ALU.add if op is ALU.max else ALU.mult, op))
                c(V.tensor_tensor_scan(flat(bwd)[:, ::-1], flat(bpen)[:, ::-1], flat(data)[:, ::-1], dead,
                                       ALU.add if op is ALU.max else ALU.mult, op))
                dve.wait_ge(dv, c.n)
                c(V.tensor_copy(ends[:, 0, :, :], fwd[:, :, :, P - 1]))
                c.then(V.tensor_copy(ends[:, 1, :, :], bwd[:, :, :, 0]))

            c.then(V.memset(cut[:, :, :], 1.0))
            c(V.tensor_tensor(cut[:, :, 1:P], gd[:, :, 1:P], gd[:, :, 0:P - 1], ALU.not_equal))
            c(V.tensor_scalar(nvalid[:, :, :], valid[:, :, :], -1.0, BIG, ALU.add, ALU.mult))
            for j in range(CH):
                c(V.tensor_scalar(keep[:, 0, j, :], gd[:, j, :], gd[:, j, 0:1], None, ALU.is_equal))
                c(V.tensor_scalar(keep[:, 1, j, :], gd[:, j, :], gd[:, j, P - 1:P], None, ALU.is_equal))
            dve.wait_ge(dv, c.n)
            c(V.tensor_scalar(first[:, :, :], keep[:, 0, :, :], -1.0, BIG, ALU.add, ALU.mult))
            c(V.tensor_scalar(last_[:, :, :], keep[:, 1, :, :], -1.0, BIG, ALU.add, ALU.mult))
            for h in range(HEADS):
                c(V.tensor_scalar(fpen[:, :, h, :], cut[:, :, 0:P], -BIG, None, ALU.mult))
                c(V.tensor_scalar(bpen[:, :, h, :], cut[:, :, 1:P + 1], -BIG, None, ALU.mult))
                c(V.tensor_copy(ends[:, 2, :, h], gd[:, :, 0]))
                c(V.tensor_copy(ends[:, 3, :, h], gd[:, :, P - 1]))
            dve.wait_ge(done, 1)
            for k in range(CH):
                c(V.tensor_tensor(T[:, k, :, :], psS[k][0:CI, :].rearrange("p (h e) -> p h e", h=HEADS),
                                  valid[:, k, :].unsqueeze(1).broadcast_to([CI, HEADS, P]), ALU.mult))
            dve.wait_ge(dv, c.n)
            for k in range(CH):
                c(V.tensor_tensor(T[:, k, :, :], T[:, k, :, :],
                                  nvalid[:, k, :].unsqueeze(1).broadcast_to([CI, HEADS, P]), ALU.add))
            dve.wait_ge(dv, c.n)
            scans(T, ALU.max, -BIG)
            dve.sem_inc(ready, 1)
            dve.wait_ge(done, 2)
            for j in range(4):
                c(V.tensor_copy(row[:, j, :], psR[j][0:HEADS, 0:NI]))
            dve.wait_ge(dv, c.n)
            c.then(V.memset(link[:, :], 0.0))
            c(V.tensor_tensor(link[:, 1:NI], row[:, 2, 1:NI], row[:, 3, 0:NI - 1], ALU.is_equal))
            c.then(V.tensor_tensor(solid[:, :], row[:, 2, :], row[:, 3, :], ALU.is_equal))

            def pen(dst_, src_):
                c(V.tensor_scalar(dst_, src_, -1.0, BIG, ALU.add, ALU.mult))

            c(V.tensor_tensor(d0[:, 0, :], link[:, 0:NI], solid[:, :], ALU.mult))
            c.then(V.tensor_tensor(d0[:, 1, :], link[:, 1:NI + 1], solid[:, :], ALU.mult))
            pen(pd0[:, :, :], d0[:, :, :])
            pen(plink[:, :], link[:, :])
            dve.wait_ge(dv, c.n)
            c(V.memset(carry[:, 0, 0:1], -BIG))
            c(V.memset(carry[:, 1, NI:NI + 1], -BIG))
            c(V.tensor_tensor_scan(carry[:, 0, 1:NI + 1], pd0[:, 0, :], row[:, 0, :], -BIG, ALU.add, ALU.max))
            c.then(V.tensor_tensor_scan(carry[:, 1, 0:NI][:, ::-1], pd0[:, 1, :][:, ::-1], row[:, 1, :][:, ::-1], -BIG,
                                        ALU.add, ALU.max))
            c(V.tensor_tensor(carry[:, 0, 0:NI], carry[:, 0, 0:NI], plink[:, 0:NI], ALU.add))
            c.then(V.tensor_tensor(carry[:, 1, 1:NI + 1], carry[:, 1, 1:NI + 1], plink[:, 1:NI + 1], ALU.add))
            dve.sem_inc(ready, 1)
            dve.wait_ge(done, 3)
            c.then(V.tensor_copy(cin[:, :, :, :], psC[0:CI, 0:2 * CH * HEADS].rearrange("p (j c h) -> p j c h", j=2, c=CH)))
            c.then(V.tensor_tensor(flat(tot), flat(fwd), flat(bwd), ALU.max))
            for j, mark in ((0, first), (1, last_)):
                for k in range(CH):
                    for h in range(HEADS):
                        c(V.scalar_tensor_tensor(out=tot[:, k, h, :], in0=mark[:, k, :], scalar=cin[:, j, k, h:h + 1],
                                                 in1=tot[:, k, h, :], op0=ALU.add, op1=ALU.max))
                dve.wait_ge(dv, c.n)
            c.then(V.tensor_tensor(flat(T), flat(T), flat(tot), ALU.subtract))
            dve.sem_inc(shifted, 1)
            dve.wait_ge(expd, 1)
            for k in range(CH):
                c(V.tensor_tensor(T[:, k, :, :], T[:, k, :, :],
                                  valid[:, k, :].unsqueeze(1).broadcast_to([CI, HEADS, P]), ALU.mult))
            c(V.tensor_scalar(flat(fpen), flat(fpen), 0.0, None, ALU.is_equal))
            c(V.tensor_scalar(flat(bpen), flat(bpen), 0.0, None, ALU.is_equal))
            dve.wait_ge(dv, c.n)
            scans(T, ALU.add, 0.0)
            dve.sem_inc(ready, 1)
            dve.wait_ge(done, 4)
            for j in range(2):
                c(V.tensor_copy(row[:, j, :], psR[j][0:HEADS, 0:NI]))
            dve.wait_ge(dv, c.n)
            c(V.memset(carry[:, 0, 0:1], 0.0))
            c(V.memset(carry[:, 1, NI:NI + 1], 0.0))
            c(V.tensor_tensor_scan(carry[:, 0, 1:NI + 1], d0[:, 0, :], row[:, 0, :], 0.0, ALU.mult, ALU.add))
            c.then(V.tensor_tensor_scan(carry[:, 1, 0:NI][:, ::-1], d0[:, 1, :][:, ::-1], row[:, 1, :][:, ::-1], 0.0,
                                        ALU.mult, ALU.add))
            c(V.tensor_tensor(carry[:, 0, 0:NI], carry[:, 0, 0:NI], link[:, 0:NI], ALU.mult))
            c.then(V.tensor_tensor(carry[:, 1, 1:NI + 1], carry[:, 1, 1:NI + 1], link[:, 1:NI + 1], ALU.mult))
            dve.sem_inc(ready, 1)
            dve.wait_ge(done, 5)
            c(V.tensor_copy(cin[:, :, :, :], psC[0:CI, 0:2 * CH * HEADS].rearrange("p (j c h) -> p j c h", j=2, c=CH)))
            c.then(V.tensor_tensor(flat(tot), flat(fwd), flat(bwd), ALU.add))
            c.then(V.tensor_tensor(flat(tot), flat(tot), flat(T), ALU.subtract))
            for j in range(2):
                for k in range(CH):
                    for h in range(HEADS):
                        c(V.scalar_tensor_tensor(out=tot[:, k, h, :], in0=keep[:, j, k, :], scalar=cin[:, j, k, h:h + 1],
                                                 in1=tot[:, k, h, :], op0=ALU.mult, op1=ALU.add))
                dve.wait_ge(dv, c.n)
            c.then(V.tensor_scalar(flat(tot), flat(tot), SM_EPS, None, ALU.add))
            c.then(V.reciprocal(flat(tot), flat(tot)))
            c.then(V.tensor_tensor(flat(T), flat(T), flat(tot), ALU.mult))
            dve.sem_inc(ready, 1)
            dve.wait_ge(done, 6)
            for h in range(HEADS):
                c(V.tensor_copy(A[:, :, h], psA[h][:, 0:NI]))
            dve.wait_ge(dv, c.n)


def aggregate_phase(nc, v):
    (gathered_d, iota32, A, REL, wrow, bg, xs, xn, h_in) = (v[k] for k in "gathered_d iota32 A REL wrow bg xs xn h_in".split())
    R2 = 3
    with ExitStack() as ctx:
        def sb(name, shape, dt=F32):
            return ctx.enter_context(nc.sbuf_tensor(name, shape, dt))

        def sem(name):
            return ctx.enter_context(nc.semaphore(name))

        R = [sb(f"R{b}", [P, U * D]) for b in range(R2)]
        msg = [sb(f"msg{b}", [P, U * D]) for b in range(R2)]
        M = [sb(f"M32_{b}", [P, U * P]) for b in range(R2)]
        zero = sb("zero", [P, 512])
        o = sb("o", [P, NW, D])
        eneg = sb("eneg", [P, NW, D])
        stats = sb("stats2", [P, 2, NW, 6])
        mv = sb("mv2", [P, 2, NW, 2])
        vare = sb("vare", [P, 2, NW])
        std = sb("std2", [P, 2, NW])
        rstd = sb("rstd2", [P, 2, NW])
        agg = ctx.enter_context(nc.psum_tensor("agg", [P, NW * D], F32))

        loaded = [sem(f"loaded{b}") for b in range(R2)]
        zset, zeroed = sem("zset"), sem("agg_zeroed")
        weighted = sem("weighted")
        added = sem("added")
        dv, negd, expd, vard, rooted = map(sem, ("dv_agg", "negd", "expd2", "vard", "rooted2"))
        block = ctx.enter_context(nc.Block())

        @block.sync
        def _(sp):
            with sp.Fori(0, STEPS // R2) as i:
                for b in range(R2):
                    s = i * R2 + b
                    sp.wait_ge(weighted, s + 1)
                    sp.dma_start(R[b][:, :], gathered_d[bass.ds(s, 1), :, :].rearrange("s p f -> (s p) f")
                                 ).then_inc(loaded[b], 16)

        @block.tensor
        def _(pe):
            pe.sem_inc(added, R2)
            regs = [pe.alloc_register(f"agg_window{u}") for u in range(U)]
            pe.wait_ge(zset, 1)
            for j in range(NW * D // 512):
                last = nc.tensor.matmul(agg[:, j * 512:(j + 1) * 512], zero[:, 0:P], zero[:, :], start=True, stop=False,
                                        skip_group_check=True)
            with pe.Fori(0, STEPS // R2) as i:
                for b in range(R2):
                    s = i * R2 + b
                    ws = load_windows(pe, regs, wrow, s)
                    pe.wait_ge(weighted, s + R2 + 1)
                    for u in range(U):
                        w = ws[u]
                        last = nc.tensor.matmul(agg[:, bass.ds(w * D, D)], M[b][:, u * P:(u + 1) * P],
                                                msg[b][:, u * D:(u + 1) * D], start=False, stop=False, skip_group_check=True)
                    last.then_inc(added, 1)

        @block.scalar
        def _(act):
            act.wait_ge(negd, 1)
            nc.scalar.activation(eneg[:, :, :], eneg[:, :, :], ACT.Exp).then_inc(expd, 1)
            for r in range(2):
                act.wait_ge(vard, r + 1)
                nc.scalar.activation(std[:, r, :], vare[:, r, :], ACT.Sqrt).then_inc(rooted, 1)

        @block.vector
        def _(dve):
            V = nc.vector
            dve.sem_inc(weighted, R2)
            V.memset(zero[:, :], 0.0).then_inc(zset, 1)
            with dve.Fori(0, STEPS // R2) as i:
                for b in range(R2):
                    s = i * R2 + b
                    dve.wait_ge(added, s + 1)
                    for u in range(U):
                        V.tensor_scalar(M[b][:, u * P:(u + 1) * P], iota32[:, :], REL[:, bass.ds(s * U + u, 1)], None,
                                        ALU.is_equal)
                    dve.wait_ge(loaded[b], i * 16 + 16)
                    V.tensor_tensor(msg[b][:, :].rearrange("p (u d) -> p u d", d=HD), R[b][:, :].rearrange("p (u d) -> p u d", d=HD),
                                    A[:, bass.ds(s * U, U), :].rearrange("p u h -> p (u h)").unsqueeze(2).broadcast_to([P, U * HEADS, HD]),
                                    ALU.mult).then_inc(weighted, 1)
            c = Chain(dve, dv)
            dve.wait_ge(added, STEPS + R2)

            def every(a):
                return a.unsqueeze(1).broadcast_to([P, NW, D])

            c.then(V.tensor_tensor(o[:, :, :], agg[:, :].rearrange("p (w f) -> p w f", w=NW), every(bg[:, 0, :]), ALU.add))
            V.tensor_scalar(eneg[:, :, :], o[:, :, :], 0.0, None, ALU.min).then_inc(negd, 1)
            dve.wait_ge(expd, 1)
            c.then(V.scalar_tensor_tensor(out=o[:, :, :], in0=o[:, :, :], scalar=0.0, in1=eneg[:, :, :], op0=ALU.max, op1=ALU.add))
            c.then(V.scalar_tensor_tensor(out=o[:, :, :], in0=o[:, :, :], scalar=-1.0, in1=xn[:, :, :], op0=ALU.add, op1=ALU.add))

            def layer_norm(r, to, of):
                for w in range(NW):
                    c(V.bn_stats(stats[:, r, w, :], of[:, w, :]))
                dve.wait_ge(dv, c.n)
                for w in range(NW):
                    c(V.bn_aggr(mv[:, r, w, :], stats[:, r, w, :]))
                dve.wait_ge(dv, c.n)
                V.tensor_scalar(vare[:, r, :], mv[:, r, :, 1], LN_EPS, None, ALU.add).then_inc(vard, 1)
                dve.wait_ge(rooted, r + 1)
                c.then(V.reciprocal(rstd[:, r, :], std[:, r, :]))
                for w in range(NW):
                    c(V.tensor_scalar(to[:, w, :], of[:, w, :], mv[:, r, w, 0:1], rstd[:, r, w:w + 1], ALU.subtract, ALU.mult))
                dve.wait_ge(dv, c.n)

            layer_norm(0, o, o)
            c.then(V.tensor_tensor(o[:, :, :], o[:, :, :], every(bg[:, 1, :]), ALU.mult))
            c.then(V.tensor_tensor(o[:, :, :], o[:, :, :], every(bg[:, 2, :]), ALU.add))
            c.then(V.tensor_tensor(xs[:, :, :], xs[:, :, :], o[:, :, :], ALU.add))
            layer_norm(1, h_in, xs)


def route_phase(nc, v):
    (ident, prow, iota32, Rw, Rb, b1, b2, b2_d, xs_d, h_in, gates, slot, nov, ovx, b1T) = (v[k] for k in (
        "ident prow iota32 Rw Rb b1 b2 b2_d xs_d h_in gates slot nov ovx b1T").split())
    with ExitStack() as ctx:
        def sb(name, shape, dt=F32):
            return ctx.enter_context(nc.sbuf_tensor(name, shape, dt))

        def sem(name):
            return ctx.enter_context(nc.semaphore(name))

        Rws = sb("Rws", [P, KC, NE])
        Rbb = sb("Rbb", [P, NE])
        hT = sb("hTr", [P, KC, NPAD])
        lg = sb("lg", [P, NW, NE])
        top = sb("top", [P, NW, 8])
        topi = sb("topi", [P, NW, 8], mybir.dt.uint32)
        topf = sb("topf", [P, NW, TOPK])
        pick = sb("pick", [P, TOPK, NW, NE])
        both = sb("both", [P, NW, NE], BF16)
        ones = sb("onesb", [P, P], BF16)
        tri = sb("tri", [P, P], BF16)
        live = sb("live", [P, 1])
        cnt = sb("cnt", [P, NE])
        more = sb("more", [P, NE])
        zrow = sb("zrow", [P, NE])
        upto = sb("upto", [P, NE + 1])
        first_at = sb("first_at", [P, NE])
        delta = sb("delta", [P, NE])
        rank = sb("rank", [P, NW, NE])
        fits = sb("fits", [P, NW, NE])
        slotf = sb("slotf", [P, NW, TOPK])
        diff = sb("diff", [P, NW])
        past = sb("past", [P, NE])
        ovc = sb("ovc", [P, 1])
        b2s = sb("b2s", [NE, D])
        b2r = sb("b2r", [NE, D])
        b2p = sb("b2p", [NE, 3, D], BF16)
        psT = ctx.enter_context(nc.psum_tensor("psTr", [P, 2, 512], F32))
        psL = ctx.enter_context(nc.psum_tensor("psL", [P, 2, 512], F32))
        psK = ctx.enter_context(nc.psum_tensor("psK", [P, 2, 512], F32))
        psN = ctx.enter_context(nc.psum_tensor("psN", [P, 512], F32))
        psO = ctx.enter_context(nc.psum_tensor("psO", [P, 512], F32))

        w_in, b2_in, b2_set, b2_out, dv, consts, hT_ps, hT_sb, lg_ps, picked, ranked, shifted, expd, slots, moved, ov_set, ov_ps = map(
            sem, ("rw_in", "b2_in", "b2_set", "b2_out", "dv_route", "consts_r", "hT_ps", "hT_sb", "lg_ps", "picked", "ranked",
                  "shifted_r", "expd_r", "slots", "moved", "ov_set", "ov_ps"))
        block = ctx.enter_context(nc.Block())

        @block.sync
        def _(sp):
            sp.dma_start(Rws[:, :, :], Rw.rearrange("(c p) n -> p c n", p=P)).then_inc(w_in, 16)
            sp.dma_start(Rbb[:, :], Rb.unsqueeze(0).broadcast_to([P, NE])).then_inc(w_in, 16)
            sp.dma_start(b2s[:, :], b2).then_inc(b2_in, 16)
            sp.dma_start(b1T[:, :, :], b1.rearrange("e (p m) -> p e m", m=HC)).then_inc(w_in, 16)
            sp.wait_ge(b2_set, 1)
            sp.dma_start(b2_d, b2p[:, :, :]).then_inc(b2_out, 16)
            sp.wait_ge(b2_out, 16)
            sp.wait_ge(w_in, 48)

        @block.scalar
        def _(act):
            for i in range(NW // 2):
                act.wait_ge(hT_ps, i + 1)
                nc.scalar.copy(hT[:, :, 2 * i * P:(2 * i + 2) * P].rearrange("p c (w q) -> p w c q", q=P),
                               psT[:, i % 2, :].rearrange("p (w c q) -> p w c q", w=2, c=KC)).then_inc(hT_sb, 1)
            act.wait_ge(shifted, 1)
            nc.scalar.activation(gates[:, :, 1], diff[:, :], ACT.Exp).then_inc(expd, 1)

        @block.gpsimd
        def _(g):
            nc.gpsimd.memset(ones[:, :], 1.0).then_inc(consts, 1)
            g.wait_ge(consts, 1)
            nc.gpsimd.affine_select(out=tri[:, :], in_=ones[:, :], compare_op=ALU.is_gt, fill=0.0, base=0,
                                    pattern=[[1, P]], channel_multiplier=-1).then_inc(consts, 1)
            g.wait_ge(slots, 1)
            for w in range(NW):
                n = P if w < NW - 1 else NREM
                for k in range(TOPK):
                    nc.gpsimd.indirect_dma_start(out=xs_d, out_offset=bass.IndirectOffsetOnAxis(ap=slot[0:n, k, w:w + 1], axis=0),
                                                 in_=h_in[0:n, w, :], in_offset=None).then_inc(moved, 16)
            g.wait_ge(moved, 16 * TOPK * NW)

        @block.tensor
        def _(pe):
            for i in range(NW // 2):
                if i >= 2:
                    pe.wait_ge(hT_sb, i - 1)
                for w in range(2):
                    for c in range(KC):
                        q = (w * KC + c) * P
                        last = nc.tensor.transpose(psT[:, i % 2, q:q + P], h_in[:, 2 * i + w, c * P:(c + 1) * P], ident[:, :])
                last.then_inc(hT_ps, 1)
            pe.wait_ge(hT_sb, NW // 2)
            pe.wait_ge(w_in, 48)
            for w in range(NW):
                for c in range(KC):
                    last = nc.tensor.matmul(psL[:, w // 8, (w % 8) * NE:(w % 8 + 1) * NE], hT[:, c, w * P:(w + 1) * P],
                                            Rws[:, c, :], start=(c == 0), stop=(c == KC - 1))
            last.then_inc(lg_ps, 1)
            pe.wait_ge(picked, 1)
            pe.wait_ge(consts, 2)
            for w in range(NW):
                to = psK[:, w // 8, (w % 8) * NE:(w % 8 + 1) * NE]
                for q in range(w):
                    nc.tensor.matmul(to, ones[:, :], both[:, q, :], start=(q == 0), stop=False)
                nc.tensor.matmul(to, tri[:, :], both[:, w, :], start=(w == 0), stop=True)
            for w in range(NW):
                last = nc.tensor.matmul(psN[:, 0:NE], ones[:, :], both[:, w, :], start=(w == 0), stop=(w == NW - 1))
            last.then_inc(ranked, 1)
            pe.wait_ge(ov_set, 1)
            nc.tensor.transpose(psO[0:1, 0:P], ovc[:, :], ident[:, :]).then_inc(ov_ps, 1)

        @block.vector
        def _(dve):
            V = nc.vector
            c = Chain(dve, dv)
            c(V.memset(zrow[:, :], 0.0))
            c(V.tensor_scalar(live[:, :], prow[:, :], float(NREM), None, ALU.is_lt))
            dve.wait_ge(b2_in, 16)
            c.then(V.tensor_copy(b2p[:, 0, :], b2s[:, :]))
            c.then(V.tensor_tensor(b2r[:, :], b2s[:, :], b2p[:, 0, :], ALU.subtract))
            c.then(V.tensor_copy(b2p[:, 1, :], b2r[:, :]))
            V.tensor_tensor(b2p[:, 2, :], b2r[:, :], b2p[:, 1, :], ALU.subtract).then_inc(b2_set, 1)
            dve.wait_ge(lg_ps, 1)
            for j, (lo, hi) in enumerate(((0, 8), (8, NW))):
                c(V.tensor_tensor(lg[:, lo:hi, :], psL[:, j, 0:(hi - lo) * NE].rearrange("p (w e) -> p w e", e=NE),
                                  Rbb[:, :].unsqueeze(1).broadcast_to([P, hi - lo, NE]), ALU.add))
            dve.wait_ge(dv, c.n)
            for w in range(NW):
                c(V.max(top[:, w, :], lg[:, w, :]))
            dve.wait_ge(dv, c.n)
            for w in range(NW):
                c(V.max_index(topi[:, w, :], top[:, w, :], lg[:, w, :]))
            V.tensor_tensor(diff[:, :], top[:, :, 1], top[:, :, 0], ALU.subtract).then_inc(shifted, 1)
            dve.wait_ge(dv, c.n)
            c.then(V.tensor_copy(topf[:, :, :], topi[:, :, 0:TOPK]))
            for k in range(TOPK):
                c(V.tensor_tensor(pick[:, k, :, :], iota32[:, 0:NE].unsqueeze(1).broadcast_to([P, NW, NE]),
                                  topf[:, :, k].unsqueeze(2).broadcast_to([P, NW, NE]), ALU.is_equal))
            dve.wait_ge(dv, c.n)
            c.then(V.tensor_tensor(both[:, :, :], pick[:, 0, :, :], pick[:, 1, :, :], ALU.add))
            V.tensor_scalar(both[:, NW - 1, :], both[:, NW - 1, :], live[:, 0:1], None, ALU.mult).then_inc(picked, 1)
            dve.wait_ge(expd, 1)
            c.then(V.tensor_scalar(gates[:, :, 0], gates[:, :, 1], 1.0, None, ALU.add))
            c.then(V.reciprocal(gates[:, :, 0], gates[:, :, 0]))
            c(V.tensor_tensor(gates[:, :, 1], gates[:, :, 1], gates[:, :, 0], ALU.mult))
            dve.wait_ge(ranked, 1)
            c(V.tensor_copy(cnt[:, :], psN[:, 0:NE]))
            c(V.tensor_copy(rank[:, 0:8, :], psK[:, 0, :].rearrange("p (w e) -> p w e", e=NE)))
            c.then(V.tensor_copy(rank[:, 8:NW, :], psK[:, 1, 0:(NW - 8) * NE].rearrange("p (w e) -> p w e", e=NE)))
            c.then(V.tensor_scalar(more[:, :], cnt[:, :], float(CAP), None, ALU.is_gt))
            for j in range(2, -(-N // CAP)):
                c.then(V.scalar_tensor_tensor(out=more[:, :], in0=cnt[:, :], scalar=float(j * CAP), in1=more[:, :],
                                              op0=ALU.is_gt, op1=ALU.add))
            c(V.memset(upto[:, 0:1], 0.0))
            c.then(V.tensor_tensor_scan(upto[:, 1:NE + 1], more[:, :], zrow[:, :], 0.0, ALU.add, ALU.add))
            c.then(V.tensor_scalar(first_at[:, :], upto[:, 0:NE], float(NE - 1), float(CAP), ALU.add, ALU.mult))
            c.then(V.scalar_tensor_tensor(out=delta[:, :], in0=iota32[:, 0:NE], scalar=float(CAP), in1=first_at[:, :],
                                          op0=ALU.mult, op1=ALU.subtract))

            def every(a):
                return a.unsqueeze(1).broadcast_to([P, NW, NE])

            c.then(V.tensor_scalar(fits[:, :, :], rank[:, :, :], float(CAP), None, ALU.is_lt))
            c.then(V.tensor_tensor(fits[:, :, :], fits[:, :, :], every(delta[:, :]), ALU.mult))
            c.then(V.tensor_tensor(rank[:, :, :], rank[:, :, :], every(first_at[:, :]), ALU.add))
            c.then(V.tensor_tensor(rank[:, :, :], rank[:, :, :], fits[:, :, :], ALU.add))
            for k in range(TOPK):
                c(V.tensor_tensor(pick[:, k, :, :], pick[:, k, :, :], rank[:, :, :], ALU.mult))
            dve.wait_ge(dv, c.n)
            for k in range(TOPK):
                c(V.tensor_reduce(slotf[:, :, k], pick[:, k, :, :], AX_X, ALU.add))
            dve.wait_ge(dv, c.n)
            V.tensor_copy(slot[:, :, :], slotf[:, :, :].rearrange("p w k -> p k w")).then_inc(slots, 1)
            c(V.tensor_copy(nov[:, :], upto[0:1, NE:NE + 1]))
            c.then(V.tensor_scalar(past[:, :], upto[:, 1:NE + 1], prow[:, 0:1], None, ALU.is_le))
            V.tensor_reduce(ovc[:, :], past[:, :], AX_X, ALU.add).then_inc(ov_set, 1)
            dve.wait_ge(ov_ps, 1)
            c(V.tensor_scalar(ovx[:, :], psO[0:1, 0:OVB], float(NE - 1), None, ALU.min))
            dve.wait_ge(dv, c.n)


def expert_phase(nc, v):
    (ident, W1, W2, b2_d, xs_d, ys_d, b1T) = (v[k] for k in "ident W1 W2 b2_d xs_d ys_d b1T".split())
    w1, w2, w_in = (v[k] for k in "w1 w2 w_in".split())
    with ExitStack() as ctx:
        def sb(name, shape, dt=F32):
            return ctx.enter_context(nc.sbuf_tensor(name, shape, dt))

        def sem(name):
            return ctx.enter_context(nc.semaphore(name))

        b2e = [sb(f"b2e_{r}", [3, D], BF16) for r in range(RING)]
        X = [sb(f"X{r}", [CAP, D]) for r in range(RING)]
        xT = sb("xT", [P, 2, KC * CAP])
        hid = sb("hid", [P, 2, HC * CAP])
        Y = [sb(f"Y{r}", [CAP, D]) for r in range(RING)]
        ones3 = sb("ones3", [3, CAP], BF16)
        psX = ctx.enter_context(nc.psum_tensor("psXe", [P, 2, 512], F32))
        psH = ctx.enter_context(nc.psum_tensor("psH", [P, 2, 512], F32))
        psY = ctx.enter_context(nc.psum_tensor("psY", [P, 2, 512], F32))

        x_in = [sem(f"xe_in{r}") for r in range(RING)]
        y_out = [sem(f"y_out{r}") for r in range(RING)]
        ones_set, biased = sem("ones_set"), sem("biased")
        turned = sem("turned_e")
        xT_set = sem("xT_set")
        hid_ps = sem("hid_ps")
        hid_set = sem("hid_set")
        y_ps = sem("y_ps")
        y_set = sem("y_set")
        block = ctx.enter_context(nc.Block())

        def load_tokens(sp, r, e):
            sp.dma_start(b2e[r][:, :], b2_d[bass.ds(e, 1), :, :].rearrange("e j n -> (e j) n")).then_inc(x_in[r], 16)
            sp.dma_start(X[r][:, :], xs_d[bass.ds(e * CAP, CAP), :]).then_inc(x_in[r], 16)

        @block.sync
        def _(sp):
            for r in range(RING):
                load_tokens(sp, r, r)
            with sp.Fori(1, NE // RING) as i:
                for r in range(RING):
                    sp.wait_ge(y_ps, i * RING + r + 1)
                    load_tokens(sp, r, i * RING + r)
                    load_weights(sp, W1, W2, w1, w2, w_in, r, i * RING + r)

        @block.gpsimd
        def _(g):
            for r in range(RING):
                g.wait_ge(y_out[r], 16 * (NE // RING) + 16)

        LASTG = NE // RING - 1

        def groups(eng, step):
            with eng.Fori(0, LASTG) as i:
                for r in range(RING):
                    step(i, r, RING)
            for r in range(RING):
                step(LASTG, r, RING - 1 - r)

        @block.tensor
        def _(pe):
            pe.sem_inc(y_ps, RING)
            pe.wait_ge(ones_set, 1)

            def turn(grp, r):
                e, b = grp * RING + r, r % 2
                r, grp = r % RING, grp + r // RING
                pe.wait_ge(x_in[r], grp * 32 + 32)
                pe.wait_ge(xT_set, e + 1)
                for c in range(KC):
                    last = nc.tensor.transpose(psX[:, b, c * CAP:(c + 1) * CAP], X[r][:, c::KC], ident[0:CAP, 0:CAP])
                last.then_inc(turned, 1)

            def first(grp, r):
                e, b = grp * RING + r, r % 2
                r, grp = r % RING, grp + r // RING
                pe.wait_ge(w_in[r], grp * 32 + 32)
                pe.wait_ge(xT_set, e + 3)
                pe.wait_ge(hid_set, e + 1)
                for m in range(HC):
                    for c in range(KC):
                        last = nc.tensor.matmul(psH[:, b, m * CAP:(m + 1) * CAP], w1[r][:, c, m::HC],
                                                xT[:, b, c * CAP:(c + 1) * CAP], start=(c == 0), stop=(c == KC - 1))
                last.then_inc(hid_ps, 1)

            def step(grp, r, left):
                e, b = grp * RING + r, r % 2
                if left >= 2:
                    turn(grp, r + 2)
                if left >= 1:
                    first(grp, r + 1)
                pe.wait_ge(hid_set, e + 3)
                pe.wait_ge(y_set, e + 1)
                for m in range(HC):
                    nc.tensor.matmul(psY[0:CAP, b, 0:D], hid[:, b, m * CAP:(m + 1) * CAP], w2[r][:, m, :],
                                     start=(m == 0), stop=False)
                nc.tensor.matmul(psY[0:CAP, b, 0:D], ones3[:, :], b2e[r][:, :], start=False, stop=True).then_inc(y_ps, 1)

            turn(0, 0)
            turn(0, 1)
            first(0, 0)
            groups(pe, step)

        @block.vector
        def _(dve):
            nc.vector.memset(ones3[:, :], 1.0).then_inc(ones_set, 1)
            dve.sem_inc(hid_set, 2)

            def hidden(grp, r):
                e, b = grp * RING + r, r % 2
                dve.wait_ge(hid_ps, e + 1)
                dve.wait_ge(y_ps, e + RING - 1)
                nc.vector.tensor_tensor(hid[:, b, :].rearrange("p (m t) -> p m t", m=HC),
                                        psH[:, b, 0:HC * CAP].rearrange("p (m t) -> p m t", m=HC),
                                        b1T[:, bass.ds(e, 1), :].rearrange("p e m -> p (e m)").unsqueeze(2).broadcast_to([P, HC, CAP]),
                                        ALU.add).then_inc(biased, 1)
                dve.wait_ge(biased, e + 1)
                nc.vector.tensor_scalar(hid[:, b, :], hid[:, b, :], 0.0, None, ALU.max).then_inc(hid_set, 1)

            def step(grp, r, left):
                if left >= 1:
                    hidden(grp, r + 1)

            hidden(0, 0)
            groups(dve, step)

        @block.scalar
        def _(act):
            act.sem_inc(xT_set, 2)
            act.sem_inc(y_set, 2)
            for r in range(RING):
                act.sem_inc(y_out[r], 16)

            def copy_x(grp, r):
                e, b = grp * RING + r, r % 2
                act.wait_ge(turned, e + 1)
                nc.scalar.copy(xT[:, b, :], psX[:, b, 0:KC * CAP]).then_inc(xT_set, 1)

            def step(grp, r, left):
                e, b = grp * RING + r, r % 2
                if left >= 2:
                    act.wait_ge(hid_ps, e + 1)
                    copy_x(grp, r + 2)
                act.wait_ge(y_ps, e + RING + 1)
                act.wait_ge(y_out[r], grp * 16 + 16)
                nc.scalar.copy(Y[r][:, :], psY[0:CAP, b, 0:D]).then_inc(y_set, 1)
                act.wait_ge(y_set, e + 3)
                act.dma_start(ys_d[bass.ds(e * CAP, CAP), :], Y[r][:, :]).then_inc(y_out[r], 16)

            copy_x(0, 0)
            copy_x(0, 1)
            groups(act, step)


def overflow_phase(nc, v):
    (ident, W1, W2, b2_d, xs_d, ys_d, b1T, nov, ovx) = (v[k] for k in "ident W1 W2 b2_d xs_d ys_d b1T nov ovx".split())
    with ExitStack() as ctx:
        def sb(name, shape, dt=F32):
            return ctx.enter_context(nc.sbuf_tensor(name, shape, dt))

        def sem(name):
            return ctx.enter_context(nc.semaphore(name))

        w1 = sb("ow1", [P, KC, HID])
        w2 = sb("ow2", [P, HC, D])
        b2e = sb("ob2e", [3, D], BF16)
        X = sb("oX", [CAP, D])
        xT = sb("oxT", [P, KC * CAP])
        hid = sb("ohid", [P, HC * CAP])
        Y = sb("oY", [CAP, D])
        ones3 = sb("oones3", [3, CAP], BF16)
        psX = ctx.enter_context(nc.psum_tensor("opsX", [P, 512], F32))
        psH = ctx.enter_context(nc.psum_tensor("opsH", [P, 512], F32))
        psY = ctx.enter_context(nc.psum_tensor("opsY", [P, 512], F32))
        came, went, turned, xT_set, hid_ps, biased, hid_set, y_ps, y_set = map(sem, (
            "came", "went", "oturned", "oxT_set", "ohid_ps", "obiased", "ohid_set", "oy_ps", "oy_set"))
        block = ctx.enter_context(nc.Block())

        @block.sync
        def _(sp):
            n = sp.value_load(nov[0:1, 0:1], min_val=0, max_val=OVB)
            with sp.If(n > 0):
                sp.sem_inc(went, 16)
                with sp.Fori(0, OVB) as k:
                    sp.wait_ge(went, k * 16 + 16)
                    e = sp.value_load(ovx[0:1, bass.ds(k, 1)], min_val=0, max_val=NE - 1)
                    sp.dma_start(w1[:, :, :], W1[bass.ds(e, 1), :, :].rearrange("e (p c) n -> (e p) c n", c=KC)).then_inc(came, 16)
                    sp.dma_start(w2[:, :, :], W2[bass.ds(e, 1), :, :].rearrange("e (p m) n -> (e p) m n", m=HC)).then_inc(came, 16)
                    sp.dma_start(b2e[:, :], b2_d[bass.ds(e, 1), :, :].rearrange("e j n -> (e j) n")).then_inc(came, 16)
                    sp.dma_start(X[:, :], xs_d[bass.ds((k + NE) * CAP, CAP), :]).then_inc(came, 16)
                    sp.wait_ge(y_set, k + 1)
                    sp.dma_start(ys_d[bass.ds((k + NE) * CAP, CAP), :], Y[:, :]).then_inc(went, 16)
                sp.wait_ge(went, OVB * 16 + 16)

        @block.tensor
        def _(pe):
            n = pe.value_load(nov[0:1, 0:1], min_val=0, max_val=OVB)
            with pe.If(n > 0):
                with pe.Fori(0, OVB) as k:
                    pe.wait_ge(came, k * 64 + 64)
                    for c in range(KC):
                        last = nc.tensor.transpose(psX[:, c * CAP:(c + 1) * CAP], X[:, c::KC], ident[0:CAP, 0:CAP])
                    last.then_inc(turned, 1)
                    pe.wait_ge(xT_set, k + 1)
                    for m in range(HC):
                        for c in range(KC):
                            last = nc.tensor.matmul(psH[:, m * CAP:(m + 1) * CAP], w1[:, c, m::HC],
                                                    xT[:, c * CAP:(c + 1) * CAP], start=(c == 0), stop=(c == KC - 1))
                    last.then_inc(hid_ps, 1)
                    pe.wait_ge(hid_set, k + 1)
                    for m in range(HC):
                        nc.tensor.matmul(psY[0:CAP, 0:D], hid[:, m * CAP:(m + 1) * CAP], w2[:, m, :], start=(m == 0), stop=False)
                    nc.tensor.matmul(psY[0:CAP, 0:D], ones3[:, :], b2e[:, :], start=False, stop=True).then_inc(y_ps, 1)

        @block.vector
        def _(dve):
            n = dve.value_load(nov[0:1, 0:1], min_val=0, max_val=OVB)
            with dve.If(n > 0):
                nc.vector.memset(ones3[:, :], 1.0)
                with dve.Fori(0, OVB) as k:
                    e = dve.value_load(ovx[0:1, bass.ds(k, 1)], min_val=0, max_val=NE - 1)
                    dve.wait_ge(turned, k + 1)
                    nc.vector.tensor_copy(xT[:, :], psX[:, 0:KC * CAP]).then_inc(xT_set, 1)
                    dve.wait_ge(hid_ps, k + 1)
                    nc.vector.tensor_tensor(hid[:, :].rearrange("p (m t) -> p m t", m=HC),
                                            psH[:, 0:HC * CAP].rearrange("p (m t) -> p m t", m=HC),
                                            b1T[:, bass.ds(e, 1), :].rearrange("p e m -> p (e m)").unsqueeze(2).broadcast_to([P, HC, CAP]),
                                            ALU.add).then_inc(biased, 1)
                    dve.wait_ge(biased, k + 1)
                    nc.vector.tensor_scalar(hid[:, :], hid[:, :], 0.0, None, ALU.max).then_inc(hid_set, 1)
                    dve.wait_ge(y_ps, k + 1)
                    nc.vector.tensor_copy(Y[:, :], psY[0:CAP, 0:D]).then_inc(y_set, 1)


def combine_phase(nc, v):
    out, xs, ys_d, slot, gates = (v[k] for k in "out xs ys_d slot gates".split())
    with ExitStack() as ctx:
        def sem(name):
            return ctx.enter_context(nc.semaphore(name))

        yg = ctx.enter_context(nc.sbuf_tensor("yg", [P, NW, TOPK, D], F32))
        fetched = [sem(f"fetched{w}") for w in range(NW)]
        half, full, outs = sem("half"), sem("full"), sem("outs")
        block = ctx.enter_context(nc.Block())

        @block.gpsimd
        def _(g):
            for w in range(NW):
                n = P if w < NW - 1 else NREM
                for k in range(TOPK):
                    nc.gpsimd.indirect_dma_start(out=yg[0:n, w, k, :], out_offset=None, in_=ys_d,
                                                 in_offset=bass.IndirectOffsetOnAxis(ap=slot[0:n, k, w:w + 1], axis=0)
                                                 ).then_inc(fetched[w], 16)

        @block.vector
        def _(dve):
            for w in range(NW):
                n = P if w < NW - 1 else NREM
                dve.wait_ge(fetched[w], 32)
                nc.vector.scalar_tensor_tensor(out=xs[0:n, w, :], in0=yg[0:n, w, 0, :], scalar=gates[0:n, w, 0:1],
                                               in1=xs[0:n, w, :], op0=ALU.mult, op1=ALU.add).then_inc(half, 1)
                dve.wait_ge(half, w + 1)
                nc.vector.scalar_tensor_tensor(out=xs[0:n, w, :], in0=yg[0:n, w, 1, :], scalar=gates[0:n, w, 1:2],
                                               in1=xs[0:n, w, :], op0=ALU.mult, op1=ALU.add).then_inc(full, 1)

        @block.sync
        def _(sp):
            for w in range(NW):
                n = P if w < NW - 1 else NREM
                sp.wait_ge(full, w + 1)
                sp.dma_start(out[w * P:w * P + n, :], xs[0:n, w, :]).then_inc(outs, 16)
            sp.wait_ge(outs, 16 * NW)


_INS = ["x", "src", "dst", "L0_gnn_W_l", "L0_gnn_W_r", "L0_gnn_att", "L0_gnn_bias", "L0_gnn_gamma", "L0_gnn_beta",
        "L0_ffn_Wr", "L0_ffn_br", "L0_ffn_W1", "L0_ffn_b1", "L0_ffn_W2", "L0_ffn_b2"]


def kernel(**inputs):
    import concourse.bacc as bacc
    from concourse.bass_utils import run_bass_kernel_spmd

    nc = bacc.Bacc("TRN2", target_bir_lowering=False, num_devices=1)
    arrays, args = {}, []
    for name in _INS:
        a = np.ascontiguousarray(inputs[name])
        arrays[f"in_{name}"] = a
        args.append(nc.dram_tensor(f"in_{name}", a.shape, mybir.dt.from_np(a.dtype), kind="ExternalInput").ap())
    args.append(nc.dram_tensor("out_x", (N, D), F32, kind="ExternalOutput").ap())
    gnn_moe(nc, *args)
    r = run_bass_kernel_spmd(nc, [arrays], core_ids=[0])
    return r.results[0]["out_x"]
```

```python
from contextlib import ExitStack

import numpy as np

import concourse.bass as bass
from concourse import mybir

ALU = mybir.AluOpType
ACT = mybir.ActivationFunctionType
AX_X = mybir.AxisListType.X
F32 = mybir.dt.float32
BF16 = mybir.dt.bfloat16
I32 = mybir.dt.int32

P = 128
N, D = 1250, 256
DX = D + 4
E = 40000
HEADS, HD = 4, 64
NW = -(-N // P)
NREM = N - (NW - 1) * P
NPAD = NW * P
TILES = -(-E // P)
U = 5
CH = 3
NI = -(-(TILES + NW - 1) // (2 * U * CH)) * 2 * U * CH
CI = NI // CH
STEPS = NI // U
ROWS = TILES + 1
EPAD = ROWS * P - E
BIG = 1e30
WPAD = 8
SLOPE = 0.2
LN_EPS = 1e-5
SM_EPS = 1e-16
NE, HID, TOPK = 64, 512, 2
KC, HC = D // P, HID // P
CAP = 96
RING = 8
OVB = (N * TOPK) // CAP
SLOTS = (NE + OVB) * CAP


class Chain:

    def __init__(self, eng, sem):
        self.eng, self.sem, self.n = eng, sem, 0

    def __call__(self, ins):
        ins.then_inc(self.sem, 1)
        self.n += 1
        return self.n

    def then(self, ins):
        self(ins)
        self.eng.wait_ge(self.sem, self.n)


def col(ap, *sizes):
    shape = list(ap.shape)
    for s in sizes:
        ap = ap.unsqueeze(len(shape))
        shape.append(s)
    return ap.broadcast_to(shape)


def load_weights(eng, W1, W2, w1, w2, w_in, q, e):
    eng.dma_start(w1[q][:, :, :], W1[bass.ds(e, 1), :, :].rearrange("e (p c) n -> (e p) c n", c=KC)).then_inc(w_in[q], 16)
    eng.dma_start(w2[q][:, :, :], W2[bass.ds(e, 1), :, :].rearrange("e (p m) n -> (e p) m n", m=HC)).then_inc(w_in[q], 16)


def load_windows(pe, regs, wrow, s):
    pe.load(regs, wrow[0:1, bass.ds(s, 1), 0:U].rearrange("o s u -> o (s u)"))
    return [pe.snap(x, min_val=0, max_val=NW - 1) for x in regs]


def gnn_moe(nc, x, src, dst, Wl, Wr, att, bias, gamma, beta, Rw, Rb, W1, b1, W2, b2, out):
    with ExitStack() as ctx:
        def sb(name, shape, dt=F32):
            return ctx.enter_context(nc.sbuf_tensor(name, shape, dt))

        def dram(name, shape, dt=F32):
            return nc.dram_tensor(name, shape, dt, kind="Internal").ap()

        def sem(name):
            return ctx.enter_context(nc.semaphore(name))

        srcp = dram("srcp", [ROWS, P], I32)
        dstp = dram("dstp", [ROWS, P], I32)
        xl_tab = dram("xl_tab", [NPAD, DX])
        gathered_d = dram("gathered_d", [STEPS, P, U * D])
        rel_d = dram("rel_d", [NI + 2 * U, P], BF16)
        xs_d = dram("xs_d", [SLOTS, D])
        ys_d = dram("ys_d", [SLOTS, D])
        b2_d = dram("b2_d", [NE, 3, D], BF16)

        ident = sb("ident", [P, P])
        prow = sb("prow", [P, 1])
        iota32 = sb("iota32", [P, P])
        xs = sb("xs", [P, NW, D])
        xn = sb("xn", [P, NW, D])
        bg = sb("bg", [P, 3, D])
        REL = sb("REL", [P, NI])
        wrow = sb("wrow", [1, STEPS, WPAD], I32)
        A = sb("A", [P, NI, HEADS])
        h_in = sb("h_in", [P, NW, D])
        gates = sb("gates", [P, NW, TOPK])
        slot = sb("slot", [P, TOPK, NW], I32)
        nov = sb("nov", [1, 1], I32)
        ovx = sb("ovx", [1, OVB], I32)
        b1T = sb("b1T", [P, NE, HC])

        w_in = [sem(f"w_in{q}") for q in range(RING)]
        w1, w2 = [], []
        with ExitStack() as graph:
            def gsb(name, shape, dt=F32):
                return graph.enter_context(nc.sbuf_tensor(name, shape, dt))

            iotai = gsb("iotai", [P, NI], I32)
            xr3 = gsb("xr3", [P, NW * 3 * DX], BF16)
            attb = gsb("attb", [P, D])
            S = gsb("S", [P, NI + U, HEADS])
            srcI = gsb("srcI", [P, NI + 3 * U], I32)
            valid = gsb("valid", [CI, CH, P])
            gd = gsb("gd", [CI, CH, P])
            pen = gsb("pen", [CI, CH * HEADS * P + 1])
            go_on = gsb("go_on", [CI, CH * HEADS * P + 1])
            masked = gsb("masked", [CI, CH, P])
            ends = gsb("ends", [CI, 2, CH, P])
            ends_pen = gsb("ends_pen", [CI, 2, CH, P])
            through = gsb("through", [HEADS, 2, NI])
            through_pen = gsb("through_pen", [HEADS, 2, NI])
            node_phase(nc, locals())
            score_phase(nc, locals())
            for q in range(RING):
                w1.append(ctx.enter_context(nc.sbuf_tensor(f"w1_{q}", [P, KC, HID], F32, side="right")))
                w2.append(ctx.enter_context(nc.sbuf_tensor(f"w2_{q}", [P, HC, D], F32, side="right")))
            softmax_phase(nc, locals())
        aggregate_phase(nc, locals())
        route_phase(nc, locals())
        expert_phase(nc, locals())
        overflow_phase(nc, locals())
        combine_phase(nc, locals())


def node_phase(nc, v):
    (x, src, dst, Wl, Wr, att, bias, gamma, beta, srcp, dstp, xl_tab, rel_d, ident, prow, iota32, iotai,
     xs, xn, xr3, attb, bg, S, REL, srcI, wrow, valid, gd) = (v[k] for k in (
         "x src dst Wl Wr att bias gamma beta srcp dstp xl_tab rel_d ident prow iota32 iotai "
         "xs xn xr3 attb bg S REL srcI wrow valid gd").split())
    with ExitStack() as ctx:
        def sb(name, shape, dt=F32):
            return ctx.enter_context(nc.sbuf_tensor(name, shape, dt))

        def sem(name):
            return ctx.enter_context(nc.semaphore(name))

        Wlr = sb("Wlr", [P, KC, 2 * D])
        pad = sb("pad", [1, 2, EPAD], I32)
        lastd = sb("lastd", [P, CH], I32)
        lastf = sb("lastf", [P, CH])
        iotak = sb("iotak", [P, NI])
        before = sb("before", [P, CH, NI])
        ones = sb("ones", [P, 1])
        trow = sb("trow", [1, NI])
        wrf = sb("wrf", [1, NI])
        kcol_i = sb("kcol_i", [CI, CH], I32)
        pcol_i = sb("pcol_i", [P, CH], I32)
        kcol = sb("kcol", [CI, CH])
        pcol = sb("pcol", [P, CH])
        tcol = sb("tcol", [CI, CH])
        wcol = sb("wcol", [CI, CH])
        tcol_i = sb("tcol_i", [CI, CH], I32)
        stats = sb("stats", [P, NW, 6])
        mv = sb("mv", [P, NW, 2])
        std = sb("std", [P, NW])
        rstd = sb("rstd", [P, NW])
        xnT = sb("xnT", [P, KC, NPAD])
        xlr = sb("xlr", [P, NW, 2, DX])
        Watt = sb("Watt", [P, KC, 2 * HEADS])
        watp = sb("watp", [P, KC, 2 * D])
        rem = sb("rem", [P, 2, DX])
        srcT = sb("srcT", [CI, CH, P], I32)
        dstT = sb("dstT", [CI, CH, P], I32)
        srcF = sb("srcF", [CI, CH, P])
        dstF = sb("dstF", [CI, CH, P])
        clampd = sb("clampd", [CI, CH, P])
        relm = sb("relm", [CI, CH, P])
        rel16 = sb("rel16", [CI, CH, P], BF16)
        psT = ctx.enter_context(nc.psum_tensor("psT", [P, 2, 512], F32))
        psX = ctx.enter_context(nc.psum_tensor("psX", [P, 2, 512], F32))
        psI = ctx.enter_context(nc.psum_tensor("psI", [P, 512], F32))
        psJ = ctx.enter_context(nc.psum_tensor("psJ", [P, 512], F32))
        psE = ctx.enter_context(nc.psum_tensor("psE", [P, 2, 512], F32))

        x_in, w_in, c_in, pad_set, tables, last_in, items_in, xl_out = map(sem, (
            "x_in", "w_in", "c_in", "pad_set", "tables", "last_in", "items_in", "xl_out"))
        consts, dv, rooted, normed, xT_ps, xT_sb, proj, xl_sb, xr_sb, before_set, t_ps, t_set, rel_set, rel_ps = map(
            sem, ("consts", "dv_node", "rooted", "normed", "xT_ps", "xT_sb", "proj", "xl_sb", "xr_sb",
                  "before_set", "t_ps", "t_set", "rel_set", "rel_ps"))
        iotas, zeroed = sem("iotas"), sem("zeroed")
        rel16_set, rel_out = sem("rel16_set"), sem("rel_out")
        var_set, proj_lin, watt_set = sem("var_set"), sem("proj_lin"), sem("watt_set")
        block = ctx.enter_context(nc.Block())

        @block.sync
        def _(sp):
            sp.wait_ge(zeroed, 1)
            sp.dma_start(xs[:, 0:NW - 1, :], x[0:(NW - 1) * P, :].rearrange("(w p) f -> p w f", p=P)).then_inc(x_in, 16)
            sp.dma_start(xs[0:NREM, NW - 1, :], x[(NW - 1) * P:N, :]).then_inc(x_in, 16)
            sp.dma_start(Wlr[:, :, 0:D], Wl.rearrange("(c p) n -> p c n", p=P)).then_inc(w_in, 16)
            sp.dma_start(Wlr[:, :, D:2 * D], Wr.rearrange("(c p) n -> p c n", p=P)).then_inc(w_in, 16)
            sp.wait_ge(xl_sb, NW)
            sp.dma_start(xl_tab.rearrange("(w p) f -> p w f", p=P), xlr[:, :, 0, :]).then_inc(xl_out, 16)
            sp.wait_ge(xl_out, 16)
            sp.wait_ge(rel16_set, 1)
            sp.dma_start(rel_d[0:NI, :].rearrange("(c k) e -> k c e", c=CH), rel16[:, :, :]).then_inc(rel_out, 16)
            sp.dma_start(rel_d[NI:NI + 2 * U, :], rel16[0:2 * U, 0, :]).then_inc(rel_out, 16)
            sp.wait_ge(rel_out, 32)

        @block.scalar
        def _(act):
            for i, (tab, a) in enumerate(((srcp, src), (dstp, dst))):
                flat = tab.rearrange("t e -> (t e)")
                act.dma_start(flat[0:E].rearrange("(a b) -> a b", a=16), a.rearrange("(a b) -> a b", a=16)).then_inc(tables, 16)
                act.wait_ge(pad_set, 2)
                act.dma_start(flat[E:E + EPAD].rearrange("(a b) -> a b", a=1), pad[0:1, i, :]).then_inc(tables, 16)
            act.wait_ge(tables, 64)
            act.wait_ge(zeroed, 2)
            for c in range(CH):
                n = min(P, TILES - c * P)
                act.dma_start(lastd[0:n, c:c + 1], dstp[c * P:c * P + n, P - 1:P],
                              allow_slow_non_contiguous=True).then_inc(last_in, 16)
            act.dma_start(attb[:, :], att.rearrange("h d -> (h d)").unsqueeze(0).broadcast_to([P, D])).then_inc(c_in, 16)
            for i, a in enumerate((bias, gamma, beta)):
                act.dma_start(bg[:, i, :], a.unsqueeze(0).broadcast_to([P, D])).then_inc(c_in, 16)
            act.wait_ge(var_set, 1)
            nc.scalar.activation(std[:, :], rstd[:, :], ACT.Sqrt).then_inc(rooted, 1)
            for i in range(NW // 2):
                act.wait_ge(xT_ps, i + 1)
                nc.scalar.copy(xnT[:, :, 2 * i * P:(2 * i + 2) * P].rearrange("p c (w q) -> p w c q", q=P),
                               psT[:, i % 2, :].rearrange("p (w c q) -> p w c q", w=2, c=KC)).then_inc(xT_sb, 1)
            for w in range(NW):
                act.wait_ge(proj, w + 1)
                nc.scalar.copy(xlr[:, w, :, 0:D], psX[:, w % 2, :].rearrange("p (j f) -> p j f", j=2))
                act.wait_ge(proj_lin, w + 1)
                nc.scalar.copy(xlr[:, w, :, D:DX], psT[:, w % 2, 0:2 * HEADS].rearrange("p (j h) -> p j h", j=2)).then_inc(xl_sb, 1)
            act.wait_ge(c_in, 64)

        @block.gpsimd
        def _(g):
            nc.gpsimd.memset(ident[:, :], 0.0).then_inc(consts, 1)
            nc.gpsimd.memset(pad[:, 0, :], 0).then_inc(pad_set, 1)
            nc.gpsimd.memset(pad[:, 1, :], NPAD - 1).then_inc(pad_set, 1)
            g.wait_ge(consts, 1)
            nc.gpsimd.affine_select(out=ident[:, :], in_=ident[:, :], compare_op=ALU.not_equal, fill=1.0, base=0,
                                    pattern=[[-1, P]], channel_multiplier=1).then_inc(consts, 1)
            nc.gpsimd.iota(iotai[:, :], pattern=[[1, NI]], base=0, channel_multiplier=0).then_inc(iotas, 1)
            nc.gpsimd.iota(kcol_i[:, :], pattern=[[CI, CH]], base=0, channel_multiplier=1).then_inc(iotas, 1)
            nc.gpsimd.iota(pcol_i[:, :], pattern=[[P, CH]], base=0, channel_multiplier=1).then_inc(iotas, 1)
            g.wait_ge(t_set, 1)
            g.wait_ge(tables, 64)
            for c in range(CH):
                for to, tab in ((srcT, srcp), (dstT, dstp)):
                    nc.gpsimd.indirect_dma_start(out=to[:, c, :], out_offset=None, in_=tab,
                                                 in_offset=bass.IndirectOffsetOnAxis(ap=tcol_i[:, c:c + 1], axis=0)
                                                 ).then_inc(items_in, 16)

        @block.tensor
        def _(pe):
            pe.wait_ge(consts, 2)
            pe.wait_ge(before_set, 1)
            for c in range(CH):
                nc.tensor.matmul(psI[0:1, 0:NI], ones[:, :], before[:, c, :], start=(c == 0), stop=(c == CH - 1))
            for m in range(CH):
                for c in range(CH):
                    last = nc.tensor.matmul(psJ[0:CI, m:m + 1], before[:, c, m * CI:(m + 1) * CI], ones[:, :],
                                            start=(c == 0), stop=(c == CH - 1))
            last.then_inc(t_ps, 1)
            pe.wait_ge(normed, NW)
            for i in range(NW // 2):
                if i >= 2:
                    pe.wait_ge(xT_sb, i - 1)
                for w in range(2):
                    for c in range(KC):
                        q = (w * KC + c) * P
                        last = nc.tensor.transpose(psT[:, i % 2, q:q + P], xn[:, 2 * i + w, c * P:(c + 1) * P], ident[:, :])
                last.then_inc(xT_ps, 1)
            pe.wait_ge(xT_sb, NW // 2)
            pe.wait_ge(w_in, 32)
            pe.wait_ge(watt_set, 1)
            for w in range(NW):
                if w >= 2:
                    pe.wait_ge(xl_sb, w - 1)
                for c in range(KC):
                    last = nc.tensor.matmul(psX[:, w % 2, :], xnT[:, c, w * P:(w + 1) * P], Wlr[:, c, :],
                                            start=(c == 0), stop=(c == KC - 1))
                last.then_inc(proj, 1)
                for c in range(KC):
                    last = nc.tensor.matmul(psT[:, w % 2, 0:2 * HEADS], xnT[:, c, w * P:(w + 1) * P], Watt[:, c, :],
                                            start=(c == 0), stop=(c == KC - 1))
                last.then_inc(proj_lin, 1)
            pe.wait_ge(rel_set, 1)
            for j, a in enumerate((srcF, relm)):
                for c in range(CH):
                    last = nc.tensor.transpose(psE[:, j, c * CI:(c + 1) * CI], a[:, c, :], ident[0:CI, 0:CI])
                last.then_inc(rel_ps, 1)

        @block.vector
        def _(dve):
            c = Chain(dve, dv)
            nc.vector.memset(xs[:, :, :], 0.0).then_inc(zeroed, 1)
            nc.vector.memset(lastd[:, :], 1 << 20).then_inc(zeroed, 1)
            c(nc.vector.memset(ones[:, :], 1.0))
            c(nc.vector.memset(S[:, :, :], 0.0))
            dve.wait_ge(consts, 2)
            dve.wait_ge(iotas, 3)
            c(nc.vector.tensor_copy(prow[:, :], pcol_i[:, 0:1]))
            c(nc.vector.tensor_copy(iota32[:, :], iotai[:, 0:P]))
            c(nc.vector.tensor_copy(iotak[:, :], iotai[:, :]))
            c(nc.vector.tensor_copy(kcol[:, :], kcol_i[:, :]))
            c(nc.vector.tensor_copy(pcol[:, :], pcol_i[:, :]))
            dve.wait_ge(last_in, 48)
            c.then(nc.vector.tensor_scalar(lastd[:, :], lastd[:, :], 7, None, ALU.logical_shift_right))
            c.then(nc.vector.tensor_copy(lastf[:, :], lastd[:, :]))
            c.then(nc.vector.tensor_tensor(lastf[:, :], lastf[:, :], pcol[:, :], ALU.add))
            for j in range(CH):
                c(nc.vector.tensor_scalar(before[:, j, :], iotak[:, :], lastf[:, j:j + 1], None, ALU.is_gt))
            dve.wait_ge(dv, c.n)
            dve.sem_inc(before_set, 1)
            dve.wait_ge(x_in, 32)
            for w in range(NW):
                c(nc.vector.bn_stats(stats[:, w, :], xs[:, w, :]))
            dve.wait_ge(dv, c.n)
            for w in range(NW):
                c(nc.vector.bn_aggr(mv[:, w, :], stats[:, w, :]))
            dve.wait_ge(dv, c.n)
            nc.vector.tensor_scalar(rstd[:, :], mv[:, :, 1], LN_EPS, None, ALU.add).then_inc(var_set, 1)
            dve.wait_ge(rooted, 1)
            c.then(nc.vector.reciprocal(rstd[:, :], std[:, :]))
            for w in range(NW):
                nc.vector.tensor_scalar(xn[:, w, :], xs[:, w, :], mv[:, w, 0:1], rstd[:, w:w + 1],
                                        ALU.subtract, ALU.mult).then_inc(normed, 1)
            dve.wait_ge(t_ps, 1)
            c.then(nc.vector.tensor_tensor(wrf[:, :], iotak[0:1, :], psI[0:1, 0:NI], ALU.subtract))
            c.then(nc.vector.tensor_scalar(wrow[:, :, 0:U], wrf[:, :].rearrange("o (s u) -> o s u", u=U), float(NW - 1), None, ALU.min))
            c.then(nc.vector.tensor_tensor(wcol[:, :], kcol[:, :], psJ[0:CI, 0:CH], ALU.subtract))
            c.then(nc.vector.tensor_scalar(wcol[:, :], wcol[:, :], float(NW - 1), float(P), ALU.min, ALU.mult))
            nc.vector.tensor_scalar(tcol_i[:, :], psJ[0:CI, 0:CH], float(ROWS - 1), None, ALU.min).then_inc(t_set, 1)
            dve.wait_ge(c_in, 64)
            dve.wait_ge(w_in, 32)
            c.then(nc.vector.tensor_tensor(watp[:, :, :].rearrange("p c (j f) -> p (c j) f", j=2),
                                           Wlr[:, :, :].rearrange("p c (j f) -> p (c j) f", j=2),
                                           attb[:, :].unsqueeze(1).broadcast_to([P, 2 * KC, D]), ALU.mult))
            c.then(nc.vector.tensor_reduce(Watt[:, :, :], watp[:, :, :].rearrange("p c (h d) -> p c h d", d=HD), AX_X, ALU.add))
            nc.vector.tensor_scalar(Watt[:, :, :], Watt[:, :, :], SLOPE, None, ALU.mult).then_inc(watt_set, 1)
            c.then(nc.vector.tensor_scalar(attb[:, :], attb[:, :], 1.0 - SLOPE, None, ALU.mult))
            for w in range(NW):
                part = [xr3[:, (3 * w + j) * DX:(3 * w + j + 1) * DX] for j in range(3)]
                dve.wait_ge(xl_sb, w + 1)
                c.then(nc.vector.tensor_copy(part[0], xlr[:, w, 1, :]))
                c.then(nc.vector.tensor_tensor(rem[:, 0, :], xlr[:, w, 1, :], part[0], ALU.subtract))
                c.then(nc.vector.tensor_copy(part[1], rem[:, 0, :]))
                nc.vector.tensor_tensor(part[2], rem[:, 0, :], part[1], ALU.subtract).then_inc(xr_sb, 1)
            dve.wait_ge(items_in, 16 * 2 * CH)
            c(nc.vector.tensor_copy(srcF[:, :, :], srcT[:, :, :]))
            c.then(nc.vector.tensor_copy(dstF[:, :, :], dstT[:, :, :]))
            for j in range(CH):
                c(nc.vector.tensor_scalar(dstF[:, j, :], dstF[:, j, :], wcol[:, j:j + 1], None, ALU.subtract))
            dve.wait_ge(dv, c.n)
            c.then(nc.vector.tensor_scalar(clampd[:, :, :], dstF[:, :, :], 0.0, float(P - 1), ALU.max, ALU.min))
            c.then(nc.vector.tensor_tensor(valid[:, :, :], clampd[:, :, :], dstF[:, :, :], ALU.is_equal))
            c.then(nc.vector.scalar_tensor_tensor(out=relm[:, :, :], in0=dstF[:, :, :], scalar=1.0, in1=valid[:, :, :],
                                                  op0=ALU.add, op1=ALU.mult))
            nc.vector.tensor_scalar(relm[:, :, :], relm[:, :, :], -1.0, None, ALU.add).then_inc(rel_set, 1)
            dve.wait_ge(rel_set, 1)
            nc.vector.tensor_copy(rel16[:, :, :], relm[:, :, :]).then_inc(rel16_set, 1)
            for j in range(CH):
                c(nc.vector.tensor_scalar(gd[:, j, :], clampd[:, j, :], wcol[:, j:j + 1], None, ALU.add))
            dve.wait_ge(rel_ps, 1)
            c(nc.vector.tensor_copy(srcI[:, 0:NI], psE[:, 0, 0:NI]))
            c(nc.vector.memset(srcI[:, NI:NI + 3 * U], 0))
            dve.wait_ge(rel_ps, 2)
            c(nc.vector.tensor_copy(REL[:, 0:NI], psE[:, 1, 0:NI]))
            dve.wait_ge(dv, c.n)


def score_phase(nc, v):
    xl_tab, gathered_d, rel_d, prow, xr3, attb, S, srcI, wrow = (
        v[k] for k in "xl_tab gathered_d rel_d prow xr3 attb S srcI wrow".split())
    ident, valid, gd, pen, go_on, masked, ends, ends_pen, through, through_pen = (
        v[k] for k in "ident valid gd pen go_on masked ends ends_pen through through_pen".split())
    GR, BODY = 3, 6
    assert STEPS % BODY == 0
    with ExitStack() as ctx:
        def sb(name, shape, dt=F32):
            return ctx.enter_context(nc.sbuf_tensor(name, shape, dt))

        def sem(name):
            return ctx.enter_context(nc.semaphore(name))

        idx = sb("idx", [P, GR, U], I32)
        G = [sb(f"G{g}", [P, U, DX]) for g in range(GR)]
        lin = sb("lin", [P, NI, HEADS])
        esum = sb("esum", [P, 2, U * D])
        leaky = sb("leaky", [P, 2, U * D])
        relb = [sb(f"relb{b}", [P, U * P], BF16) for b in range(2)]
        MT = sb("MT", [P, 2, U * P], BF16)
        cut = sb("cut", [CI, CH, P])
        pen1 = sb("pen1", [CI, CH, P])
        go_on1 = sb("go_on1", [CI, CH, P])
        link = sb("link", [HEADS, NI + 1])
        solid = sb("solid", [HEADS, NI])
        ends_gd = sb("ends_gd", [HEADS, 2, NI])
        linkc = sb("linkc", [CI, 2, CH])
        psE = [ctx.enter_context(nc.psum_tensor(f"psE{b}", [P, 3 * 512], F32)) for b in range(2)]
        psG = ctx.enter_context(nc.psum_tensor("psG", [P, 2, 512], F32))
        marks, ends_ps, linked, link_ps = sem("marks"), sem("ends_ps"), sem("linked"), sem("link_ps")
        cut_set, by_head = sem("cut_set"), sem("by_head")

        gathered = [sem(f"gathered{g}") for g in range(GR)]
        spilled = [sem(f"spilled{g}") for g in range(GR)]
        turn = sem("turn")
        idx_set = sem("idx_set")
        rel_in = [sem(f"rel_in{b}") for b in range(2)]
        onehot = sem("onehot")
        expanded = sem("expanded")
        summed = sem("summed")
        leaked = sem("leaked")
        weighted = sem("att_mul")
        scored = sem("scored")
        lin_set, totalled = sem("lin_set"), sem("totalled")
        block = ctx.enter_context(nc.Block())

        def steps(eng, step):
            with eng.Fori(0, STEPS // BODY) as i:
                for j in range(BODY):
                    step(i * BODY + j, j % 2, j % GR, i * (BODY // GR) + (j // GR + 1))

        @block.gpsimd
        def _(g):
            for r in range(GR):
                g.sem_inc(spilled[r], 16)

            def gather(s, b, r, n):
                g.wait_ge(summed, s + 1)
                g.sem_inc(turn, 1)
                g.wait_ge(spilled[r], n * 16)
                g.sem_inc(turn, 1)
                g.wait_ge(idx_set, s + 1)
                g.sem_inc(turn, 1)
                for u in range(U):
                    nc.gpsimd.indirect_dma_start(
                        out=G[r][:, u, :], out_offset=None, in_=xl_tab,
                        in_offset=bass.IndirectOffsetOnAxis(ap=idx[:, r, u:u + 1], axis=0)).then_inc(gathered[r], 16)

            steps(g, gather)

        @block.sync
        def _(sp):
            def load_rel(b, s):
                sp.dma_start(relb[b][:, :], rel_d[bass.ds(s * U, U), :].rearrange("(o u) e -> o (u e)", o=1)
                             .broadcast_to([P, U * P])).then_inc(rel_in[b], 16)

            def step(s, b, r, n):
                sp.wait_ge(onehot, s + 1)
                load_rel(b, s + 2)
                sp.wait_ge(gathered[r], n * (16 * U))
                sp.dma_start(gathered_d[bass.ds(s, 1), :, :].rearrange("s p f -> (s p) f"),
                             G[r][:, :, 0:D]).then_inc(spilled[r], 16)

            for b in range(2):
                load_rel(b, b)
            steps(sp, step)
            for r in range(GR):
                sp.wait_ge(spilled[r], 16 * (STEPS // GR + 1))
            for b in range(2):
                sp.wait_ge(rel_in[b], 16 * (STEPS // 2 + 1))

        @block.tensor
        def _(pe):
            pe.sem_inc(expanded, 2)
            regs = [pe.alloc_register(f"window{u}") for u in range(U)]
            for j, e in ((0, 0), (1, P - 1)):
                for c in range(CH):
                    last = nc.tensor.transpose(psG[0:HEADS, j, c * CI:(c + 1) * CI], gd[:, c, e:e + 1].broadcast_to([CI, HEADS]),
                                               ident[0:CI, 0:CI])
            last.then_inc(ends_ps, 1)
            pe.wait_ge(linked, 1)
            for j in range(2):
                for c in range(CH):
                    q = (j * CH + c) * HEADS
                    last = nc.tensor.transpose(psG[0:CI, 0, q:q + HEADS], link[:, c * CI + j:(c + 1) * CI + j],
                                               ident[0:HEADS, 0:HEADS])
            last.then_inc(link_ps, 1)

            def expand(s, b, r, n):
                ws = load_windows(pe, regs, wrow, s)
                pe.wait_ge(onehot, s + 1)
                pe.wait_ge(summed, s + GR - 1)
                for u in range(U):
                    w = ws[u]
                    for j in range(3):
                        last = nc.tensor.matmul(psE[b][:, u * D:(u + 1) * D], MT[:, b, u * P:(u + 1) * P],
                                                xr3[:, bass.ds(w * (3 * DX) + j * DX, D)],
                                                start=(j == 0), stop=(j == 2))
                    q = U * D + u * HEADS
                    for j in range(3):
                        last = nc.tensor.matmul(psE[b][:, q:q + HEADS], MT[:, b, u * P:(u + 1) * P],
                                                xr3[:, bass.ds(w * (3 * DX) + j * DX + D, HEADS)],
                                                start=(j == 0), stop=(j == 2))
                last.then_inc(expanded, 1)

            steps(pe, expand)

        @block.scalar
        def _(act):
            act.sem_inc(leaked, 1)

            def copy_idx(r, s):
                nc.scalar.copy(idx[:, r, :], srcI[:, bass.ds(s * U, U)]).then_inc(idx_set, 1)

            def leak(s, b, r, n):
                act.wait_ge(summed, s + GR + 1)
                act.wait_ge(scored, s + 1)
                nc.scalar.activation(leaky[:, b, :], esum[:, b, :], ACT.Relu).then_inc(leaked, 1)
                copy_idx(r, s + GR)

            for r in range(GR):
                copy_idx(r, r)
            for n, (one, each) in enumerate(((pen1, pen), (go_on1, go_on))):
                act.wait_ge(cut_set, n + 1)
                nc.scalar.copy(each[:, 0:CH * HEADS * P].rearrange("p (c h e) -> p c h e", c=CH, h=HEADS),
                               one[:, :, :].unsqueeze(2).broadcast_to([CI, CH, HEADS, P])).then_inc(by_head, 1)
            steps(act, leak)
            act.wait_ge(by_head, 2)

        @block.vector
        def _(dve):
            dve.sem_inc(summed, GR)
            nc.vector.memset(leaky[:, 1, :], 0.0).then_inc(scored, 1)
            dve.wait_ge(scored, 1)

            def build_onehot(b, n):
                dve.wait_ge(rel_in[b], n)
                nc.vector.tensor_scalar(MT[:, b, :], relb[b][:, :], prow[:, 0:1], None, ALU.is_equal).then_inc(onehot, 1)

            def weight(b, s):
                dve.wait_ge(leaked, s + 1)
                nc.vector.tensor_tensor(leaky[:, b, :].rearrange("p (u f) -> p u f", u=U),
                                        leaky[:, b, :].rearrange("p (u f) -> p u f", u=U),
                                        attb[:, :].unsqueeze(1).broadcast_to([P, U, D]), ALU.mult).then_inc(weighted, 1)

            def dot(b, s):
                dve.wait_ge(weighted, s + 1)
                nc.vector.tensor_reduce(S[:, bass.ds(s * U, U), :], leaky[:, b, :].rearrange("p (u h d) -> p u h d", u=U, h=HEADS),
                                        AX_X, ALU.add).then_inc(scored, 1)

            def step(i, j):
                s, b, r = i * BODY + j, j % 2, j % GR
                weight(1 - b, s)
                dve.wait_ge(expanded, s + 2)
                build_onehot(1 - b, i * (16 * BODY // 2) + 16 * ((j + 1) // 2 + 1))
                dve.wait_ge(expanded, s + 3)
                dve.wait_ge(gathered[r], i * (BODY // GR * 16 * U) + (j // GR + 1) * 16 * U)
                nc.vector.tensor_tensor(esum[:, b, :].rearrange("p (u f) -> p u f", u=U),
                                        psE[b][:, 0:U * D].rearrange("p (u f) -> p u f", u=U), G[r][:, :, 0:D], ALU.add)
                nc.vector.tensor_tensor(lin[:, bass.ds(s * U, U), :], psE[b][:, U * D:U * DX].rearrange("p (u h) -> p u h", u=U),
                                        G[r][:, :, D:DX], ALU.add).then_inc(summed, 1)
                dot(1 - b, s)

            def mark_segments():
                c, V = Chain(dve, marks), nc.vector
                c(V.memset(cut[:, :, :], 1.0))
                c(V.memset(link[:, :], 0.0))
                c(V.memset(pen[:, CH * HEADS * P:CH * HEADS * P + 1], -BIG))
                c(V.memset(go_on[:, CH * HEADS * P:CH * HEADS * P + 1], 0.0))
                c(V.tensor_scalar(masked[:, :, :], valid[:, :, :], -1.0, 3 * BIG, ALU.add, ALU.mult))
                dve.wait_ge(ends_ps, 1)
                c(V.tensor_copy(ends_gd[:, :, :], psG[0:HEADS, :, 0:NI]))
                dve.wait_ge(marks, c.n)
                c(V.tensor_tensor(cut[:, :, 1:P], gd[:, :, 1:P], gd[:, :, 0:P - 1], ALU.not_equal))
                V.tensor_tensor(link[:, 1:NI], ends_gd[:, 0, 1:NI], ends_gd[:, 1, 0:NI - 1], ALU.is_equal).then_inc(linked, 1)
                c(V.tensor_tensor(solid[:, :], ends_gd[:, 0, :], ends_gd[:, 1, :], ALU.is_equal))
                dve.wait_ge(marks, c.n)
                dve.wait_ge(linked, 1)
                V.tensor_scalar(pen1[:, :, :], cut[:, :, :], -BIG, None, ALU.mult).then_inc(cut_set, 1)
                V.tensor_scalar(go_on1[:, :, :], cut[:, :, :], 0.0, None, ALU.is_equal).then_inc(cut_set, 1)
                c(V.tensor_tensor(through[:, 0, :], link[:, 0:NI], solid[:, :], ALU.mult))
                c(V.tensor_tensor(through[:, 1, :], link[:, 1:NI + 1], solid[:, :], ALU.mult))
                dve.wait_ge(link_ps, 1)
                c(V.tensor_copy(linkc[:, :, :], psG[0:CI, 0, 0:2 * CH * HEADS].rearrange(
                    "p (j c h) -> p j c h", j=2, c=CH)[:, :, :, 0]))
                dve.wait_ge(marks, c.n)
                c(V.tensor_scalar(through_pen[:, :, :], through[:, :, :], -1.0, BIG, ALU.add, ALU.mult))
                for j, e in ((0, 0), (1, P - 1)):
                    for k in range(CH):
                        c(V.tensor_scalar(ends[:, j, k, :], gd[:, k, :], gd[:, k, e:e + 1], linkc[:, j, k:k + 1],
                                          ALU.is_equal, ALU.mult))
                dve.wait_ge(marks, c.n)
                c.then(V.tensor_scalar(ends_pen[:, :, :, :], ends[:, :, :, :], -1.0, BIG, ALU.add, ALU.mult))

            build_onehot(0, 16)
            mark_segments()
            with dve.Fori(0, STEPS // BODY) as i:
                for j in range(BODY):
                    step(i, j)
            weight(1, STEPS)
            dot(1, STEPS)
            dve.wait_ge(scored, STEPS + 2)
            dve.wait_ge(summed, STEPS + GR)
            nc.vector.tensor_tensor(S[:, U:U + NI, :], S[:, U:U + NI, :], lin[:, :, :], ALU.add).then_inc(totalled, 1)
            dve.wait_ge(totalled, 1)


def softmax_phase(nc, v):
    ident, S, A, xs_d, ys_d, W1, W2, w1, w2, w_in = (
        v[k] for k in "ident S A xs_d ys_d W1 W2 w1 w2 w_in".split())
    pen, go_on, masked, ends, ends_pen, through, through_pen = (
        v[k] for k in "pen go_on masked ends ends_pen through through_pen".split())
    with ExitStack() as ctx:
        def sb(name, shape, dt=F32):
            return ctx.enter_context(nc.sbuf_tensor(name, shape, dt))

        def sem(name):
            return ctx.enter_context(nc.semaphore(name))

        full = [CI, CH, HEADS, P]
        T = sb("T", full)
        fwd = sb("fwd", full)
        bwd = sb("bwd", full)
        tot = sb("tot", full)
        carry = sb("carry", [HEADS, 2, NI + 1])
        cin = sb("cin", [CI, 2, CH, HEADS])
        psS = [ctx.enter_context(nc.psum_tensor(f"psS{c}", [P, 512], F32)) for c in range(CH)]
        psR = [ctx.enter_context(nc.psum_tensor(f"psR{j}", [P, 512], F32)) for j in range(2)]
        psC = ctx.enter_context(nc.psum_tensor("psC", [P, 512], F32))

        dv = sem("dv_soft")
        scores_ps = sem("scores_ps")
        scanned = [sem("scanned_fwd"), sem("scanned_bwd")]
        rows_ps = [sem("rows_fwd"), sem("rows_bwd")]
        carried, cin_ps = sem("carried"), sem("cin_ps")
        shifted, expd = sem("shifted"), sem("expd")
        alpha, alpha_ps, alpha_set = sem("alpha"), sem("alpha_ps"), sem("alpha_set")
        zslot = sb("zslot", [CAP, D])
        zset, zout = sem("zslot_set"), sem("zslot_out")
        block = ctx.enter_context(nc.Block())

        @block.sync
        def _(sp):
            sp.wait_ge(zset, 1)
            sp.dma_start(xs_d.rearrange("(b s) f -> s b f", s=CAP), zslot[:, :].unsqueeze(1).broadcast_to([CAP, NE + OVB, D])
                         ).then_inc(zout, 16)
            sp.dma_start(ys_d[NE * CAP:SLOTS, :].rearrange("(b s) f -> s b f", s=CAP),
                         zslot[:, :].unsqueeze(1).broadcast_to([CAP, OVB, D])).then_inc(zout, 16)
            for q in range(RING):
                load_weights(sp, W1, W2, w1, w2, w_in, q, q)
            sp.wait_ge(zout, 32)

        @block.gpsimd
        def _(g):
            nc.gpsimd.memset(zslot[:, :], 0.0).then_inc(zset, 1)

        @block.tensor
        def _(pe):
            for c in range(CH):
                for h in range(HEADS):
                    last = nc.tensor.transpose(psS[c][0:CI, h * P:(h + 1) * P], S[:, U + c * CI:U + (c + 1) * CI, h], ident[:, :])
                last.then_inc(scores_ps, 1)
            for r in range(2):
                for j, (scan, e) in enumerate(((fwd, P - 1), (bwd, 0))):
                    for c in range(CH):
                        pe.wait_ge(scanned[j], r * CH + c + 1)
                        last = nc.tensor.transpose(psR[j][0:HEADS, c * CI:(c + 1) * CI], scan[:, c, :, e], ident[0:CI, 0:CI])
                    last.then_inc(rows_ps[j], 1)
                for j in range(2):
                    pe.wait_ge(carried, 2 * r + j + 1)
                    for c in range(CH):
                        q = (j * CH + c) * HEADS
                        last = nc.tensor.transpose(psC[0:CI, q:q + HEADS], carry[:, j, c * CI + j:(c + 1) * CI + j],
                                                   ident[0:HEADS, 0:HEADS])
                last.then_inc(cin_ps, 1)
            for c in range(CH):
                pe.wait_ge(alpha, c + 1)
                for h in range(HEADS):
                    last = nc.tensor.transpose(psS[c][:, h * CI:(h + 1) * CI], T[:, c, h, :], ident[0:CI, 0:CI])
                last.then_inc(alpha_ps, 1)

        @block.scalar
        def _(act):
            for k in range(CH):
                act.wait_ge(shifted, k + 1)
                nc.scalar.activation(T[:, k, :, :], T[:, k, :, :], ACT.Exp).then_inc(expd, 1)
            for k in range(CH):
                act.wait_ge(alpha_ps, k + 1)
                nc.scalar.copy(A[:, k * CI:(k + 1) * CI, :], psS[k][:, 0:HEADS * CI].rearrange("p (h i) -> p i h", h=HEADS)
                               ).then_inc(alpha_set, 1)
            act.wait_ge(alpha_set, CH)

        @block.vector
        def _(dve):
            c = Chain(dve, dv)
            V = nc.vector

            def by_head(mark):
                return mark.unsqueeze(1).broadcast_to([CI, HEADS, P])

            def chunk(a, k):
                return a[:, k, :, :].rearrange("p h e -> p (h e)")

            def scan_chunk(k, marks, at_start, op0, op1):
                lo, hi = k * HEADS * P, (k + 1) * HEADS * P
                V.tensor_tensor_scan(chunk(fwd, k), marks[:, lo:hi], chunk(T, k), at_start, op0, op1).then_inc(scanned[0], 1)
                V.tensor_tensor_scan(chunk(bwd, k)[:, ::-1], marks[:, lo + 1:hi + 1][:, ::-1], chunk(T, k)[:, ::-1],
                                     at_start, op0, op1).then_inc(scanned[1], 1)

            def scan_items(r, marks, at_start, op0, op1):
                V.memset(carry[:, 0, 0:1], at_start)
                V.memset(carry[:, 1, NI:NI + 1], at_start)
                dve.wait_ge(rows_ps[0], r + 1)
                V.tensor_tensor_scan(carry[:, 0, 1:NI + 1], marks[:, 0, :], psR[0][0:HEADS, 0:NI], at_start, op0, op1
                                     ).then_inc(carried, 1)
                dve.wait_ge(rows_ps[1], r + 1)
                V.tensor_tensor_scan(carry[:, 1, 0:NI][:, ::-1], marks[:, 1, :][:, ::-1], psR[1][0:HEADS, 0:NI][:, ::-1],
                                     at_start, op0, op1).then_inc(carried, 1)
                dve.wait_ge(cin_ps, r + 1)
                c.then(V.tensor_copy(cin[:, :, :, :], psC[0:CI, 0:2 * CH * HEADS].rearrange("p (j c h) -> p j c h", j=2, c=CH)))

            for k in range(CH):
                dve.wait_ge(scores_ps, k + 1)
                c(V.tensor_tensor(T[:, k, :, :], psS[k][0:CI, :].rearrange("p (h e) -> p h e", h=HEADS), by_head(masked[:, k, :]), ALU.add))
            dve.wait_ge(dv, c.n)
            for k in range(CH):
                scan_chunk(k, pen, -BIG, ALU.add, ALU.max)
            dve.wait_ge(scanned[0], CH)
            dve.wait_ge(scanned[1], CH)
            c(V.scalar_tensor_tensor(out=tot[:, :, :, :], in0=fwd[:, :, :, :], scalar=-BIG, in1=bwd[:, :, :, :],
                                     op0=ALU.max, op1=ALU.max))
            scan_items(0, through_pen, -BIG, ALU.add, ALU.max)
            for j in range(2):
                for k in range(CH):
                    for h in range(HEADS):
                        c(V.scalar_tensor_tensor(out=tot[:, k, h, :], in0=ends_pen[:, j, k, :], scalar=cin[:, j, k, h:h + 1],
                                                 in1=tot[:, k, h, :], op0=ALU.add, op1=ALU.max))
                dve.wait_ge(dv, c.n)
            for k in range(CH):
                V.tensor_tensor(T[:, k, :, :], T[:, k, :, :], tot[:, k, :, :], ALU.subtract).then_inc(shifted, 1)
            for k in range(CH):
                dve.wait_ge(expd, k + 1)
                scan_chunk(k, go_on, 0.0, ALU.mult, ALU.add)
            dve.wait_ge(scanned[0], 2 * CH)
            dve.wait_ge(scanned[1], 2 * CH)
            c.then(V.scalar_tensor_tensor(out=tot[:, :, :, :], in0=fwd[:, :, :, :], scalar=SM_EPS, in1=bwd[:, :, :, :],
                                          op0=ALU.add, op1=ALU.add))
            c(V.tensor_tensor(tot[:, :, :, :], tot[:, :, :, :], T[:, :, :, :], ALU.subtract))
            scan_items(1, through, 0.0, ALU.mult, ALU.add)
            for j in range(2):
                for k in range(CH):
                    for h in range(HEADS):
                        c(V.scalar_tensor_tensor(out=tot[:, k, h, :], in0=ends[:, j, k, :], scalar=cin[:, j, k, h:h + 1],
                                                 in1=tot[:, k, h, :], op0=ALU.mult, op1=ALU.add))
                dve.wait_ge(dv, c.n)
            for k in range(CH):
                c(V.reciprocal(tot[:, k, :, :], tot[:, k, :, :]))
            for k in range(CH):
                dve.wait_ge(dv, c.n - CH + k + 1)
                V.tensor_tensor(T[:, k, :, :], T[:, k, :, :], tot[:, k, :, :], ALU.mult).then_inc(alpha, 1)


def aggregate_phase(nc, v):
    (gathered_d, iota32, A, REL, wrow, bg, xs, xn, h_in) = (v[k] for k in "gathered_d iota32 A REL wrow bg xs xn h_in".split())
    R2 = 3
    with ExitStack() as ctx:
        def sb(name, shape, dt=F32):
            return ctx.enter_context(nc.sbuf_tensor(name, shape, dt))

        def sem(name):
            return ctx.enter_context(nc.semaphore(name))

        R = [sb(f"R{b}", [P, U * D]) for b in range(R2)]
        msg = [sb(f"msg{b}", [P, U * D]) for b in range(R2)]
        M = [sb(f"M32_{b}", [P, U * P]) for b in range(R2)]
        zero = sb("zero", [P, 512])
        o = sb("o", [P, NW, D])
        eneg = sb("eneg", [P, NW, D])
        stats = sb("stats2", [P, 2, NW, 6])
        mv = sb("mv2", [P, 2, NW, 2])
        vare = sb("vare", [P, 2, NW])
        std = sb("std2", [P, 2, NW])
        rstd = sb("rstd2", [P, 2, NW])
        agg = ctx.enter_context(nc.psum_tensor("agg", [P, NW * D], F32))

        loaded = [sem(f"loaded{b}") for b in range(R2)]
        zset, zeroed = sem("zset"), sem("agg_zeroed")
        weighted = sem("weighted")
        added = sem("added")
        dv, negd, expd, vard, rooted = map(sem, ("dv_agg", "negd", "expd2", "vard", "rooted2"))
        block = ctx.enter_context(nc.Block())

        @block.sync
        def _(sp):
            with sp.Fori(0, STEPS // R2) as i:
                for b in range(R2):
                    s = i * R2 + b
                    sp.wait_ge(weighted, s + 1)
                    sp.dma_start(R[b][:, :], gathered_d[bass.ds(s, 1), :, :].rearrange("s p f -> (s p) f")
                                 ).then_inc(loaded[b], 16)

        @block.tensor
        def _(pe):
            pe.sem_inc(added, R2)
            regs = [pe.alloc_register(f"agg_window{u}") for u in range(U)]
            pe.wait_ge(zset, 1)
            for j in range(NW * D // 512):
                last = nc.tensor.matmul(agg[:, j * 512:(j + 1) * 512], zero[:, 0:P], zero[:, :], start=True, stop=False,
                                        skip_group_check=True)
            with pe.Fori(0, STEPS // R2) as i:
                for b in range(R2):
                    s = i * R2 + b
                    ws = load_windows(pe, regs, wrow, s)
                    pe.wait_ge(weighted, s + R2 + 1)
                    for u in range(U):
                        w = ws[u]
                        last = nc.tensor.matmul(agg[:, bass.ds(w * D, D)], M[b][:, u * P:(u + 1) * P],
                                                msg[b][:, u * D:(u + 1) * D], start=False, stop=False, skip_group_check=True)
                    last.then_inc(added, 1)

        @block.scalar
        def _(act):
            act.wait_ge(negd, 1)
            nc.scalar.activation(eneg[:, :, :], eneg[:, :, :], ACT.Exp).then_inc(expd, 1)
            for r in range(2):
                act.wait_ge(vard, r + 1)
                nc.scalar.activation(std[:, r, :], vare[:, r, :], ACT.Sqrt).then_inc(rooted, 1)

        @block.vector
        def _(dve):
            V = nc.vector
            dve.sem_inc(weighted, R2)
            V.memset(zero[:, :], 0.0).then_inc(zset, 1)
            with dve.Fori(0, STEPS // R2) as i:
                for b in range(R2):
                    s = i * R2 + b
                    dve.wait_ge(added, s + 1)
                    for u in range(U):
                        V.tensor_scalar(M[b][:, u * P:(u + 1) * P], iota32[:, :], REL[:, bass.ds(s * U + u, 1)], None,
                                        ALU.is_equal)
                    dve.wait_ge(loaded[b], i * 16 + 16)
                    V.tensor_tensor(msg[b][:, :].rearrange("p (u d) -> p u d", d=HD), R[b][:, :].rearrange("p (u d) -> p u d", d=HD),
                                    A[:, bass.ds(s * U, U), :].rearrange("p u h -> p (u h)").unsqueeze(2).broadcast_to([P, U * HEADS, HD]),
                                    ALU.mult).then_inc(weighted, 1)
            c = Chain(dve, dv)
            dve.wait_ge(added, STEPS + R2)

            def every(a):
                return a.unsqueeze(1).broadcast_to([P, NW, D])

            c.then(V.tensor_tensor(o[:, :, :], agg[:, :].rearrange("p (w f) -> p w f", w=NW), every(bg[:, 0, :]), ALU.add))
            V.tensor_scalar(eneg[:, :, :], o[:, :, :], 0.0, None, ALU.min).then_inc(negd, 1)
            dve.wait_ge(expd, 1)
            c.then(V.scalar_tensor_tensor(out=o[:, :, :], in0=o[:, :, :], scalar=0.0, in1=eneg[:, :, :], op0=ALU.max, op1=ALU.add))
            c.then(V.scalar_tensor_tensor(out=o[:, :, :], in0=o[:, :, :], scalar=-1.0, in1=xn[:, :, :], op0=ALU.add, op1=ALU.add))

            def layer_norm(r, to, of):
                for w in range(NW):
                    c(V.bn_stats(stats[:, r, w, :], of[:, w, :]))
                dve.wait_ge(dv, c.n)
                for w in range(NW):
                    c(V.bn_aggr(mv[:, r, w, :], stats[:, r, w, :]))
                dve.wait_ge(dv, c.n)
                V.tensor_scalar(vare[:, r, :], mv[:, r, :, 1], LN_EPS, None, ALU.add).then_inc(vard, 1)
                dve.wait_ge(rooted, r + 1)
                c.then(V.reciprocal(rstd[:, r, :], std[:, r, :]))
                for w in range(NW):
                    c(V.tensor_scalar(to[:, w, :], of[:, w, :], mv[:, r, w, 0:1], rstd[:, r, w:w + 1], ALU.subtract, ALU.mult))
                dve.wait_ge(dv, c.n)

            layer_norm(0, o, o)
            c.then(V.tensor_tensor(o[:, :, :], o[:, :, :], every(bg[:, 1, :]), ALU.mult))
            c.then(V.tensor_tensor(o[:, :, :], o[:, :, :], every(bg[:, 2, :]), ALU.add))
            c.then(V.tensor_tensor(xs[:, :, :], xs[:, :, :], o[:, :, :], ALU.add))
            layer_norm(1, h_in, xs)


def route_phase(nc, v):
    (ident, prow, iota32, Rw, Rb, b1, b2, b2_d, xs_d, h_in, gates, slot, nov, ovx, b1T) = (v[k] for k in (
        "ident prow iota32 Rw Rb b1 b2 b2_d xs_d h_in gates slot nov ovx b1T").split())
    with ExitStack() as ctx:
        def sb(name, shape, dt=F32):
            return ctx.enter_context(nc.sbuf_tensor(name, shape, dt))

        def sem(name):
            return ctx.enter_context(nc.semaphore(name))

        Rws = sb("Rws", [P, KC, NE])
        Rbb = sb("Rbb", [P, NE])
        hT = sb("hTr", [P, KC, NPAD])
        lg = sb("lg", [P, NW, NE])
        top = sb("top", [P, NW, 8])
        topi = sb("topi", [P, NW, 8], mybir.dt.uint32)
        topf = sb("topf", [P, NW, TOPK])
        pick = sb("pick", [P, TOPK, NW, NE])
        both = sb("both", [P, NW, NE], BF16)
        ones = sb("onesb", [P, P], BF16)
        tri = sb("tri", [P, P], BF16)
        live = sb("live", [P, 1])
        cnt = sb("cnt", [P, NE])
        more = sb("more", [P, NE])
        zrow = sb("zrow", [P, NE])
        upto = sb("upto", [P, NE + 1])
        first_at = sb("first_at", [P, NE])
        delta = sb("delta", [P, NE])
        rank = sb("rank", [P, NW, NE])
        fits = sb("fits", [P, NW, NE])
        slotf = sb("slotf", [P, NW, TOPK])
        diff = sb("diff", [P, NW])
        past = sb("past", [P, NE])
        ovc = sb("ovc", [P, 1])
        b2s = sb("b2s", [NE, D])
        b2r = sb("b2r", [NE, D])
        b2p = sb("b2p", [NE, 3, D], BF16)
        psT = ctx.enter_context(nc.psum_tensor("psTr", [P, 2, 512], F32))
        psL = ctx.enter_context(nc.psum_tensor("psL", [P, 2, 512], F32))
        psK = ctx.enter_context(nc.psum_tensor("psK", [P, 2, 512], F32))
        psN = ctx.enter_context(nc.psum_tensor("psN", [P, 512], F32))
        psO = ctx.enter_context(nc.psum_tensor("psO", [P, 512], F32))

        w_in, b2_in, b2_set, b2_out, dv, consts, hT_ps, hT_sb, lg_ps, picked, ranked, shifted, expd, slots, moved, ov_set, ov_ps = map(
            sem, ("rw_in", "b2_in", "b2_set", "b2_out", "dv_route", "consts_r", "hT_ps", "hT_sb", "lg_ps", "picked", "ranked",
                  "shifted_r", "expd_r", "slots", "moved", "ov_set", "ov_ps"))
        block = ctx.enter_context(nc.Block())

        @block.sync
        def _(sp):
            sp.dma_start(Rws[:, :, :], Rw.rearrange("(c p) n -> p c n", p=P)).then_inc(w_in, 16)
            sp.dma_start(Rbb[:, :], Rb.unsqueeze(0).broadcast_to([P, NE])).then_inc(w_in, 16)
            sp.dma_start(b2s[:, :], b2).then_inc(b2_in, 16)
            sp.dma_start(b1T[:, :, :], b1.rearrange("e (p m) -> p e m", m=HC)).then_inc(w_in, 16)
            sp.wait_ge(b2_set, 1)
            sp.dma_start(b2_d, b2p[:, :, :]).then_inc(b2_out, 16)
            sp.wait_ge(b2_out, 16)
            sp.wait_ge(w_in, 48)

        @block.scalar
        def _(act):
            for i in range(NW // 2):
                act.wait_ge(hT_ps, i + 1)
                nc.scalar.copy(hT[:, :, 2 * i * P:(2 * i + 2) * P].rearrange("p c (w q) -> p w c q", q=P),
                               psT[:, i % 2, :].rearrange("p (w c q) -> p w c q", w=2, c=KC)).then_inc(hT_sb, 1)
            act.wait_ge(shifted, 1)
            nc.scalar.activation(gates[:, :, 1], diff[:, :], ACT.Exp).then_inc(expd, 1)

        @block.gpsimd
        def _(g):
            nc.gpsimd.memset(ones[:, :], 1.0).then_inc(consts, 1)
            g.wait_ge(consts, 1)
            nc.gpsimd.affine_select(out=tri[:, :], in_=ones[:, :], compare_op=ALU.is_gt, fill=0.0, base=0,
                                    pattern=[[1, P]], channel_multiplier=-1).then_inc(consts, 1)
            g.wait_ge(slots, 1)
            for w in range(NW):
                n = P if w < NW - 1 else NREM
                for k in range(TOPK):
                    nc.gpsimd.indirect_dma_start(out=xs_d, out_offset=bass.IndirectOffsetOnAxis(ap=slot[0:n, k, w:w + 1], axis=0),
                                                 in_=h_in[0:n, w, :], in_offset=None).then_inc(moved, 16)
            g.wait_ge(moved, 16 * TOPK * NW)

        @block.tensor
        def _(pe):
            for i in range(NW // 2):
                if i >= 2:
                    pe.wait_ge(hT_sb, i - 1)
                for w in range(2):
                    for c in range(KC):
                        q = (w * KC + c) * P
                        last = nc.tensor.transpose(psT[:, i % 2, q:q + P], h_in[:, 2 * i + w, c * P:(c + 1) * P], ident[:, :])
                last.then_inc(hT_ps, 1)
            pe.wait_ge(hT_sb, NW // 2)
            pe.wait_ge(w_in, 48)
            for w in range(NW):
                for c in range(KC):
                    last = nc.tensor.matmul(psL[:, w // 8, (w % 8) * NE:(w % 8 + 1) * NE], hT[:, c, w * P:(w + 1) * P],
                                            Rws[:, c, :], start=(c == 0), stop=(c == KC - 1))
            last.then_inc(lg_ps, 1)
            pe.wait_ge(picked, 1)
            pe.wait_ge(consts, 2)
            for w in range(NW):
                to = psK[:, w // 8, (w % 8) * NE:(w % 8 + 1) * NE]
                for q in range(w):
                    nc.tensor.matmul(to, ones[:, :], both[:, q, :], start=(q == 0), stop=False)
                nc.tensor.matmul(to, tri[:, :], both[:, w, :], start=(w == 0), stop=True)
            for w in range(NW):
                last = nc.tensor.matmul(psN[:, 0:NE], ones[:, :], both[:, w, :], start=(w == 0), stop=(w == NW - 1))
            last.then_inc(ranked, 1)
            pe.wait_ge(ov_set, 1)
            nc.tensor.transpose(psO[0:1, 0:P], ovc[:, :], ident[:, :]).then_inc(ov_ps, 1)

        @block.vector
        def _(dve):
            V = nc.vector
            c = Chain(dve, dv)
            c(V.memset(zrow[:, :], 0.0))
            c(V.tensor_scalar(live[:, :], prow[:, :], float(NREM), None, ALU.is_lt))
            dve.wait_ge(b2_in, 16)
            c.then(V.tensor_copy(b2p[:, 0, :], b2s[:, :]))
            c.then(V.tensor_tensor(b2r[:, :], b2s[:, :], b2p[:, 0, :], ALU.subtract))
            c.then(V.tensor_copy(b2p[:, 1, :], b2r[:, :]))
            V.tensor_tensor(b2p[:, 2, :], b2r[:, :], b2p[:, 1, :], ALU.subtract).then_inc(b2_set, 1)
            dve.wait_ge(lg_ps, 1)
            for j, (lo, hi) in enumerate(((0, 8), (8, NW))):
                c(V.tensor_tensor(lg[:, lo:hi, :], psL[:, j, 0:(hi - lo) * NE].rearrange("p (w e) -> p w e", e=NE),
                                  Rbb[:, :].unsqueeze(1).broadcast_to([P, hi - lo, NE]), ALU.add))
            dve.wait_ge(dv, c.n)
            for w in range(NW):
                c(V.max(top[:, w, :], lg[:, w, :]))
            dve.wait_ge(dv, c.n)
            for w in range(NW):
                c(V.max_index(topi[:, w, :], top[:, w, :], lg[:, w, :]))
            V.tensor_tensor(diff[:, :], top[:, :, 1], top[:, :, 0], ALU.subtract).then_inc(shifted, 1)
            dve.wait_ge(dv, c.n)
            c.then(V.tensor_copy(topf[:, :, :], topi[:, :, 0:TOPK]))
            for k in range(TOPK):
                c(V.tensor_tensor(pick[:, k, :, :], iota32[:, 0:NE].unsqueeze(1).broadcast_to([P, NW, NE]),
                                  topf[:, :, k].unsqueeze(2).broadcast_to([P, NW, NE]), ALU.is_equal))
            dve.wait_ge(dv, c.n)
            c.then(V.tensor_tensor(both[:, :, :], pick[:, 0, :, :], pick[:, 1, :, :], ALU.add))
            V.tensor_scalar(both[:, NW - 1, :], both[:, NW - 1, :], live[:, 0:1], None, ALU.mult).then_inc(picked, 1)
            dve.wait_ge(expd, 1)
            c.then(V.tensor_scalar(gates[:, :, 0], gates[:, :, 1], 1.0, None, ALU.add))
            c.then(V.reciprocal(gates[:, :, 0], gates[:, :, 0]))
            c(V.tensor_tensor(gates[:, :, 1], gates[:, :, 1], gates[:, :, 0], ALU.mult))
            dve.wait_ge(ranked, 1)
            c(V.tensor_copy(cnt[:, :], psN[:, 0:NE]))
            c(V.tensor_copy(rank[:, 0:8, :], psK[:, 0, :].rearrange("p (w e) -> p w e", e=NE)))
            c.then(V.tensor_copy(rank[:, 8:NW, :], psK[:, 1, 0:(NW - 8) * NE].rearrange("p (w e) -> p w e", e=NE)))
            c.then(V.tensor_scalar(more[:, :], cnt[:, :], float(CAP), None, ALU.is_gt))
            for j in range(2, -(-N // CAP)):
                c.then(V.scalar_tensor_tensor(out=more[:, :], in0=cnt[:, :], scalar=float(j * CAP), in1=more[:, :],
                                              op0=ALU.is_gt, op1=ALU.add))
            c(V.memset(upto[:, 0:1], 0.0))
            c.then(V.tensor_tensor_scan(upto[:, 1:NE + 1], more[:, :], zrow[:, :], 0.0, ALU.add, ALU.add))
            c.then(V.tensor_scalar(first_at[:, :], upto[:, 0:NE], float(NE - 1), float(CAP), ALU.add, ALU.mult))
            c.then(V.scalar_tensor_tensor(out=delta[:, :], in0=iota32[:, 0:NE], scalar=float(CAP), in1=first_at[:, :],
                                          op0=ALU.mult, op1=ALU.subtract))

            def every(a):
                return a.unsqueeze(1).broadcast_to([P, NW, NE])

            c.then(V.tensor_scalar(fits[:, :, :], rank[:, :, :], float(CAP), None, ALU.is_lt))
            c.then(V.tensor_tensor(fits[:, :, :], fits[:, :, :], every(delta[:, :]), ALU.mult))
            c.then(V.tensor_tensor(rank[:, :, :], rank[:, :, :], every(first_at[:, :]), ALU.add))
            c.then(V.tensor_tensor(rank[:, :, :], rank[:, :, :], fits[:, :, :], ALU.add))
            for k in range(TOPK):
                c(V.tensor_tensor(pick[:, k, :, :], pick[:, k, :, :], rank[:, :, :], ALU.mult))
            dve.wait_ge(dv, c.n)
            for k in range(TOPK):
                c(V.tensor_reduce(slotf[:, :, k], pick[:, k, :, :], AX_X, ALU.add))
            dve.wait_ge(dv, c.n)
            V.tensor_copy(slot[:, :, :], slotf[:, :, :].rearrange("p w k -> p k w")).then_inc(slots, 1)
            c(V.tensor_copy(nov[:, :], upto[0:1, NE:NE + 1]))
            c.then(V.tensor_scalar(past[:, :], upto[:, 1:NE + 1], prow[:, 0:1], None, ALU.is_le))
            V.tensor_reduce(ovc[:, :], past[:, :], AX_X, ALU.add).then_inc(ov_set, 1)
            dve.wait_ge(ov_ps, 1)
            c(V.tensor_scalar(ovx[:, :], psO[0:1, 0:OVB], float(NE - 1), None, ALU.min))
            dve.wait_ge(dv, c.n)


def expert_phase(nc, v):
    (ident, W1, W2, b2_d, xs_d, ys_d, b1T) = (v[k] for k in "ident W1 W2 b2_d xs_d ys_d b1T".split())
    w1, w2, w_in = (v[k] for k in "w1 w2 w_in".split())
    with ExitStack() as ctx:
        def sb(name, shape, dt=F32):
            return ctx.enter_context(nc.sbuf_tensor(name, shape, dt))

        def sem(name):
            return ctx.enter_context(nc.semaphore(name))

        b2e = [sb(f"b2e_{r}", [3, D], BF16) for r in range(RING)]
        X = [sb(f"X{r}", [CAP, D]) for r in range(RING)]
        xT = sb("xT", [P, 2, KC * CAP])
        hid = sb("hid", [P, 2, HC * CAP])
        Y = [sb(f"Y{r}", [CAP, D]) for r in range(RING)]
        ones3 = sb("ones3", [3, CAP], BF16)
        psX = ctx.enter_context(nc.psum_tensor("psXe", [P, 2, 512], F32))
        psH = ctx.enter_context(nc.psum_tensor("psH", [P, 2, 512], F32))
        psY = ctx.enter_context(nc.psum_tensor("psY", [P, 2, 512], F32))

        x_in = [sem(f"xe_in{r}") for r in range(RING)]
        y_out = [sem(f"y_out{r}") for r in range(RING)]
        ones_set, biased = sem("ones_set"), sem("biased")
        turned = sem("turned_e")
        xT_set = sem("xT_set")
        hid_ps = sem("hid_ps")
        hid_set = sem("hid_set")
        y_ps = sem("y_ps")
        y_set = sem("y_set")
        block = ctx.enter_context(nc.Block())

        def load_tokens(sp, r, e):
            sp.dma_start(b2e[r][:, :], b2_d[bass.ds(e, 1), :, :].rearrange("e j n -> (e j) n")).then_inc(x_in[r], 16)
            sp.dma_start(X[r][:, :], xs_d[bass.ds(e * CAP, CAP), :]).then_inc(x_in[r], 16)

        @block.sync
        def _(sp):
            for r in range(RING):
                load_tokens(sp, r, r)
            with sp.Fori(1, NE // RING) as i:
                for r in range(RING):
                    sp.wait_ge(y_ps, i * RING + r + 1)
                    load_tokens(sp, r, i * RING + r)
                    load_weights(sp, W1, W2, w1, w2, w_in, r, i * RING + r)

        @block.gpsimd
        def _(g):
            for r in range(RING):
                g.wait_ge(y_out[r], 16 * (NE // RING) + 16)

        LASTG = NE // RING - 1

        def groups(eng, step):
            with eng.Fori(0, LASTG) as i:
                for r in range(RING):
                    step(i, r, RING)
            for r in range(RING):
                step(LASTG, r, RING - 1 - r)

        @block.tensor
        def _(pe):
            pe.sem_inc(y_ps, RING)
            pe.wait_ge(ones_set, 1)

            def turn(grp, r):
                e, b = grp * RING + r, r % 2
                r, grp = r % RING, grp + r // RING
                pe.wait_ge(x_in[r], grp * 32 + 32)
                pe.wait_ge(xT_set, e + 1)
                for c in range(KC):
                    last = nc.tensor.transpose(psX[:, b, c * CAP:(c + 1) * CAP], X[r][:, c::KC], ident[0:CAP, 0:CAP])
                last.then_inc(turned, 1)

            def first(grp, r):
                e, b = grp * RING + r, r % 2
                r, grp = r % RING, grp + r // RING
                pe.wait_ge(w_in[r], grp * 32 + 32)
                pe.wait_ge(xT_set, e + 3)
                pe.wait_ge(hid_set, e + 1)
                for m in range(HC):
                    for c in range(KC):
                        last = nc.tensor.matmul(psH[:, b, m * CAP:(m + 1) * CAP], w1[r][:, c, m::HC],
                                                xT[:, b, c * CAP:(c + 1) * CAP], start=(c == 0), stop=(c == KC - 1))
                last.then_inc(hid_ps, 1)

            def step(grp, r, left):
                e, b = grp * RING + r, r % 2
                if left >= 2:
                    turn(grp, r + 2)
                if left >= 1:
                    first(grp, r + 1)
                pe.wait_ge(hid_set, e + 3)
                pe.wait_ge(y_set, e + 1)
                for m in range(HC):
                    nc.tensor.matmul(psY[0:CAP, b, 0:D], hid[:, b, m * CAP:(m + 1) * CAP], w2[r][:, m, :],
                                     start=(m == 0), stop=False)
                nc.tensor.matmul(psY[0:CAP, b, 0:D], ones3[:, :], b2e[r][:, :], start=False, stop=True).then_inc(y_ps, 1)

            turn(0, 0)
            turn(0, 1)
            first(0, 0)
            groups(pe, step)

        @block.vector
        def _(dve):
            nc.vector.memset(ones3[:, :], 1.0).then_inc(ones_set, 1)
            dve.sem_inc(hid_set, 2)

            def hidden(grp, r):
                e, b = grp * RING + r, r % 2
                dve.wait_ge(hid_ps, e + 1)
                dve.wait_ge(y_ps, e + RING - 1)
                nc.vector.tensor_tensor(hid[:, b, :].rearrange("p (m t) -> p m t", m=HC),
                                        psH[:, b, 0:HC * CAP].rearrange("p (m t) -> p m t", m=HC),
                                        b1T[:, bass.ds(e, 1), :].rearrange("p e m -> p (e m)").unsqueeze(2).broadcast_to([P, HC, CAP]),
                                        ALU.add).then_inc(biased, 1)
                dve.wait_ge(biased, e + 1)
                nc.vector.tensor_scalar(hid[:, b, :], hid[:, b, :], 0.0, None, ALU.max).then_inc(hid_set, 1)

            def step(grp, r, left):
                if left >= 1:
                    hidden(grp, r + 1)

            hidden(0, 0)
            groups(dve, step)

        @block.scalar
        def _(act):
            act.sem_inc(xT_set, 2)
            act.sem_inc(y_set, 2)
            for r in range(RING):
                act.sem_inc(y_out[r], 16)

            def copy_x(grp, r):
                e, b = grp * RING + r, r % 2
                act.wait_ge(turned, e + 1)
                nc.scalar.copy(xT[:, b, :], psX[:, b, 0:KC * CAP]).then_inc(xT_set, 1)

            def step(grp, r, left):
                e, b = grp * RING + r, r % 2
                if left >= 2:
                    act.wait_ge(hid_ps, e + 1)
                    copy_x(grp, r + 2)
                act.wait_ge(y_ps, e + RING + 1)
                act.wait_ge(y_out[r], grp * 16 + 16)
                nc.scalar.copy(Y[r][:, :], psY[0:CAP, b, 0:D]).then_inc(y_set, 1)
                act.wait_ge(y_set, e + 3)
                act.dma_start(ys_d[bass.ds(e * CAP, CAP), :], Y[r][:, :]).then_inc(y_out[r], 16)

            copy_x(0, 0)
            copy_x(0, 1)
            groups(act, step)


def overflow_phase(nc, v):
    (ident, W1, W2, b2_d, xs_d, ys_d, b1T, nov, ovx) = (v[k] for k in "ident W1 W2 b2_d xs_d ys_d b1T nov ovx".split())
    with ExitStack() as ctx:
        def sb(name, shape, dt=F32):
            return ctx.enter_context(nc.sbuf_tensor(name, shape, dt))

        def sem(name):
            return ctx.enter_context(nc.semaphore(name))

        w1 = sb("ow1", [P, KC, HID])
        w2 = sb("ow2", [P, HC, D])
        b2e = sb("ob2e", [3, D], BF16)
        X = sb("oX", [CAP, D])
        xT = sb("oxT", [P, KC * CAP])
        hid = sb("ohid", [P, HC * CAP])
        Y = sb("oY", [CAP, D])
        ones3 = sb("oones3", [3, CAP], BF16)
        psX = ctx.enter_context(nc.psum_tensor("opsX", [P, 512], F32))
        psH = ctx.enter_context(nc.psum_tensor("opsH", [P, 512], F32))
        psY = ctx.enter_context(nc.psum_tensor("opsY", [P, 512], F32))
        came, went, turned, xT_set, hid_ps, biased, hid_set, y_ps, y_set = map(sem, (
            "came", "went", "oturned", "oxT_set", "ohid_ps", "obiased", "ohid_set", "oy_ps", "oy_set"))
        block = ctx.enter_context(nc.Block())

        @block.sync
        def _(sp):
            n = sp.value_load(nov[0:1, 0:1], min_val=0, max_val=OVB)
            with sp.If(n > 0):
                sp.sem_inc(went, 16)
                with sp.Fori(0, OVB) as k:
                    sp.wait_ge(went, k * 16 + 16)
                    e = sp.value_load(ovx[0:1, bass.ds(k, 1)], min_val=0, max_val=NE - 1)
                    sp.dma_start(w1[:, :, :], W1[bass.ds(e, 1), :, :].rearrange("e (p c) n -> (e p) c n", c=KC)).then_inc(came, 16)
                    sp.dma_start(w2[:, :, :], W2[bass.ds(e, 1), :, :].rearrange("e (p m) n -> (e p) m n", m=HC)).then_inc(came, 16)
                    sp.dma_start(b2e[:, :], b2_d[bass.ds(e, 1), :, :].rearrange("e j n -> (e j) n")).then_inc(came, 16)
                    sp.dma_start(X[:, :], xs_d[bass.ds((k + NE) * CAP, CAP), :]).then_inc(came, 16)
                    sp.wait_ge(y_set, k + 1)
                    sp.dma_start(ys_d[bass.ds((k + NE) * CAP, CAP), :], Y[:, :]).then_inc(went, 16)
                sp.wait_ge(went, OVB * 16 + 16)

        @block.tensor
        def _(pe):
            n = pe.value_load(nov[0:1, 0:1], min_val=0, max_val=OVB)
            with pe.If(n > 0):
                with pe.Fori(0, OVB) as k:
                    pe.wait_ge(came, k * 64 + 64)
                    for c in range(KC):
                        last = nc.tensor.transpose(psX[:, c * CAP:(c + 1) * CAP], X[:, c::KC], ident[0:CAP, 0:CAP])
                    last.then_inc(turned, 1)
                    pe.wait_ge(xT_set, k + 1)
                    for m in range(HC):
                        for c in range(KC):
                            last = nc.tensor.matmul(psH[:, m * CAP:(m + 1) * CAP], w1[:, c, m::HC],
                                                    xT[:, c * CAP:(c + 1) * CAP], start=(c == 0), stop=(c == KC - 1))
                    last.then_inc(hid_ps, 1)
                    pe.wait_ge(hid_set, k + 1)
                    for m in range(HC):
                        nc.tensor.matmul(psY[0:CAP, 0:D], hid[:, m * CAP:(m + 1) * CAP], w2[:, m, :], start=(m == 0), stop=False)
                    nc.tensor.matmul(psY[0:CAP, 0:D], ones3[:, :], b2e[:, :], start=False, stop=True).then_inc(y_ps, 1)

        @block.vector
        def _(dve):
            n = dve.value_load(nov[0:1, 0:1], min_val=0, max_val=OVB)
            with dve.If(n > 0):
                nc.vector.memset(ones3[:, :], 1.0)
                with dve.Fori(0, OVB) as k:
                    e = dve.value_load(ovx[0:1, bass.ds(k, 1)], min_val=0, max_val=NE - 1)
                    dve.wait_ge(turned, k + 1)
                    nc.vector.tensor_copy(xT[:, :], psX[:, 0:KC * CAP]).then_inc(xT_set, 1)
                    dve.wait_ge(hid_ps, k + 1)
                    nc.vector.tensor_tensor(hid[:, :].rearrange("p (m t) -> p m t", m=HC),
                                            psH[:, 0:HC * CAP].rearrange("p (m t) -> p m t", m=HC),
                                            b1T[:, bass.ds(e, 1), :].rearrange("p e m -> p (e m)").unsqueeze(2).broadcast_to([P, HC, CAP]),
                                            ALU.add).then_inc(biased, 1)
                    dve.wait_ge(biased, k + 1)
                    nc.vector.tensor_scalar(hid[:, :], hid[:, :], 0.0, None, ALU.max).then_inc(hid_set, 1)
                    dve.wait_ge(y_ps, k + 1)
                    nc.vector.tensor_copy(Y[:, :], psY[0:CAP, 0:D]).then_inc(y_set, 1)


def combine_phase(nc, v):
    out, xs, ys_d, slot, gates = (v[k] for k in "out xs ys_d slot gates".split())
    with ExitStack() as ctx:
        def sem(name):
            return ctx.enter_context(nc.semaphore(name))

        yg = ctx.enter_context(nc.sbuf_tensor("yg", [P, NW, TOPK, D], F32))
        fetched = [sem(f"fetched{w}") for w in range(NW)]
        half, full, outs = sem("half"), sem("full"), sem("outs")
        block = ctx.enter_context(nc.Block())

        @block.gpsimd
        def _(g):
            for w in range(NW):
                n = P if w < NW - 1 else NREM
                for k in range(TOPK):
                    nc.gpsimd.indirect_dma_start(out=yg[0:n, w, k, :], out_offset=None, in_=ys_d,
                                                 in_offset=bass.IndirectOffsetOnAxis(ap=slot[0:n, k, w:w + 1], axis=0)
                                                 ).then_inc(fetched[w], 16)

        @block.vector
        def _(dve):
            for w in range(NW):
                n = P if w < NW - 1 else NREM
                dve.wait_ge(fetched[w], 32)
                nc.vector.scalar_tensor_tensor(out=xs[0:n, w, :], in0=yg[0:n, w, 0, :], scalar=gates[0:n, w, 0:1],
                                               in1=xs[0:n, w, :], op0=ALU.mult, op1=ALU.add).then_inc(half, 1)
                dve.wait_ge(half, w + 1)
                nc.vector.scalar_tensor_tensor(out=xs[0:n, w, :], in0=yg[0:n, w, 1, :], scalar=gates[0:n, w, 1:2],
                                               in1=xs[0:n, w, :], op0=ALU.mult, op1=ALU.add).then_inc(full, 1)

        @block.sync
        def _(sp):
            for w in range(NW):
                n = P if w < NW - 1 else NREM
                sp.wait_ge(full, w + 1)
                sp.dma_start(out[w * P:w * P + n, :], xs[0:n, w, :]).then_inc(outs, 16)
            sp.wait_ge(outs, 16 * NW)


_INS = ["x", "src", "dst", "L0_gnn_W_l", "L0_gnn_W_r", "L0_gnn_att", "L0_gnn_bias", "L0_gnn_gamma", "L0_gnn_beta",
        "L0_ffn_Wr", "L0_ffn_br", "L0_ffn_W1", "L0_ffn_b1", "L0_ffn_W2", "L0_ffn_b2"]


def kernel(**inputs):
    import concourse.bacc as bacc
    from concourse.bass_utils import run_bass_kernel_spmd

    nc = bacc.Bacc("TRN2", target_bir_lowering=False, num_devices=1)
    arrays, args = {}, []
    for name in _INS:
        a = np.ascontiguousarray(inputs[name])
        arrays[f"in_{name}"] = a
        args.append(nc.dram_tensor(f"in_{name}", a.shape, mybir.dt.from_np(a.dtype), kind="ExternalInput").ap())
    args.append(nc.dram_tensor("out_x", (N, D), F32, kind="ExternalOutput").ap())
    gnn_moe(nc, *args)
    r = run_bass_kernel_spmd(nc, [arrays], core_ids=[0])
    return r.results[0]["out_x"]
```

```python
from contextlib import ExitStack

import numpy as np

import concourse.bass as bass
from concourse import mybir

ALU = mybir.AluOpType
ACT = mybir.ActivationFunctionType
AX_X = mybir.AxisListType.X
F32 = mybir.dt.float32
BF16 = mybir.dt.bfloat16
I32 = mybir.dt.int32

P = 128
N, D = 1250, 256
DX = D + 4
E = 40000
HEADS, HD = 4, 64
NW = -(-N // P)
NREM = N - (NW - 1) * P
NPAD = NW * P
TILES = -(-E // P)
U = 6
CH = 3
NI = -(-(TILES + NW - 1) // (2 * U * CH)) * 2 * U * CH
CI = NI // CH
STEPS = NI // U
ROWS = TILES + 1
EPAD = ROWS * P - E
BIG = 1e30
WPAD = 8
SLOPE = 0.2
LN_EPS = 1e-5
SM_EPS = 1e-16
NE, HID, TOPK = 64, 512, 2
KC, HC = D // P, HID // P
CAP = 96
RING = 16
GR, AHEAD = 3, 1
EARLY = 7
XR, YR = RING // 2, RING // 4
AR = 3
OVB = (N * TOPK) // CAP
SLOTS = (NE + OVB) * CAP


class Chain:

    def __init__(self, eng, sem):
        self.eng, self.sem, self.n = eng, sem, 0

    def __call__(self, ins):
        ins.then_inc(self.sem, 1)
        self.n += 1
        return self.n

    def then(self, ins):
        self(ins)
        self.eng.wait_ge(self.sem, self.n)


def col(ap, *sizes):
    shape = list(ap.shape)
    for s in sizes:
        ap = ap.unsqueeze(len(shape))
        shape.append(s)
    return ap.broadcast_to(shape)


def load_weights(eng, W1, W2, w1, w2, w_in, q, e):
    eng.dma_start(w1[q][:, :, :], W1[bass.ds(e, 1), :, :].rearrange("e (p c) n -> (e p) c n", c=KC)).then_inc(w_in[q], 16)
    eng.dma_start(w2[q][:, :, :], W2[bass.ds(e, 1), :, :].rearrange("e (p m) n -> (e p) m n", m=HC)).then_inc(w_in[q], 16)


def gather_step(nc, G, xl_tab, idx, gathered):
    for u in range(U):
        nc.gpsimd.indirect_dma_start(out=G[:, u, :], out_offset=None, in_=xl_tab,
                                     in_offset=bass.IndirectOffsetOnAxis(ap=idx[:, u:u + 1], axis=0)).then_inc(gathered, 16)


def load_sources(eng, gathered_d, R, loaded, b, s):
    eng.dma_start(R[b][:, :], gathered_d[bass.ds(s, 1), :, :].rearrange("s p f -> (s p) f")).then_inc(loaded[b], 16)


def load_windows(pe, regs, wrow, s):
    pe.load(regs, wrow[0:1, bass.ds(s, 1), 0:U].rearrange("o s u -> o (s u)"))
    return [pe.snap(x, min_val=0, max_val=NW - 1) for x in regs]


def gnn_moe(nc, x, src, dst, Wl, Wr, att, bias, gamma, beta, Rw, Rb, W1, b1, W2, b2, out):
    with ExitStack() as ctx:
        def sb(name, shape, dt=F32):
            return ctx.enter_context(nc.sbuf_tensor(name, shape, dt))

        def dram(name, shape, dt=F32):
            return nc.dram_tensor(name, shape, dt, kind="Internal").ap()

        def sem(name):
            return ctx.enter_context(nc.semaphore(name))

        srcp = dram("srcp", [ROWS, P], I32)
        dstp = dram("dstp", [ROWS, P], I32)
        xl_tab = dram("xl_tab", [NPAD, DX])
        gathered_d = dram("gathered_d", [STEPS, P, U * D])
        rel_d = dram("rel_d", [NI + 2 * U, P], BF16)
        xs_d = dram("xs_d", [SLOTS, D])
        ys_d = dram("ys_d", [SLOTS, D])

        ident = sb("ident", [P, P])
        prow = sb("prow", [P, 1])
        iota32 = sb("iota32", [P, P])
        xs = sb("xs", [P, NW, D])
        xn = sb("xn", [P, NW, D])
        bg = sb("bg", [P, 3, D])

        w_in = [sem(f"w_in{q}") for q in range(RING)]
        fetched = [sem(f"fetched{w}") for w in range(NW // 2)]
        w1, w2 = [], []
        loaded = [sem(f"loaded{b}") for b in range(AR)]
        edges = ctx.enter_context(ExitStack())

        def esb(name, shape, dt=F32):
            return edges.enter_context(nc.sbuf_tensor(name, shape, dt, side="right"))

        REL = esb("REL", [P, NI])
        wrow = esb("wrow", [1, STEPS, WPAD], I32)
        A = esb("A", [P, NI, HEADS])
        R = [esb(f"R{b}", [P, U * D]) for b in range(AR)]
        with ExitStack() as graph:
            def gsb(name, shape, dt=F32):
                return graph.enter_context(nc.sbuf_tensor(name, shape, dt))

            iotai = gsb("iotai", [P, NI], I32)
            xr3 = gsb("xr3", [P, NW * 3 * DX], BF16)
            attb = gsb("attb", [P, D])
            S = gsb("S", [P, NI + U, HEADS])
            srcI = gsb("srcI", [P, NI + 3 * U], I32)
            valid = gsb("valid", [CI, CH, P])
            gd = gsb("gd", [CI, CH, P])
            pen = gsb("pen", [CI, CH * HEADS * P + 1])
            go_on = gsb("go_on", [CI, CH * HEADS * P + 1])
            masked = gsb("masked", [CI, CH, P])
            ends = gsb("ends", [CI, 2, CH, P])
            ends_pen = gsb("ends_pen", [CI, 2, CH, P])
            through = gsb("through", [HEADS, 2, NI])
            through_pen = gsb("through_pen", [HEADS, 2, NI])
            G = [gsb(f"G{g}", [P, U, DX]) for g in range(GR)]
            gathered = [sem(f"gathered{g}") for g in range(GR)]
            node_phase(nc, locals())
            score_phase(nc, locals())
            softmax_phase(nc, locals())
        for q in range(RING):
            w1.append(ctx.enter_context(nc.sbuf_tensor(f"w1_{q}", [P, KC, HID], F32)))
            w2.append(ctx.enter_context(nc.sbuf_tensor(f"w2_{q}", [P, HC, D], F32)))
        with nc.psum_tensor("agg", [P, NW * D], F32) as agg:
            aggregate_phase(nc, locals())
            edges.close()
            h_in = sb("h_in", [P, NW, D])
            gates = sb("gates", [P, NW, TOPK])
            slot = sb("slot", [P, TOPK, NW], I32)
            nov = sb("nov", [1, 1], I32)
            ovx = sb("ovx", [1, OVB], I32)
            b1T = sb("b1T", [P, NE, HC])
            route_phase(nc, locals())
        expert_phase(nc, locals())
        overflow_phase(nc, locals())
        combine_phase(nc, locals())


def node_phase(nc, v):
    (x, src, dst, Wl, Wr, att, bias, gamma, beta, srcp, dstp, xl_tab, rel_d, ident, prow, iota32, iotai,
     xs, xn, xr3, attb, bg, S, REL, srcI, wrow, valid, gd) = (v[k] for k in (
         "x src dst Wl Wr att bias gamma beta srcp dstp xl_tab rel_d ident prow iota32 iotai "
         "xs xn xr3 attb bg S REL srcI wrow valid gd").split())
    pen, go_on, masked, ends, ends_pen, through, through_pen, G, gathered = (
        v[k] for k in "pen go_on masked ends ends_pen through through_pen G gathered".split())
    with ExitStack() as ctx:
        def sb(name, shape, dt=F32):
            return ctx.enter_context(nc.sbuf_tensor(name, shape, dt))

        def sem(name):
            return ctx.enter_context(nc.semaphore(name))

        Wlr = sb("Wlr", [P, KC, 2 * D])
        pad = sb("pad", [1, 2, EPAD], I32)
        lastd = sb("lastd", [P, CH], I32)
        lastf = sb("lastf", [P, CH])
        iotak = sb("iotak", [P, NI])
        before = sb("before", [P, CH, NI])
        ones = sb("ones", [P, 1])
        trow = sb("trow", [1, NI])
        wrf = sb("wrf", [1, NI])
        kcol_i = sb("kcol_i", [CI, CH], I32)
        pcol_i = sb("pcol_i", [P, CH], I32)
        kcol = sb("kcol", [CI, CH])
        pcol = sb("pcol", [P, CH])
        tcol = sb("tcol", [CI, CH])
        wcol = sb("wcol", [CI, CH])
        tcol_i = sb("tcol_i", [CI, CH], I32)
        stats = sb("stats", [P, NW, 6])
        mv = sb("mv", [P, NW, 2])
        std = sb("std", [P, NW])
        rstd = sb("rstd", [P, NW])
        xnT = sb("xnT", [P, KC, NPAD])
        xlr = sb("xlr", [P, NW, 2, DX])
        Watt = sb("Watt", [P, KC, 2 * HEADS])
        watp = sb("watp", [P, KC, 2 * D])
        rem = sb("rem", [P, NW, DX])
        cut = sb("cut", [CI, CH, P])
        pen1 = sb("pen1", [CI, CH, P])
        go_on1 = sb("go_on1", [CI, CH, P])
        link = sb("link", [HEADS, NI + 1])
        solid = sb("solid", [HEADS, NI])
        ends_gd = sb("ends_gd", [HEADS, 2, NI])
        linkc = sb("linkc", [CI, 2, CH])
        srcT = sb("srcT", [CI, CH, P], I32)
        dstT = sb("dstT", [CI, CH, P], I32)
        srcF = sb("srcF", [CI, CH, P])
        dstF = sb("dstF", [CI, CH, P])
        clampd = sb("clampd", [CI, CH, P])
        relm = sb("relm", [CI, CH, P])
        rel16 = sb("rel16", [CI, CH, P], BF16)
        psT = ctx.enter_context(nc.psum_tensor("psT", [P, 2, 512], F32))
        psX = ctx.enter_context(nc.psum_tensor("psX", [P, 2, 512], F32))
        psI = ctx.enter_context(nc.psum_tensor("psI", [P, 512], F32))
        psJ = ctx.enter_context(nc.psum_tensor("psJ", [P, 512], F32))
        psE = ctx.enter_context(nc.psum_tensor("psE", [P, 2, 512], F32))

        x_in, w_in, c_in, pad_set, tables, last_in, items_in, xl_out = map(sem, (
            "x_in", "w_in", "c_in", "pad_set", "tables", "last_in", "items_in", "xl_out"))
        consts, dv, rooted, normed, xT_ps, xT_sb, proj, xlr_sb, before_set, t_ps, t_set, rel_set, rel_ps = map(
            sem, ("consts", "dv_node", "rooted", "normed", "xT_ps", "xT_sb", "proj", "xlr_sb",
                  "before_set", "t_ps", "t_set", "rel_set", "rel_ps"))
        xr_hi = sem("xr_hi")
        gd_set, srcI_set, ends_ps, linked, link_ps, cut_set, by_head, lin_sb = map(
            sem, ("gd_set", "srcI_set", "ends_ps", "linked", "link_ps", "cut_set", "by_head", "lin_sb"))
        iotas, zeroed = sem("iotas"), sem("zeroed")
        rel16_set, rel_out = sem("rel16_set"), sem("rel_out")
        var_set, proj_lin, watt_set = sem("var_set"), sem("proj_lin"), sem("watt_set")
        block = ctx.enter_context(nc.Block())

        def xr3_part(i, j):
            return xr3[:, 6 * i * DX:6 * (i + 1) * DX].rearrange("p (w j f) -> p w j f", w=2, j=3)[:, :, j, :]

        @block.sync
        def _(sp):
            sp.wait_ge(zeroed, 1)
            sp.dma_start(xs[:, 0:NW - 1, :], x[0:(NW - 1) * P, :].rearrange("(w p) f -> p w f", p=P)).then_inc(x_in, 16)
            sp.dma_start(xs[0:NREM, NW - 1, :], x[(NW - 1) * P:N, :]).then_inc(x_in, 16)
            sp.dma_start(Wlr[:, :, 0:D], Wl.rearrange("(c p) n -> p c n", p=P)).then_inc(w_in, 16)
            sp.dma_start(Wlr[:, :, D:2 * D], Wr.rearrange("(c p) n -> p c n", p=P)).then_inc(w_in, 16)
            sp.wait_ge(rel16_set, 1)
            sp.dma_start(rel_d[0:NI, :].rearrange("(c k) e -> k c e", c=CH), rel16[:, :, :]).then_inc(rel_out, 16)
            sp.dma_start(rel_d[NI:NI + 2 * U, :], rel16[0:2 * U, 0, :]).then_inc(rel_out, 16)
            sp.wait_ge(lin_sb, 1)
            sp.wait_ge(xlr_sb, NW // 2)
            sp.dma_start(xl_tab.rearrange("(w p) f -> p w f", p=P), xlr[:, :, 0, :]).then_inc(xl_out, 16)
            sp.wait_ge(rel_out, 32)

        @block.scalar
        def _(act):
            for i, (tab, a) in enumerate(((srcp, src), (dstp, dst))):
                flat = tab.rearrange("t e -> (t e)")
                act.dma_start(flat[0:E].rearrange("(a b) -> a b", a=16), a.rearrange("(a b) -> a b", a=16)).then_inc(tables, 16)
                act.wait_ge(pad_set, 2)
                act.dma_start(flat[E:E + EPAD].rearrange("(a b) -> a b", a=1), pad[0:1, i, :]).then_inc(tables, 16)
            act.wait_ge(tables, 64)
            act.wait_ge(zeroed, 2)
            for c in range(CH):
                n = min(P, TILES - c * P)
                act.dma_start(lastd[0:n, c:c + 1], dstp[c * P:c * P + n, P - 1:P],
                              allow_slow_non_contiguous=True).then_inc(last_in, 16)
            act.dma_start(attb[:, :], att.rearrange("h d -> (h d)").unsqueeze(0).broadcast_to([P, D])).then_inc(c_in, 16)
            for i, a in enumerate((bias, gamma, beta)):
                act.dma_start(bg[:, i, :], a.unsqueeze(0).broadcast_to([P, D])).then_inc(c_in, 16)
            act.wait_ge(var_set, 1)
            nc.scalar.activation(std[:, :], rstd[:, :], ACT.Sqrt).then_inc(rooted, 1)
            for i in range(NW // 2):
                act.wait_ge(xT_ps, i + 1)
                nc.scalar.copy(xnT[:, :, 2 * i * P:(2 * i + 2) * P].rearrange("p c (w q) -> p w c q", q=P),
                               psT[:, i % 2, :].rearrange("p (w c q) -> p w c q", w=2, c=KC)).then_inc(xT_sb, 1)
            for j in range(2):
                for i in range(NW // 2):
                    n = j * (NW // 2) + i
                    act.wait_ge(proj, n + 1)
                    nc.scalar.copy(xlr[:, 2 * i:2 * i + 2, j, 0:D], psX[:, n % 2, :].rearrange("p (w f) -> p w f", w=2)
                                   ).then_inc(xlr_sb, 1)
                    if n == 2:
                        act.wait_ge(proj_lin, 1)
                        nc.scalar.copy(xlr[:, :, :, D:DX], psT[:, 0, 0:2 * HEADS * NW].rearrange(
                            "p (w j h) -> p w j h", w=NW, j=2)).then_inc(lin_sb, 1)
                    if j == 1:
                        act.wait_ge(lin_sb, 1)
                        act.wait_ge(xlr_sb, n + 1)
                        nc.scalar.copy(xr3_part(i, 0), xlr[:, 2 * i:2 * i + 2, 1, :]).then_inc(xr_hi, 1)
                if j == 0:
                    for n, (one, each) in enumerate(((pen1, pen), (go_on1, go_on))):
                        act.wait_ge(cut_set, n + 1)
                        nc.scalar.copy(each[:, 0:CH * HEADS * P].rearrange("p (c h e) -> p c h e", c=CH, h=HEADS),
                                       one[:, :, :].unsqueeze(2).broadcast_to([CI, CH, HEADS, P])).then_inc(by_head, 1)
            act.wait_ge(by_head, 2)
            act.wait_ge(c_in, 64)

        @block.gpsimd
        def _(g):
            nc.gpsimd.memset(ident[:, :], 0.0).then_inc(consts, 1)
            nc.gpsimd.memset(pad[:, 0, :], 0).then_inc(pad_set, 1)
            nc.gpsimd.memset(pad[:, 1, :], NPAD - 1).then_inc(pad_set, 1)
            g.wait_ge(consts, 1)
            nc.gpsimd.affine_select(out=ident[:, :], in_=ident[:, :], compare_op=ALU.not_equal, fill=1.0, base=0,
                                    pattern=[[-1, P]], channel_multiplier=1).then_inc(consts, 1)
            nc.gpsimd.iota(iotai[:, :], pattern=[[1, NI]], base=0, channel_multiplier=0).then_inc(iotas, 1)
            nc.gpsimd.iota(kcol_i[:, :], pattern=[[CI, CH]], base=0, channel_multiplier=1).then_inc(iotas, 1)
            nc.gpsimd.iota(pcol_i[:, :], pattern=[[P, CH]], base=0, channel_multiplier=1).then_inc(iotas, 1)
            g.wait_ge(t_set, 1)
            g.wait_ge(tables, 64)
            for c in range(CH):
                for to, tab in ((srcT, srcp), (dstT, dstp)):
                    nc.gpsimd.indirect_dma_start(out=to[:, c, :], out_offset=None, in_=tab,
                                                 in_offset=bass.IndirectOffsetOnAxis(ap=tcol_i[:, c:c + 1], axis=0)
                                                 ).then_inc(items_in, 16)
            g.wait_ge(srcI_set, 1)
            g.wait_ge(xl_out, 16)
            for r in range(AHEAD):
                gather_step(nc, G[r], xl_tab, srcI[:, r * U:(r + 1) * U], gathered[r])

        @block.tensor
        def _(pe):
            pe.wait_ge(consts, 2)
            pe.wait_ge(before_set, 1)
            for c in range(CH):
                nc.tensor.matmul(psI[0:1, 0:NI], ones[:, :], before[:, c, :], start=(c == 0), stop=(c == CH - 1))
            for m in range(CH):
                for c in range(CH):
                    last = nc.tensor.matmul(psJ[0:CI, m:m + 1], before[:, c, m * CI:(m + 1) * CI], ones[:, :],
                                            start=(c == 0), stop=(c == CH - 1))
            last.then_inc(t_ps, 1)
            pe.wait_ge(normed, NW)
            for i in range(NW // 2):
                if i >= 2:
                    pe.wait_ge(xT_sb, i - 1)
                for w in range(2):
                    for c in range(KC):
                        q = (w * KC + c) * P
                        last = nc.tensor.transpose(psT[:, i % 2, q:q + P], xn[:, 2 * i + w, c * P:(c + 1) * P], ident[:, :])
                last.then_inc(xT_ps, 1)
            pe.wait_ge(xT_sb, NW // 2)
            pe.wait_ge(w_in, 32)
            pe.wait_ge(watt_set, 1)
            def project(j, i):
                n = j * (NW // 2) + i
                if n >= 2:
                    pe.wait_ge(xlr_sb, n - 1)
                for w in range(2 * i, 2 * i + 2):
                    for c in range(KC):
                        last = nc.tensor.matmul(psX[:, n % 2, (w % 2) * D:(w % 2 + 1) * D], xnT[:, c, w * P:(w + 1) * P],
                                                Wlr[:, c, j * D:(j + 1) * D], start=(c == 0), stop=(c == KC - 1))
                last.then_inc(proj, 1)

            for i in range(3):
                project(0, i)
            for w in range(NW):
                for c in range(KC):
                    last = nc.tensor.matmul(psT[:, 0, w * 2 * HEADS:(w + 1) * 2 * HEADS], xnT[:, c, w * P:(w + 1) * P],
                                            Watt[:, c, :], start=(c == 0), stop=(c == KC - 1))
            last.then_inc(proj_lin, 1)
            for k, a in enumerate((srcF, relm)):
                pe.wait_ge(rel_set, k + 1)
                for c in range(CH):
                    last = nc.tensor.transpose(psE[:, k, c * CI:(c + 1) * CI], a[:, c, :], ident[0:CI, 0:CI])
                last.then_inc(rel_ps, 1)
            pe.wait_ge(gd_set, 1)
            for ps, e in ((psI, 0), (psJ, P - 1)):
                for c in range(CH):
                    last = nc.tensor.transpose(ps[0:HEADS, c * CI:(c + 1) * CI], gd[:, c, e:e + 1].broadcast_to([CI, HEADS]),
                                               ident[0:CI, 0:CI])
            last.then_inc(ends_ps, 1)
            for i in range(3, NW // 2):
                project(0, i)
            pe.wait_ge(linked, 1)
            for j in range(2):
                for c in range(CH):
                    q = (j * CH + c) * HEADS
                    last = nc.tensor.transpose(psI[0:CI, q:q + HEADS], link[:, c * CI + j:(c + 1) * CI + j],
                                               ident[0:HEADS, 0:HEADS])
            last.then_inc(link_ps, 1)
            for i in range(NW // 2):
                project(1, i)

        @block.vector
        def _(dve):
            c = Chain(dve, dv)
            nc.vector.memset(xs[:, :, :], 0.0).then_inc(zeroed, 1)
            nc.vector.memset(lastd[:, :], 1 << 20).then_inc(zeroed, 1)
            c(nc.vector.memset(ones[:, :], 1.0))
            c(nc.vector.memset(S[:, :, :], 0.0))
            dve.wait_ge(consts, 2)
            dve.wait_ge(iotas, 3)
            c(nc.vector.tensor_copy(prow[:, :], pcol_i[:, 0:1]))
            c(nc.vector.tensor_copy(iota32[:, :], iotai[:, 0:P]))
            c(nc.vector.tensor_copy(iotak[:, :], iotai[:, :]))
            c(nc.vector.tensor_copy(kcol[:, :], kcol_i[:, :]))
            c(nc.vector.tensor_copy(pcol[:, :], pcol_i[:, :]))
            dve.wait_ge(last_in, 48)
            c.then(nc.vector.tensor_scalar(lastd[:, :], lastd[:, :], 7, None, ALU.logical_shift_right))
            c.then(nc.vector.tensor_copy(lastf[:, :], lastd[:, :]))
            c.then(nc.vector.tensor_tensor(lastf[:, :], lastf[:, :], pcol[:, :], ALU.add))
            for j in range(CH):
                c(nc.vector.tensor_scalar(before[:, j, :], iotak[:, :], lastf[:, j:j + 1], None, ALU.is_gt))
            dve.wait_ge(dv, c.n)
            dve.sem_inc(before_set, 1)
            dve.wait_ge(x_in, 32)
            for w in range(NW):
                c(nc.vector.bn_stats(stats[:, w, :], xs[:, w, :]))
            dve.wait_ge(dv, c.n)
            for w in range(NW):
                c(nc.vector.bn_aggr(mv[:, w, :], stats[:, w, :]))
            dve.wait_ge(dv, c.n)
            nc.vector.tensor_scalar(rstd[:, :], mv[:, :, 1], LN_EPS, None, ALU.add).then_inc(var_set, 1)
            dve.wait_ge(rooted, 1)
            c.then(nc.vector.reciprocal(rstd[:, :], std[:, :]))
            for w in range(NW):
                nc.vector.tensor_scalar(xn[:, w, :], xs[:, w, :], mv[:, w, 0:1], rstd[:, w:w + 1],
                                        ALU.subtract, ALU.mult).then_inc(normed, 1)
            dve.wait_ge(t_ps, 1)
            c.then(nc.vector.tensor_tensor(wrf[:, :], iotak[0:1, :], psI[0:1, 0:NI], ALU.subtract))
            c.then(nc.vector.tensor_scalar(wrow[:, :, 0:U], wrf[:, :].rearrange("o (s u) -> o s u", u=U), float(NW - 1), None, ALU.min))
            c.then(nc.vector.tensor_tensor(wcol[:, :], kcol[:, :], psJ[0:CI, 0:CH], ALU.subtract))
            c.then(nc.vector.tensor_scalar(wcol[:, :], wcol[:, :], float(NW - 1), float(P), ALU.min, ALU.mult))
            nc.vector.tensor_scalar(tcol_i[:, :], psJ[0:CI, 0:CH], float(ROWS - 1), None, ALU.min).then_inc(t_set, 1)
            dve.wait_ge(c_in, 64)
            dve.wait_ge(w_in, 32)
            c.then(nc.vector.tensor_tensor(watp[:, :, :].rearrange("p c (j f) -> p (c j) f", j=2),
                                           Wlr[:, :, :].rearrange("p c (j f) -> p (c j) f", j=2),
                                           attb[:, :].unsqueeze(1).broadcast_to([P, 2 * KC, D]), ALU.mult))
            c.then(nc.vector.tensor_reduce(Watt[:, :, :], watp[:, :, :].rearrange("p c (h d) -> p c h d", d=HD), AX_X, ALU.add))
            nc.vector.tensor_scalar(Watt[:, :, :], Watt[:, :, :], SLOPE, None, ALU.mult).then_inc(watt_set, 1)
            c.then(nc.vector.tensor_scalar(attb[:, :], attb[:, :], 1.0 - SLOPE, None, ALU.mult))
            dve.wait_ge(items_in, 16 * 2 * CH)
            nc.vector.tensor_copy(srcF[:, :, :], srcT[:, :, :]).then_inc(rel_set, 1)
            c.then(nc.vector.tensor_copy(dstF[:, :, :], dstT[:, :, :]))
            for j in range(CH):
                c(nc.vector.tensor_scalar(dstF[:, j, :], dstF[:, j, :], wcol[:, j:j + 1], None, ALU.subtract))
            dve.wait_ge(dv, c.n)
            c.then(nc.vector.tensor_scalar(clampd[:, :, :], dstF[:, :, :], 0.0, float(P - 1), ALU.max, ALU.min))
            c.then(nc.vector.tensor_tensor(valid[:, :, :], clampd[:, :, :], dstF[:, :, :], ALU.is_equal))
            c.then(nc.vector.scalar_tensor_tensor(out=relm[:, :, :], in0=dstF[:, :, :], scalar=1.0, in1=valid[:, :, :],
                                                  op0=ALU.add, op1=ALU.mult))
            nc.vector.tensor_scalar(relm[:, :, :], relm[:, :, :], -1.0, None, ALU.add).then_inc(rel_set, 1)
            dve.wait_ge(rel_set, 2)
            nc.vector.tensor_copy(rel16[:, :, :], relm[:, :, :]).then_inc(rel16_set, 1)
            for j in range(CH):
                last = nc.vector.tensor_scalar(gd[:, j, :], clampd[:, j, :], wcol[:, j:j + 1], None, ALU.add)
                c(last) if j < CH - 1 else last.then_inc(gd_set, 1)
            dve.wait_ge(rel_ps, 1)
            nc.vector.tensor_copy(srcI[:, 0:NI], psE[:, 0, 0:NI]).then_inc(srcI_set, 1)
            c(nc.vector.memset(srcI[:, NI:NI + 3 * U], 0))
            dve.wait_ge(rel_ps, 2)
            c(nc.vector.tensor_copy(REL[:, 0:NI], psE[:, 1, 0:NI]))
            dve.wait_ge(gd_set, 1)
            V = nc.vector
            c(V.memset(cut[:, :, :], 1.0))
            c(V.memset(link[:, :], 0.0))
            c(V.memset(pen[:, CH * HEADS * P:CH * HEADS * P + 1], -BIG))
            c(V.memset(go_on[:, CH * HEADS * P:CH * HEADS * P + 1], 0.0))
            c(V.tensor_scalar(masked[:, :, :], valid[:, :, :], -1.0, 3 * BIG, ALU.add, ALU.mult))
            dve.wait_ge(ends_ps, 1)
            c(V.tensor_copy(ends_gd[:, 0, :], psI[0:HEADS, 0:NI]))
            c(V.tensor_copy(ends_gd[:, 1, :], psJ[0:HEADS, 0:NI]))
            dve.wait_ge(dv, c.n)
            c(V.tensor_tensor(cut[:, :, 1:P], gd[:, :, 1:P], gd[:, :, 0:P - 1], ALU.not_equal))
            V.tensor_tensor(link[:, 1:NI], ends_gd[:, 0, 1:NI], ends_gd[:, 1, 0:NI - 1], ALU.is_equal).then_inc(linked, 1)
            c(V.tensor_tensor(solid[:, :], ends_gd[:, 0, :], ends_gd[:, 1, :], ALU.is_equal))
            dve.wait_ge(dv, c.n)
            dve.wait_ge(linked, 1)
            V.tensor_scalar(pen1[:, :, :], cut[:, :, :], -BIG, None, ALU.mult).then_inc(cut_set, 1)
            V.tensor_scalar(go_on1[:, :, :], cut[:, :, :], 0.0, None, ALU.is_equal).then_inc(cut_set, 1)
            c(V.tensor_tensor(through[:, 0, :], link[:, 0:NI], solid[:, :], ALU.mult))
            c(V.tensor_tensor(through[:, 1, :], link[:, 1:NI + 1], solid[:, :], ALU.mult))
            dve.wait_ge(link_ps, 1)
            c(V.tensor_copy(linkc[:, :, :], psI[0:CI, 0:2 * CH * HEADS].rearrange(
                "p (j c h) -> p j c h", j=2, c=CH)[:, :, :, 0]))
            dve.wait_ge(dv, c.n)
            c(V.tensor_scalar(through_pen[:, :, :], through[:, :, :], -1.0, BIG, ALU.add, ALU.mult))
            for j, e in ((0, 0), (1, P - 1)):
                for k in range(CH):
                    c(V.tensor_scalar(ends[:, j, k, :], gd[:, k, :], gd[:, k, e:e + 1], linkc[:, j, k:k + 1],
                                      ALU.is_equal, ALU.mult))
            dve.wait_ge(dv, c.n)
            c.then(V.tensor_scalar(ends_pen[:, :, :, :], ends[:, :, :, :], -1.0, BIG, ALU.add, ALU.mult))
            for i in range(NW // 2):
                xr = xlr[:, 2 * i:2 * i + 2, 1, :]
                part = [xr3_part(i, j) for j in range(3)]
                dve.wait_ge(xr_hi, i + 1)
                c.then(V.tensor_tensor(rem[:, 2 * i:2 * i + 2, :], xr, part[0], ALU.subtract))
                c.then(V.tensor_copy(part[1], rem[:, 2 * i:2 * i + 2, :]))
                c(V.tensor_tensor(part[2], rem[:, 2 * i:2 * i + 2, :], part[1], ALU.subtract))
            dve.wait_ge(dv, c.n)


def score_phase(nc, v):
    xs_d, ys_d, G, gathered = (v[k] for k in "xs_d ys_d G gathered".split())
    xl_tab, gathered_d, rel_d, prow, xr3, attb, S, srcI, wrow = (
        v[k] for k in "xl_tab gathered_d rel_d prow xr3 attb S srcI wrow".split())
    BODY = 6
    assert STEPS % BODY == 0
    with ExitStack() as ctx:
        def sb(name, shape, dt=F32):
            return ctx.enter_context(nc.sbuf_tensor(name, shape, dt))

        def sem(name):
            return ctx.enter_context(nc.semaphore(name))

        idx = sb("idx", [P, GR, U], I32)
        lin = sb("lin", [P, NI, HEADS])
        esum = sb("esum", [P, 2, U * D])
        leaky = sb("leaky", [P, 2, U * D])
        relb = [sb(f"relb{b}", [P, U * P], BF16) for b in range(2)]
        MT = sb("MT", [P, 2, U * P], BF16)
        psE = [ctx.enter_context(nc.psum_tensor(f"psE{b}", [P, -(-U * DX // 512) * 512], F32)) for b in range(2)]
        zslot = sb("zslot", [CAP, D])
        zset, zout = sem("zslot_set"), sem("zslot_out")
        spilled = [sem(f"spilled{g}") for g in range(GR)]
        turn = sem("turn")
        idx_set = sem("idx_set")
        rel_in = [sem(f"rel_in{b}") for b in range(2)]
        onehot = sem("onehot")
        expanded = sem("expanded")
        summed = sem("summed")
        leaked = sem("leaked")
        weighted = sem("att_mul")
        scored = sem("scored")
        lin_set, totalled = sem("lin_set"), sem("totalled")
        block = ctx.enter_context(nc.Block())

        def steps(eng, step, first=None):
            with eng.Fori(0, STEPS // BODY) as i:
                if first:
                    first(i)
                for j in range(BODY):
                    step(i * BODY + j, j % 2, j % GR, i * (BODY // GR) + (j // GR + 1))

        @block.gpsimd
        def _(g):
            nc.gpsimd.memset(zslot[:, :], 0.0).then_inc(zset, 1)
            for r in range(GR):
                g.sem_inc(spilled[r], 16)

            for r in range(AHEAD, GR):
                gather_step(nc, G[r], xl_tab, srcI[:, r * U:(r + 1) * U], gathered[r])
            with g.Fori(1, STEPS // GR) as i:
                for r in range(GR):
                    s = i * GR + r
                    g.wait_ge(summed, s + 1)
                    g.sem_inc(turn, 1)
                    g.wait_ge(spilled[r], i * 16 + 16)
                    g.sem_inc(turn, 1)
                    g.wait_ge(idx_set, s - (GR - 1))
                    g.sem_inc(turn, 1)
                    gather_step(nc, G[r], xl_tab, idx[:, r, :], gathered[r])

        @block.sync
        def _(sp):
            def load_rel(b, s):
                sp.dma_start(relb[b][:, :], rel_d[bass.ds(s * U, U), :].rearrange("(o u) e -> o (u e)", o=1)
                             .broadcast_to([P, U * P])).then_inc(rel_in[b], 16)

            def clear(of, lo, n):
                sp.dma_start(of.rearrange("(b s) f -> s b f", s=CAP)[:, bass.ds(lo, n), :],
                             zslot[:, :].unsqueeze(1).broadcast_to([CAP, n, D])).then_inc(zout, 16)

            def step(s, b, r, n):
                sp.wait_ge(onehot, s + 1)
                load_rel(b, s + 2)
                sp.wait_ge(gathered[r], n * (16 * U))
                sp.dma_start(gathered_d[bass.ds(s, 1), :, :].rearrange("s p f -> (s p) f"),
                             G[r][:, :, 0:D]).then_inc(spilled[r], 16)

            for b in range(2):
                load_rel(b, b)
            turns = STEPS // BODY
            nx, ny = (NE + OVB) // turns, OVB // turns
            sp.wait_ge(zset, 1)
            rest = [(xs_d, turns * nx, NE + OVB - turns * nx), (ys_d, NE + turns * ny, OVB - turns * ny)]
            rest = [r for r in rest if r[2]]
            for r in rest:
                clear(*r)
            steps(sp, step, lambda i: (clear(xs_d, i * nx, nx), clear(ys_d, i * ny + NE, ny)))
            sp.wait_ge(zout, 16 * (2 * turns + len(rest)))
            for r in range(GR):
                sp.wait_ge(spilled[r], 16 * (STEPS // GR + 1))
            for b in range(2):
                sp.wait_ge(rel_in[b], 16 * (STEPS // 2 + 1))

        @block.tensor
        def _(pe):
            pe.sem_inc(expanded, 2)
            regs = [pe.alloc_register(f"window{u}") for u in range(U)]
            def expand(s, b, r, n):
                ws = load_windows(pe, regs, wrow, s)
                pe.wait_ge(onehot, s + 1)
                pe.wait_ge(summed, s + GR - 1)
                for u in range(U):
                    w = ws[u]
                    for j in range(3):
                        last = nc.tensor.matmul(psE[b][:, u * D:(u + 1) * D], MT[:, b, u * P:(u + 1) * P],
                                                xr3[:, bass.ds(w * (3 * DX) + j * DX, D)],
                                                start=(j == 0), stop=(j == 2))
                    q = U * D + u * HEADS
                    for j in range(3):
                        last = nc.tensor.matmul(psE[b][:, q:q + HEADS], MT[:, b, u * P:(u + 1) * P],
                                                xr3[:, bass.ds(w * (3 * DX) + j * DX + D, HEADS)],
                                                start=(j == 0), stop=(j == 2))
                last.then_inc(expanded, 1)

            steps(pe, expand)

        @block.scalar
        def _(act):
            act.sem_inc(leaked, 1)

            def copy_idx(r, s):
                nc.scalar.copy(idx[:, r, :], srcI[:, bass.ds(s * U, U)]).then_inc(idx_set, 1)

            def leak(s, b, r, n):
                act.wait_ge(summed, s + GR + 1)
                act.wait_ge(scored, s + 1)
                nc.scalar.activation(leaky[:, b, :], esum[:, b, :], ACT.Relu).then_inc(leaked, 1)
                copy_idx(r, s + GR)

            steps(act, leak)

        @block.vector
        def _(dve):
            dve.sem_inc(summed, GR)
            nc.vector.memset(leaky[:, 1, :], 0.0).then_inc(scored, 1)
            dve.wait_ge(scored, 1)

            def build_onehot(b, n):
                dve.wait_ge(rel_in[b], n)
                nc.vector.tensor_scalar(MT[:, b, :], relb[b][:, :], prow[:, 0:1], None, ALU.is_equal).then_inc(onehot, 1)

            def weight(b, s):
                dve.wait_ge(leaked, s + 1)
                nc.vector.tensor_tensor(leaky[:, b, :].rearrange("p (u f) -> p u f", u=U),
                                        leaky[:, b, :].rearrange("p (u f) -> p u f", u=U),
                                        attb[:, :].unsqueeze(1).broadcast_to([P, U, D]), ALU.mult).then_inc(weighted, 1)

            def dot(b, s):
                dve.wait_ge(weighted, s + 1)
                nc.vector.tensor_reduce(S[:, bass.ds(s * U, U), :], leaky[:, b, :].rearrange("p (u h d) -> p u h d", u=U, h=HEADS),
                                        AX_X, ALU.add).then_inc(scored, 1)

            def step(i, j):
                s, b, r = i * BODY + j, j % 2, j % GR
                weight(1 - b, s)
                dve.wait_ge(expanded, s + 2)
                build_onehot(1 - b, i * (16 * BODY // 2) + 16 * ((j + 1) // 2 + 1))
                dve.wait_ge(expanded, s + 3)
                dve.wait_ge(gathered[r], i * (BODY // GR * 16 * U) + (j // GR + 1) * 16 * U)
                nc.vector.tensor_tensor(esum[:, b, :].rearrange("p (u f) -> p u f", u=U),
                                        psE[b][:, 0:U * D].rearrange("p (u f) -> p u f", u=U), G[r][:, :, 0:D], ALU.add)
                nc.vector.tensor_tensor(lin[:, bass.ds(s * U, U), :], psE[b][:, U * D:U * DX].rearrange("p (u h) -> p u h", u=U),
                                        G[r][:, :, D:DX], ALU.add).then_inc(summed, 1)
                dot(1 - b, s)

            build_onehot(0, 16)
            with dve.Fori(0, STEPS // BODY) as i:
                for j in range(BODY):
                    step(i, j)
            weight(1, STEPS)
            dot(1, STEPS)
            dve.wait_ge(scored, STEPS + 2)
            dve.wait_ge(summed, STEPS + GR)
            nc.vector.tensor_tensor(S[:, U:U + NI, :], S[:, U:U + NI, :], lin[:, :, :], ALU.add).then_inc(totalled, 1)
            dve.wait_ge(totalled, 1)


def softmax_phase(nc, v):
    ident, S, A, gathered_d, R, loaded = (v[k] for k in "ident S A gathered_d R loaded".split())
    pen, go_on, masked, ends, ends_pen, through, through_pen = (
        v[k] for k in "pen go_on masked ends ends_pen through through_pen".split())
    with ExitStack() as ctx:
        def sb(name, shape, dt=F32):
            return ctx.enter_context(nc.sbuf_tensor(name, shape, dt))

        def sem(name):
            return ctx.enter_context(nc.semaphore(name))

        full = [CI, CH, HEADS, P]
        T = sb("T", full)
        fwd = sb("fwd", full)
        bwd = sb("bwd", full)
        tot = sb("tot", full)
        carry = sb("carry", [HEADS, 2, NI + 1])
        cin = sb("cin", [CI, 2, CH, HEADS])
        psS = [ctx.enter_context(nc.psum_tensor(f"psS{c}", [P, 512], F32)) for c in range(CH)]
        psR = [ctx.enter_context(nc.psum_tensor(f"psR{j}", [P, 512], F32)) for j in range(2)]
        psC = ctx.enter_context(nc.psum_tensor("psC", [P, 512], F32))

        dv = sem("dv_soft")
        scores_ps = sem("scores_ps")
        scanned = [sem("scanned_fwd"), sem("scanned_bwd")]
        rows_ps = [sem("rows_fwd"), sem("rows_bwd")]
        carried, cin_ps = sem("carried"), sem("cin_ps")
        shifted, expd = sem("shifted"), sem("expd")
        alpha, alpha_ps, alpha_set = sem("alpha"), sem("alpha_ps"), sem("alpha_set")
        block = ctx.enter_context(nc.Block())

        @block.sync
        def _(sp):
            for b in range(AR):
                load_sources(sp, gathered_d, R, loaded, b, b)

        @block.tensor
        def _(pe):
            for c in range(CH):
                for h in range(HEADS):
                    last = nc.tensor.transpose(psS[c][0:CI, h * P:(h + 1) * P], S[:, U + c * CI:U + (c + 1) * CI, h], ident[:, :])
                last.then_inc(scores_ps, 1)
            for r in range(2):
                for j, (scan, e) in enumerate(((fwd, P - 1), (bwd, 0))):
                    for c in range(CH):
                        pe.wait_ge(scanned[j], r * CH + c + 1)
                        last = nc.tensor.transpose(psR[j][0:HEADS, c * CI:(c + 1) * CI], scan[:, c, :, e], ident[0:CI, 0:CI])
                    last.then_inc(rows_ps[j], 1)
                for j in range(2):
                    pe.wait_ge(carried, 2 * r + j + 1)
                    for c in range(CH):
                        q = (j * CH + c) * HEADS
                        last = nc.tensor.transpose(psC[0:CI, q:q + HEADS], carry[:, j, c * CI + j:(c + 1) * CI + j],
                                                   ident[0:HEADS, 0:HEADS])
                last.then_inc(cin_ps, 1)
            for c in range(CH):
                pe.wait_ge(alpha, c + 1)
                for h in range(HEADS):
                    last = nc.tensor.transpose(psS[c][:, h * CI:(h + 1) * CI], T[:, c, h, :], ident[0:CI, 0:CI])
                last.then_inc(alpha_ps, 1)

        @block.scalar
        def _(act):
            for k in range(CH):
                act.wait_ge(shifted, k + 1)
                nc.scalar.activation(T[:, k, :, :], T[:, k, :, :], ACT.Exp).then_inc(expd, 1)
            for k in range(CH):
                act.wait_ge(alpha_ps, k + 1)
                nc.scalar.copy(A[:, k * CI:(k + 1) * CI, :], psS[k][:, 0:HEADS * CI].rearrange("p (h i) -> p i h", h=HEADS)
                               ).then_inc(alpha_set, 1)
            act.wait_ge(alpha_set, CH)

        @block.vector
        def _(dve):
            c = Chain(dve, dv)
            V = nc.vector

            def by_head(mark):
                return mark.unsqueeze(1).broadcast_to([CI, HEADS, P])

            def chunk(a, k):
                return a[:, k, :, :].rearrange("p h e -> p (h e)")

            def scan_chunk(k, marks, at_start, op0, op1):
                lo, hi = k * HEADS * P, (k + 1) * HEADS * P
                V.tensor_tensor_scan(chunk(fwd, k), marks[:, lo:hi], chunk(T, k), at_start, op0, op1).then_inc(scanned[0], 1)
                V.tensor_tensor_scan(chunk(bwd, k)[:, ::-1], marks[:, lo + 1:hi + 1][:, ::-1], chunk(T, k)[:, ::-1],
                                     at_start, op0, op1).then_inc(scanned[1], 1)

            def scan_items(r, marks, at_start, op0, op1):
                V.memset(carry[:, 0, 0:1], at_start)
                V.memset(carry[:, 1, NI:NI + 1], at_start)
                dve.wait_ge(rows_ps[0], r + 1)
                V.tensor_tensor_scan(carry[:, 0, 1:NI + 1], marks[:, 0, :], psR[0][0:HEADS, 0:NI], at_start, op0, op1
                                     ).then_inc(carried, 1)
                dve.wait_ge(rows_ps[1], r + 1)
                V.tensor_tensor_scan(carry[:, 1, 0:NI][:, ::-1], marks[:, 1, :][:, ::-1], psR[1][0:HEADS, 0:NI][:, ::-1],
                                     at_start, op0, op1).then_inc(carried, 1)
                dve.wait_ge(cin_ps, r + 1)
                c.then(V.tensor_copy(cin[:, :, :, :], psC[0:CI, 0:2 * CH * HEADS].rearrange("p (j c h) -> p j c h", j=2, c=CH)))

            for k in range(CH):
                dve.wait_ge(scores_ps, k + 1)
                c(V.tensor_tensor(T[:, k, :, :], psS[k][0:CI, :].rearrange("p (h e) -> p h e", h=HEADS), by_head(masked[:, k, :]), ALU.add))
            dve.wait_ge(dv, c.n)
            for k in range(CH):
                scan_chunk(k, pen, -BIG, ALU.add, ALU.max)
            dve.wait_ge(scanned[0], CH)
            dve.wait_ge(scanned[1], CH)
            c(V.scalar_tensor_tensor(out=tot[:, :, :, :], in0=fwd[:, :, :, :], scalar=-BIG, in1=bwd[:, :, :, :],
                                     op0=ALU.max, op1=ALU.max))
            scan_items(0, through_pen, -BIG, ALU.add, ALU.max)
            for j in range(2):
                for k in range(CH):
                    for h in range(HEADS):
                        c(V.scalar_tensor_tensor(out=tot[:, k, h, :], in0=ends_pen[:, j, k, :], scalar=cin[:, j, k, h:h + 1],
                                                 in1=tot[:, k, h, :], op0=ALU.add, op1=ALU.max))
                dve.wait_ge(dv, c.n)
            for k in range(CH):
                V.tensor_tensor(T[:, k, :, :], T[:, k, :, :], tot[:, k, :, :], ALU.subtract).then_inc(shifted, 1)
            for k in range(CH):
                dve.wait_ge(expd, k + 1)
                scan_chunk(k, go_on, 0.0, ALU.mult, ALU.add)
            dve.wait_ge(scanned[0], 2 * CH)
            dve.wait_ge(scanned[1], 2 * CH)
            c.then(V.scalar_tensor_tensor(out=tot[:, :, :, :], in0=fwd[:, :, :, :], scalar=SM_EPS, in1=bwd[:, :, :, :],
                                          op0=ALU.add, op1=ALU.add))
            c(V.tensor_tensor(tot[:, :, :, :], tot[:, :, :, :], T[:, :, :, :], ALU.subtract))
            scan_items(1, through, 0.0, ALU.mult, ALU.add)
            for j in range(2):
                for k in range(CH):
                    for h in range(HEADS):
                        c(V.scalar_tensor_tensor(out=tot[:, k, h, :], in0=ends[:, j, k, :], scalar=cin[:, j, k, h:h + 1],
                                                 in1=tot[:, k, h, :], op0=ALU.mult, op1=ALU.add))
                dve.wait_ge(dv, c.n)
            for k in range(CH):
                c(V.reciprocal(tot[:, k, :, :], tot[:, k, :, :]))
            for k in range(CH):
                dve.wait_ge(dv, c.n - CH + k + 1)
                V.tensor_tensor(T[:, k, :, :], T[:, k, :, :], tot[:, k, :, :], ALU.mult).then_inc(alpha, 1)


def aggregate_phase(nc, v):
    (gathered_d, iota32, A, REL, wrow, bg, xs, xn, R, loaded, agg, W1, W2, w1, w2, w_in) = (
        v[k] for k in "gathered_d iota32 A REL wrow bg xs xn R loaded agg W1 W2 w1 w2 w_in".split())
    with ExitStack() as ctx:
        def sb(name, shape, dt=F32):
            return ctx.enter_context(nc.sbuf_tensor(name, shape, dt))

        def sem(name):
            return ctx.enter_context(nc.semaphore(name))

        msg = [sb(f"msg{b}", [P, U * D]) for b in range(AR)]
        M = [sb(f"M32_{b}", [P, U * P]) for b in range(AR)]
        zero = sb("zero", [P, 512])

        zset, zeroed = sem("zset"), sem("agg_zeroed")
        shared = sem("msg_shared")
        weighted = sem("weighted")
        added = sem("added")
        folded = sem("folded")
        block = ctx.enter_context(nc.Block())

        @block.sync
        def _(sp):
            turns = (STEPS // AR - 1) // EARLY
            for q in range(EARLY):
                load_weights(sp, W1, W2, w1, w2, w_in, q, q)
                with sp.Fori(1 + q * turns, 1 + (q + 1) * turns if q < EARLY - 1 else STEPS // AR) as i:
                    for b in range(AR):
                        s = i * AR + b
                        sp.wait_ge(weighted, s + 1)
                        sp.wait_ge(shared, s + 1)
                        load_sources(sp, gathered_d, R, loaded, b, s)

        @block.tensor
        def _(pe):
            pe.sem_inc(added, AR)
            regs = [pe.alloc_register(f"agg_window{u}") for u in range(U)]
            pe.wait_ge(zset, 1)
            for j in range(NW * D // 512):
                nc.tensor.matmul(agg[:, j * 512:(j + 1) * 512], zero[:, 0:P], zero[:, :], start=True, stop=False,
                                 skip_group_check=True)
            with pe.Fori(0, STEPS // AR) as i:
                for b in range(AR):
                    s = i * AR + b
                    ws = load_windows(pe, regs, wrow, s)
                    pe.wait_ge(shared, s + AR + 1)
                    pe.wait_ge(weighted, s + AR + 1)
                    for u in range(U):
                        w = ws[u]
                        last = nc.tensor.matmul(agg[:, bass.ds(w * D, D)], M[b][:, u * P:(u + 1) * P],
                                                msg[b][:, u * D:(u + 1) * D], start=False, stop=False, skip_group_check=True)
                    last.then_inc(added, 1)

        @block.scalar
        def _(act):
            act.sem_inc(shared, AR)
            with act.Fori(0, STEPS // AR) as i:
                for b in range(AR):
                    s = i * AR + b
                    act.wait_ge(added, s + 1)
                    act.wait_ge(loaded[b], i * 16 + 16)
                    for h in range(HEADS):
                        q = (U - 1) * D + h * HD
                        last = nc.scalar.activation(msg[b][:, q:q + HD], R[b][:, q:q + HD], ACT.Copy,
                                                    scale=A[:, bass.ds(s * U + U - 1, 1), h])
                    last.then_inc(shared, 1)

        @block.gpsimd
        def _(g):
            nc.gpsimd.tensor_tensor(xs[:, :, :], xs[:, :, :], bg[:, 2, :].unsqueeze(1).broadcast_to([P, NW, D]), ALU.add
                                    ).then_inc(folded, 1)
            nc.gpsimd.tensor_scalar(xn[:, :, :], xn[:, :, :], -1.0, None, ALU.add).then_inc(folded, 1)
            g.wait_ge(folded, 2)

        @block.vector
        def _(dve):
            V = nc.vector
            dve.sem_inc(weighted, AR)
            V.memset(zero[:, :], 0.0).then_inc(zset, 1)
            with dve.Fori(0, STEPS // AR) as i:
                for b in range(AR):
                    s = i * AR + b
                    dve.wait_ge(added, s + 1)
                    for u in range(U):
                        V.tensor_scalar(M[b][:, u * P:(u + 1) * P], iota32[:, :], REL[:, bass.ds(s * U + u, 1)], None,
                                        ALU.is_equal)
                    dve.wait_ge(loaded[b], i * 16 + 16)
                    n = U - 1
                    V.tensor_tensor(msg[b][:, 0:n * D].rearrange("p (u d) -> p u d", d=HD),
                                    R[b][:, 0:n * D].rearrange("p (u d) -> p u d", d=HD),
                                    A[:, bass.ds(s * U, n), :].rearrange("p u h -> p (u h)").unsqueeze(2).broadcast_to([P, n * HEADS, HD]),
                                    ALU.mult).then_inc(weighted, 1)
            dve.wait_ge(added, STEPS + AR)


def route_phase(nc, v):
    (ident, prow, iota32, Rw, Rb, b1, xs_d, h_in, gates, slot, nov, ovx, b1T) = (v[k] for k in (
        "ident prow iota32 Rw Rb b1 xs_d h_in gates slot nov ovx b1T").split())
    (bg, xs, xn, agg, W1, W2, w1, w2, w_in) = (v[k] for k in "bg xs xn agg W1 W2 w1 w2 w_in".split())
    GROUPS = (range(0, 6), range(6, NW))
    B1W = 512 // NE
    MORE = -(-N // CAP) - 1
    PARTS = ((0, 0, 2), (0, 2, 5), (0, 5, B1W), (1, B1W, NW))
    with ExitStack() as ctx:
        def sb(name, shape, dt=F32):
            return ctx.enter_context(nc.sbuf_tensor(name, shape, dt))

        def sem(name):
            return ctx.enter_context(nc.semaphore(name))

        z = sb("z", [P, NW, D])
        ez = sb("ez", [P, NW, D])
        rz = h_in
        hT = ez
        stats = sb("stats2", [P, 2, NW, 6])
        mv = sb("mv2", [P, 2, NW, 2])
        vare = sb("vare", [P, 2, NW])
        std = sb("std2", [P, 2, NW])
        rstd = sb("rstd2", [P, 2, NW])
        Rws = sb("Rws", [P, KC, NE])
        Rbb = sb("Rbb", [P, NE])
        lg = sb("lg", [P, NW, NE])
        top = sb("top", [P, NW, 8])
        topi = sb("topi", [P, NW, 8], mybir.dt.uint32)
        topf = sb("topf", [P, TOPK, NW])
        pick = sb("pick", [P, TOPK, NW, NE])
        both = sb("both", [P, NW, NE], BF16)
        ones = sb("onesb", [P, P], BF16)
        tri = sb("tri", [P, P], BF16)
        nil = sb("nil", [P, 512], BF16)
        live = sb("live", [P, 1])
        cnt = sb("cnt", [P, NE])
        more = sb("more", [P, NE])
        zrow = sb("zrow", [P, NE])
        fulls = sb("fulls", [P, MORE])
        over = sb("over", [P, NE, MORE])
        upto = sb("upto", [P, NE + 1])
        first_at = sb("first_at", [P, NE])
        delta = sb("delta", [P, NE])
        place = lg
        slotf = sb("slotf", [P, TOPK, NW])
        diff = sb("diff", [P, NW])
        past = sb("past", [P, NE])
        ovc = sb("ovc", [P, 1])
        psT = ctx.enter_context(nc.psum_tensor("psTr", [P, 2, 512], F32))
        psK = agg[:, 0:1024].rearrange("p (j n) -> p j n", j=2)
        psL = agg[:, 1024:2048].rearrange("p (j n) -> p j n", j=2)
        psO = agg[:, 2048:2048 + P]

        rw_in, dv, consts = sem("rw_in"), sem("dv_route"), sem("consts_r")
        z_set = sem("z_set")
        expz, relu_set, lifted = sem("expz"), sem("relu_set"), sem("lifted")
        vard, rooted = sem("vard"), sem("rooted2")
        normed = sem("normed")
        hT_ps, hT_sb = sem("hT_ps"), sem("hT_sb")
        lg_ps, picked, ranked, shifted, expd, slots, moved, ov_set, ov_ps = map(
            sem, ("lg_ps", "picked", "ranked", "shifted_r", "expd_r", "slots", "moved", "ov_set", "ov_ps"))
        block = ctx.enter_context(nc.Block())

        @block.sync
        def _(sp):
            sp.dma_start(Rws[:, :, :], Rw.rearrange("(c p) n -> p c n", p=P)).then_inc(rw_in, 16)
            sp.dma_start(Rbb[:, :], Rb.unsqueeze(0).broadcast_to([P, NE])).then_inc(rw_in, 16)
            sp.dma_start(b1T[:, :, :], b1.rearrange("e (p m) -> p e m", m=HC)).then_inc(rw_in, 16)
            for q in range(EARLY, RING):
                load_weights(sp, W1, W2, w1, w2, w_in, q, q)
            sp.wait_ge(rw_in, 48)

        @block.scalar
        def _(act):
            for i in range(NW // 2):
                act.wait_ge(z_set, i + 1)
                nc.scalar.activation(rz[:, 2 * i:2 * i + 2, :], z[:, 2 * i:2 * i + 2, :], ACT.Relu).then_inc(relu_set, 1)
                nc.scalar.activation(ez[:, 2 * i:2 * i + 2, :], z[:, 2 * i:2 * i + 2, :], ACT.Exp).then_inc(expz, 1)
            n = 0
            for r in range(2):
                for ws in GROUPS:
                    lo, hi = ws[0], ws[-1] + 1
                    n += 1
                    act.wait_ge(vard, n)
                    nc.scalar.activation(std[:, r, lo:hi], vare[:, r, lo:hi], ACT.Sqrt).then_inc(rooted, 1)
            for w in range(NW):
                act.wait_ge(hT_ps, w + 1)
                nc.scalar.copy(hT[:, w, :], psT[:, w % 2, 0:KC * P]).then_inc(hT_sb, 1)
            act.wait_ge(shifted, 1)
            nc.scalar.activation(gates[:, :, 1], diff[:, :], ACT.Exp).then_inc(expd, 1)

        @block.gpsimd
        def _(g):
            G = nc.gpsimd
            c = Chain(g, consts)
            c(G.memset(nil[:, :], 0.0))
            c.then(G.memset(ones[:, :], 1.0))
            c(G.affine_select(out=tri[:, :], in_=ones[:, :], compare_op=ALU.is_gt, fill=0.0, base=0,
                              pattern=[[1, P]], channel_multiplier=-1))
            for i in range(NW // 2):
                two = slice(2 * i, 2 * i + 2)
                g.wait_ge(relu_set, i + 1)
                G.tensor_tensor(rz[:, two, :], rz[:, two, :], xn[:, two, :], ALU.add).then_inc(lifted, 1)
            for w in range(NW):
                for j, (bank, lo, hi) in enumerate(PARTS):
                    if w == lo:
                        g.wait_ge(slots, j + 1)
                n = P if w < NW - 1 else NREM
                for k in range(TOPK):
                    G.indirect_dma_start(out=xs_d, out_offset=bass.IndirectOffsetOnAxis(ap=slot[0:n, k, w:w + 1], axis=0),
                                         in_=h_in[0:n, w, :], in_offset=None).then_inc(moved, 16)
            g.wait_ge(moved, 16 * TOPK * NW)

        @block.tensor
        def _(pe):
            pe.wait_ge(rw_in, 48)
            for j, ws in enumerate(GROUPS):
                for w in ws:
                    pe.wait_ge(normed, w + 1)
                    if w >= 2:
                        pe.wait_ge(hT_sb, w - 1)
                    for c in range(KC):
                        last = nc.tensor.transpose(psT[:, w % 2, c * P:(c + 1) * P], h_in[:, w, c * P:(c + 1) * P], ident[:, :])
                    last.then_inc(hT_ps, 1)
                for w in ws:
                    pe.wait_ge(hT_sb, w + 1)
                    to = psL[:, j, (w - ws[0]) * NE:(w - ws[0] + 1) * NE]
                    for c in range(KC):
                        last = nc.tensor.matmul(to, hT[:, w, c * P:(c + 1) * P], Rws[:, c, :], start=(c == 0), stop=(c == KC - 1))
                last.then_inc(lg_ps, 1)
            pe.wait_ge(consts, 3)
            for bank in range(2):
                nc.tensor.matmul(psK[:, bank, :], nil[:, 0:P], nil[:, :], start=True, stop=False, skip_group_check=True)
            for j, ws in enumerate(GROUPS):
                pe.wait_ge(picked, j + 1)
                for w in ws:
                    for bank, lo, hi in ((0, w + 1, B1W), (1, max(w + 1, B1W), NW + 1)):
                        if lo < hi:
                            nc.tensor.matmul(psK[:, bank, (lo - bank * B1W) * NE:(hi - bank * B1W) * NE], ones[:, :],
                                             both[:, w, :].unsqueeze(1).broadcast_to([P, hi - lo, NE]),
                                             start=False, stop=False, skip_group_check=True)
                    last = nc.tensor.matmul(psK[:, w // B1W, (w % B1W) * NE:(w % B1W + 1) * NE], tri[:, :], both[:, w, :],
                                            start=False, stop=(w == NW - 1), skip_group_check=True)
            last.then_inc(ranked, 1)
            pe.wait_ge(ov_set, 1)
            nc.tensor.transpose(psO[0:1, :], ovc[:, :], ident[:, :]).then_inc(ov_ps, 1)

        @block.vector
        def _(dve):
            V = nc.vector
            c = Chain(dve, dv)

            for i in range(NW // 2):
                V.tensor_tensor(z[:, 2 * i:2 * i + 2, :], agg[:, 2 * i * D:(2 * i + 2) * D].rearrange("p (w f) -> p w f", w=2),
                                bg[:, 0, :].unsqueeze(1).broadcast_to([P, 2, D]), ALU.add).then_inc(z_set, 1)

            def variances(r, of, ws):
                for w in ws:
                    c(V.bn_stats(stats[:, r, w, :], of[:, w, :]))
                for n, w in enumerate(ws):
                    dve.wait_ge(dv, c.n - len(ws) + 1)
                    c(V.bn_aggr(mv[:, r, w, :], stats[:, r, w, :]))
                dve.wait_ge(dv, c.n)
                V.tensor_scalar(vare[:, r, ws[0]:ws[-1] + 1], mv[:, r, ws[0]:ws[-1] + 1, 1], LN_EPS, None, ALU.add
                                ).then_inc(vard, 1)

            def inverse_roots(r, ws, n):
                dve.wait_ge(rooted, n)
                c.then(V.reciprocal(rstd[:, r, ws[0]:ws[-1] + 1], std[:, r, ws[0]:ws[-1] + 1]))

            for ws in GROUPS:
                for i in range(ws[0] // 2, (ws[-1] + 1) // 2):
                    two = slice(2 * i, 2 * i + 2)
                    dve.wait_ge(expz, i + 1)
                    dve.wait_ge(lifted, i + 1)
                    c(V.scalar_tensor_tensor(out=z[:, two, :], in0=ez[:, two, :], scalar=1.0, in1=rz[:, two, :],
                                             op0=ALU.min, op1=ALU.add))
                dve.wait_ge(dv, c.n)
                variances(0, z, ws)
            for j, ws in enumerate(GROUPS):
                inverse_roots(0, ws, j + 1)
                for w in ws:
                    c(V.scalar_tensor_tensor(out=z[:, w, :], in0=z[:, w, :], scalar=mv[:, 0, w, 0:1], in1=bg[:, 1, :],
                                             op0=ALU.subtract, op1=ALU.mult))
                for n, w in enumerate(ws):
                    dve.wait_ge(dv, c.n - len(ws) + 1)
                    c(V.scalar_tensor_tensor(out=xs[:, w, :], in0=z[:, w, :], scalar=rstd[:, 0, w:w + 1], in1=xs[:, w, :],
                                             op0=ALU.mult, op1=ALU.add))
                dve.wait_ge(dv, c.n)
                variances(1, xs, ws)
            for j, ws in enumerate(GROUPS):
                inverse_roots(1, ws, j + 3)
                for w in ws:
                    V.tensor_scalar(h_in[:, w, :], xs[:, w, :], mv[:, 1, w, 0:1], rstd[:, 1, w:w + 1], ALU.subtract, ALU.mult
                                    ).then_inc(normed, 1)
            c(V.memset(zrow[:, :], 0.0))
            c(V.memset(upto[:, 0:1], 0.0))
            c(V.tensor_scalar(fulls[:, :], iota32[:, 1:MORE + 1], float(CAP), None, ALU.mult))
            c.then(V.tensor_scalar(live[:, :], prow[:, :], float(NREM), None, ALU.is_lt))
            for j, ws in enumerate(GROUPS):
                lo, hi, n = ws[0], ws[-1] + 1, len(ws)
                dve.wait_ge(lg_ps, j + 1)
                c.then(V.tensor_tensor(lg[:, lo:hi, :], psL[:, j, 0:n * NE].rearrange("p (w e) -> p w e", e=NE),
                                       Rbb[:, :].unsqueeze(1).broadcast_to([P, n, NE]), ALU.add))
                for w in ws:
                    c(V.max(top[:, w, :], lg[:, w, :]))
                for w in ws:
                    dve.wait_ge(dv, c.n - n + 1)
                    c(V.max_index(topi[:, w, :], top[:, w, :], lg[:, w, :]))
                dve.wait_ge(dv, c.n)
                c.then(V.tensor_copy(topf[:, :, lo:hi], topi[:, lo:hi, 0:TOPK].rearrange("p w k -> p k w")))
                for k in range(TOPK):
                    c(V.tensor_tensor(pick[:, k, lo:hi, :], iota32[:, 0:NE].unsqueeze(1).broadcast_to([P, n, NE]),
                                      topf[:, k, lo:hi].unsqueeze(2).broadcast_to([P, n, NE]), ALU.is_equal))
                dve.wait_ge(dv, c.n)
                last = V.tensor_tensor(both[:, lo:hi, :], pick[:, 0, lo:hi, :], pick[:, 1, lo:hi, :], ALU.add)
                if hi == NW:
                    c.then(last)
                    last = V.tensor_scalar(both[:, NW - 1, :], both[:, NW - 1, :], live[:, 0:1], None, ALU.mult)
                last.then_inc(picked, 1)
            V.tensor_tensor(diff[:, :], top[:, :, 1], top[:, :, 0], ALU.subtract).then_inc(shifted, 1)
            dve.wait_ge(expd, 1)
            c.then(V.tensor_scalar(gates[:, :, 0], gates[:, :, 1], 1.0, None, ALU.add))
            c.then(V.reciprocal(gates[:, :, 0], gates[:, :, 0]))
            c(V.tensor_tensor(gates[:, :, 1], gates[:, :, 1], gates[:, :, 0], ALU.mult))
            dve.wait_ge(ranked, 1)
            c.then(V.tensor_copy(cnt[:, :], psK[:, 1, (NW - B1W) * NE:(NW - B1W + 1) * NE]))
            c.then(V.tensor_tensor(over[:, :, :], cnt[:, :].unsqueeze(2).broadcast_to([P, NE, MORE]),
                                   fulls[:, :].unsqueeze(1).broadcast_to([P, NE, MORE]), ALU.is_gt))
            c.then(V.tensor_reduce(more[:, :], over[:, :, :], AX_X, ALU.add))
            c.then(V.tensor_tensor_scan(upto[:, 1:NE + 1], more[:, :], zrow[:, :], 0.0, ALU.add, ALU.add))
            c.then(V.tensor_scalar(first_at[:, :], upto[:, 0:NE], float(NE - 1), float(CAP), ALU.add, ALU.mult))
            c.then(V.scalar_tensor_tensor(out=delta[:, :], in0=iota32[:, 0:NE], scalar=float(CAP), in1=first_at[:, :],
                                          op0=ALU.mult, op1=ALU.subtract))
            for bank, lo, hi in PARTS:
                n, at = hi - lo, (lo - bank * B1W) * NE
                rank = psK[:, bank, at:at + n * NE].rearrange("p (w e) -> p w e", e=NE)

                def every(a):
                    return a.unsqueeze(1).broadcast_to([P, n, NE])

                c.then(V.scalar_tensor_tensor(out=place[:, lo:hi, :], in0=rank, scalar=float(CAP), in1=every(delta[:, :]),
                                              op0=ALU.is_lt, op1=ALU.mult))
                c.then(V.tensor_tensor(place[:, lo:hi, :], place[:, lo:hi, :], rank, ALU.add))
                c.then(V.tensor_tensor(place[:, lo:hi, :], place[:, lo:hi, :], every(first_at[:, :]), ALU.add))
                for k in range(TOPK):
                    c(V.tensor_tensor(pick[:, k, lo:hi, :], pick[:, k, lo:hi, :], place[:, lo:hi, :], ALU.mult))
                for k in range(TOPK):
                    dve.wait_ge(dv, c.n - 1)
                    c(V.tensor_reduce(slotf[:, k, lo:hi], pick[:, k, lo:hi, :], AX_X, ALU.add))
                dve.wait_ge(dv, c.n)
                V.tensor_copy(slot[:, :, lo:hi], slotf[:, :, lo:hi]).then_inc(slots, 1)
            c(V.tensor_copy(nov[:, :], upto[0:1, NE:NE + 1]))
            c.then(V.tensor_scalar(past[:, :], upto[:, 1:NE + 1], prow[:, 0:1], None, ALU.is_le))
            V.tensor_reduce(ovc[:, :], past[:, :], AX_X, ALU.add).then_inc(ov_set, 1)
            dve.wait_ge(ov_ps, 1)
            c(V.tensor_scalar(ovx[:, :], psO[0:1, 0:OVB], float(NE - 1), None, ALU.min))
            dve.wait_ge(dv, c.n)


def expert_phase(nc, v):
    (ident, W1, W2, b2, xs_d, ys_d, b1T) = (v[k] for k in "ident W1 W2 b2 xs_d ys_d b1T".split())
    w1, w2, w_in = (v[k] for k in "w1 w2 w_in".split())
    with ExitStack() as ctx:
        def sb(name, shape, dt=F32):
            return ctx.enter_context(nc.sbuf_tensor(name, shape, dt))

        def sem(name):
            return ctx.enter_context(nc.semaphore(name))

        b2e = [sb(f"b2e_{r}", [CAP, D]) for r in range(XR)]
        X = [sb(f"X{r}", [CAP, D]) for r in range(XR)]
        xT = sb("xT", [P, 2, KC * CAP])
        hid = sb("hid", [P, 2, HC * CAP])
        Y = [sb(f"Y{r}", [CAP, D]) for r in range(YR)]
        psX = ctx.enter_context(nc.psum_tensor("psXe", [P, 2, 512], F32))
        psH = ctx.enter_context(nc.psum_tensor("psH", [P, 2, 512], F32))
        psY = ctx.enter_context(nc.psum_tensor("psY", [P, 2, 512], F32))

        x_in = [sem(f"xe_in{r}") for r in range(XR)]
        y_out = [sem(f"y_out{r}") for r in range(YR)]
        biased = sem("biased")
        turned = sem("turned_e")
        xT_set = sem("xT_set")
        hid_ps = sem("hid_ps")
        hid_set = sem("hid_set")
        y_ps = sem("y_ps")
        y_set = sem("y_set")
        block = ctx.enter_context(nc.Block())

        def load_tokens(sp, r, e):
            sp.dma_start(b2e[r][:, :], b2[bass.ds(e, 1), :].broadcast_to([CAP, D])).then_inc(x_in[r], 16)
            sp.dma_start(X[r][:, :], xs_d[bass.ds(e * CAP, CAP), :]).then_inc(x_in[r], 16)

        @block.sync
        def _(sp):
            for r in range(XR):
                load_tokens(sp, r, r)

            def refill(i, r, weights):
                sp.wait_ge(y_set, i * RING + r + 3)
                load_tokens(sp, r % XR, i * RING + (r + XR))
                if weights:
                    load_weights(sp, W1, W2, w1, w2, w_in, r, i * RING + (r + RING))

            with sp.Fori(0, NE // RING - 1) as i:
                for r in range(RING):
                    refill(i, r, True)
            for r in range(RING - XR):
                refill(NE // RING - 1, r, False)

        @block.gpsimd
        def _(g):
            for r in range(YR):
                g.wait_ge(y_out[r], 16 * (NE // YR) + 16)

        LASTG = NE // RING - 1

        def groups(eng, step):
            with eng.Fori(0, LASTG) as i:
                for r in range(RING):
                    step(i, r, RING)
            for r in range(RING):
                step(LASTG, r, RING - 1 - r)

        @block.tensor
        def _(pe):
            pe.sem_inc(y_ps, RING)

            def turn(grp, r):
                e, b = grp * RING + r, r % 2
                x = r % XR
                pe.wait_ge(x_in[x], grp * (32 * (RING // XR)) + 32 * (r // XR + 1))
                pe.wait_ge(xT_set, e + 1)
                for c in range(KC):
                    last = nc.tensor.transpose(psX[:, b, c * CAP:(c + 1) * CAP], X[x][:, c::KC], ident[0:CAP, 0:CAP])
                last.then_inc(turned, 1)

            def first(grp, r):
                e, b = grp * RING + r, r % 2
                r, grp = r % RING, grp + r // RING
                pe.wait_ge(w_in[r], grp * 32 + 32)
                pe.wait_ge(xT_set, e + 3)
                pe.wait_ge(hid_set, e + 1)
                for m in range(HC):
                    for c in range(KC):
                        last = nc.tensor.matmul(psH[:, b, m * CAP:(m + 1) * CAP], w1[r][:, c, m::HC],
                                                xT[:, b, c * CAP:(c + 1) * CAP], start=(c == 0), stop=(c == KC - 1))
                last.then_inc(hid_ps, 1)

            def step(grp, r, left):
                e, b = grp * RING + r, r % 2
                if left >= 2:
                    turn(grp, r + 2)
                if left >= 1:
                    first(grp, r + 1)
                pe.wait_ge(hid_set, e + 3)
                pe.wait_ge(y_set, e + 1)
                for m in range(HC):
                    last = nc.tensor.matmul(psY[0:CAP, b, 0:D], hid[:, b, m * CAP:(m + 1) * CAP], w2[r][:, m, :],
                                            start=(m == 0), stop=(m == HC - 1))
                last.then_inc(y_ps, 1)

            turn(0, 0)
            turn(0, 1)
            first(0, 0)
            groups(pe, step)

        @block.vector
        def _(dve):
            dve.sem_inc(hid_set, 2)
            dve.sem_inc(y_set, 2)

            def hidden(grp, r):
                e, b = grp * RING + r, r % 2
                dve.wait_ge(hid_ps, e + 1)
                dve.wait_ge(y_ps, e + RING - 1)
                nc.vector.tensor_tensor(hid[:, b, :].rearrange("p (m t) -> p m t", m=HC),
                                        psH[:, b, 0:HC * CAP].rearrange("p (m t) -> p m t", m=HC),
                                        b1T[:, bass.ds(e, 1), :].rearrange("p e m -> p (e m)").unsqueeze(2).broadcast_to([P, HC, CAP]),
                                        ALU.add).then_inc(biased, 1)
                dve.wait_ge(biased, e + 1)
                nc.vector.tensor_scalar(hid[:, b, :], hid[:, b, :], 0.0, None, ALU.max).then_inc(hid_set, 1)

            def step(grp, r, left):
                e, b = grp * RING + r, r % 2
                if left >= 1:
                    hidden(grp, r + 1)
                dve.wait_ge(y_ps, e + RING + 1)
                q = r % YR
                dve.wait_ge(y_out[q], grp * (16 * (RING // YR)) + 16 * (r // YR + 1))
                nc.vector.tensor_tensor(Y[q][:, :], psY[0:CAP, b, 0:D], b2e[r % XR][:, :], ALU.add).then_inc(y_set, 1)

            for q in range(YR):
                dve.sem_inc(y_out[q], 16)
            hidden(0, 0)
            groups(dve, step)

        @block.scalar
        def _(act):
            act.sem_inc(xT_set, 2)

            def copy_x(grp, r):
                e, b = grp * RING + r, r % 2
                act.wait_ge(turned, e + 1)
                nc.scalar.copy(xT[:, b, :], psX[:, b, 0:KC * CAP]).then_inc(xT_set, 1)

            def step(grp, r, left):
                e, b = grp * RING + r, r % 2
                if left >= 2:
                    act.wait_ge(hid_ps, e + 1)
                    copy_x(grp, r + 2)
                act.wait_ge(y_set, e + 3)
                q = r % YR
                act.dma_start(ys_d[bass.ds(e * CAP, CAP), :], Y[q][:, :]).then_inc(y_out[q], 16)

            copy_x(0, 0)
            copy_x(0, 1)
            groups(act, step)


def overflow_phase(nc, v):
    (ident, W1, W2, b2, xs_d, ys_d, b1T, nov, ovx) = (v[k] for k in "ident W1 W2 b2 xs_d ys_d b1T nov ovx".split())
    with ExitStack() as ctx:
        def sb(name, shape, dt=F32):
            return ctx.enter_context(nc.sbuf_tensor(name, shape, dt))

        def sem(name):
            return ctx.enter_context(nc.semaphore(name))

        w1 = sb("ow1", [P, KC, HID])
        w2 = sb("ow2", [P, HC, D])
        b2e = sb("ob2e", [CAP, D])
        X = sb("oX", [CAP, D])
        xT = sb("oxT", [P, KC * CAP])
        hid = sb("ohid", [P, HC * CAP])
        Y = sb("oY", [CAP, D])
        psX = ctx.enter_context(nc.psum_tensor("opsX", [P, 512], F32))
        psH = ctx.enter_context(nc.psum_tensor("opsH", [P, 512], F32))
        psY = ctx.enter_context(nc.psum_tensor("opsY", [P, 512], F32))
        came, went, turned, xT_set, hid_ps, biased, hid_set, y_ps, y_set = map(sem, (
            "came", "went", "oturned", "oxT_set", "ohid_ps", "obiased", "ohid_set", "oy_ps", "oy_set"))
        block = ctx.enter_context(nc.Block())

        @block.sync
        def _(sp):
            n = sp.value_load(nov[0:1, 0:1], min_val=0, max_val=OVB)
            with sp.If(n > 0):
                sp.sem_inc(went, 16)
                with sp.Fori(0, OVB) as k:
                    sp.wait_ge(went, k * 16 + 16)
                    e = sp.value_load(ovx[0:1, bass.ds(k, 1)], min_val=0, max_val=NE - 1)
                    sp.dma_start(w1[:, :, :], W1[bass.ds(e, 1), :, :].rearrange("e (p c) n -> (e p) c n", c=KC)).then_inc(came, 16)
                    sp.dma_start(w2[:, :, :], W2[bass.ds(e, 1), :, :].rearrange("e (p m) n -> (e p) m n", m=HC)).then_inc(came, 16)
                    sp.dma_start(b2e[:, :], b2[bass.ds(e, 1), :].broadcast_to([CAP, D])).then_inc(came, 16)
                    sp.dma_start(X[:, :], xs_d[bass.ds((k + NE) * CAP, CAP), :]).then_inc(came, 16)
                    sp.wait_ge(y_set, k + 1)
                    sp.dma_start(ys_d[bass.ds((k + NE) * CAP, CAP), :], Y[:, :]).then_inc(went, 16)
                sp.wait_ge(went, OVB * 16 + 16)

        @block.tensor
        def _(pe):
            n = pe.value_load(nov[0:1, 0:1], min_val=0, max_val=OVB)
            with pe.If(n > 0):
                with pe.Fori(0, OVB) as k:
                    pe.wait_ge(came, k * 64 + 64)
                    for c in range(KC):
                        last = nc.tensor.transpose(psX[:, c * CAP:(c + 1) * CAP], X[:, c::KC], ident[0:CAP, 0:CAP])
                    last.then_inc(turned, 1)
                    pe.wait_ge(xT_set, k + 1)
                    for m in range(HC):
                        for c in range(KC):
                            last = nc.tensor.matmul(psH[:, m * CAP:(m + 1) * CAP], w1[:, c, m::HC],
                                                    xT[:, c * CAP:(c + 1) * CAP], start=(c == 0), stop=(c == KC - 1))
                    last.then_inc(hid_ps, 1)
                    pe.wait_ge(hid_set, k + 1)
                    for m in range(HC):
                        last = nc.tensor.matmul(psY[0:CAP, 0:D], hid[:, m * CAP:(m + 1) * CAP], w2[:, m, :],
                                                start=(m == 0), stop=(m == HC - 1))
                    last.then_inc(y_ps, 1)

        @block.vector
        def _(dve):
            n = dve.value_load(nov[0:1, 0:1], min_val=0, max_val=OVB)
            with dve.If(n > 0):
                with dve.Fori(0, OVB) as k:
                    e = dve.value_load(ovx[0:1, bass.ds(k, 1)], min_val=0, max_val=NE - 1)
                    dve.wait_ge(turned, k + 1)
                    nc.vector.tensor_copy(xT[:, :], psX[:, 0:KC * CAP]).then_inc(xT_set, 1)
                    dve.wait_ge(hid_ps, k + 1)
                    nc.vector.tensor_tensor(hid[:, :].rearrange("p (m t) -> p m t", m=HC),
                                            psH[:, 0:HC * CAP].rearrange("p (m t) -> p m t", m=HC),
                                            b1T[:, bass.ds(e, 1), :].rearrange("p e m -> p (e m)").unsqueeze(2).broadcast_to([P, HC, CAP]),
                                            ALU.add).then_inc(biased, 1)
                    dve.wait_ge(biased, k + 1)
                    nc.vector.tensor_scalar(hid[:, :], hid[:, :], 0.0, None, ALU.max).then_inc(hid_set, 1)
                    dve.wait_ge(y_ps, k + 1)
                    nc.vector.tensor_tensor(Y[:, :], psY[0:CAP, 0:D], b2e[:, :], ALU.add).then_inc(y_set, 1)


def combine_phase(nc, v):
    out, xs, ys_d, slot, gates, fetched = (v[k] for k in "out xs ys_d slot gates fetched".split())
    with ExitStack() as ctx:
        def sem(name):
            return ctx.enter_context(nc.semaphore(name))

        yg = ctx.enter_context(nc.sbuf_tensor("yg", [P, NW, TOPK, D], F32))
        half, full, outs = sem("half"), sem("full"), sem("outs")
        block = ctx.enter_context(nc.Block())

        @block.gpsimd
        def _(g):
            for w in range(NW):
                n = P if w < NW - 1 else NREM
                for k in range(TOPK):
                    nc.gpsimd.indirect_dma_start(out=yg[0:n, w, k, :], out_offset=None, in_=ys_d,
                                                 in_offset=bass.IndirectOffsetOnAxis(ap=slot[0:n, k, w:w + 1], axis=0)
                                                 ).then_inc(fetched[w // 2], 16)

        @block.vector
        def _(dve):
            for w in range(NW):
                n = P if w < NW - 1 else NREM
                dve.wait_ge(fetched[w // 2], 64)
                nc.vector.scalar_tensor_tensor(out=xs[0:n, w, :], in0=yg[0:n, w, 0, :], scalar=gates[0:n, w, 0:1],
                                               in1=xs[0:n, w, :], op0=ALU.mult, op1=ALU.add).then_inc(half, 1)
                dve.wait_ge(half, w + 1)
                nc.vector.scalar_tensor_tensor(out=xs[0:n, w, :], in0=yg[0:n, w, 1, :], scalar=gates[0:n, w, 1:2],
                                               in1=xs[0:n, w, :], op0=ALU.mult, op1=ALU.add).then_inc(full, 1)

        @block.sync
        def _(sp):
            for w in range(NW):
                n = P if w < NW - 1 else NREM
                sp.wait_ge(full, w + 1)
                sp.dma_start(out[w * P:w * P + n, :], xs[0:n, w, :]).then_inc(outs, 16)
            sp.wait_ge(outs, 16 * NW)


_INS = ["x", "src", "dst", "L0_gnn_W_l", "L0_gnn_W_r", "L0_gnn_att", "L0_gnn_bias", "L0_gnn_gamma", "L0_gnn_beta",
        "L0_ffn_Wr", "L0_ffn_br", "L0_ffn_W1", "L0_ffn_b1", "L0_ffn_W2", "L0_ffn_b2"]


def kernel(**inputs):
    import concourse.bacc as bacc
    from concourse.bass_utils import run_bass_kernel_spmd

    nc = bacc.Bacc("TRN2", target_bir_lowering=False, num_devices=1)
    arrays, args = {}, []
    for name in _INS:
        a = np.ascontiguousarray(inputs[name])
        arrays[f"in_{name}"] = a
        args.append(nc.dram_tensor(f"in_{name}", a.shape, mybir.dt.from_np(a.dtype), kind="ExternalInput").ap())
    args.append(nc.dram_tensor("out_x", (N, D), F32, kind="ExternalOutput").ap())
    gnn_moe(nc, *args)
    r = run_bass_kernel_spmd(nc, [arrays], core_ids=[0])
    return r.results[0]["out_x"]
```
